# Optimizing a Trainium2 kernel written in Bass

```python
import numpy as np
import jax
import jax.numpy as jnp

def _softmax(x, axis=-1):
    return jax.nn.softmax(x, axis=axis)

def _gelu(x):
    return jax.nn.gelu(x, approximate=True)

def _silu(x):
    return jax.nn.silu(x)

def _sigmoid(x):
    return jax.nn.sigmoid(x)

def _layernorm(x, axis=-1, eps=1e-05):
    m = jnp.mean(x, axis=axis, keepdims=True)
    v = jnp.var(x, axis=axis, keepdims=True)
    return (x - m) / jnp.sqrt(v + eps)

def _scatter_add(tgt, idx, src, axis=0):
    return tgt.at[idx].add(src)

def _segment_sum(src, seg, n):
    return jax.ops.segment_sum(src, seg, n)
kernel_name = 'mk_perceiver_d1_seqx_r2_c4324b'

def setup_inputs(seed: int=0):
    np.random.seed(seed)
    _w = jnp.asarray

    def _rec_inputs():
        import jax
        import jax.numpy as jnp
        _rk = jax.random.key(seed)
        x = -0.0002928 + 1 * jax.random.normal(jax.random.fold_in(_rk, 1), (1, 512, 512), jnp.float32)
        _lenS = 512 - jax.random.randint(jax.random.fold_in(_rk, 7), (1,), 0, max(1, 512 // 4) + 1, jnp.int32)
        _lenS2 = 8192 - jax.random.randint(jax.random.fold_in(_rk, 8), (1,), 0, max(1, 8192 // 4) + 1, jnp.int32)
        _ctx_1024P = jax.random.normal(jax.random.fold_in(_rk, 11), (1, 16, 512), jnp.float32)
        _ctx_1024c = jax.random.dirichlet(jax.random.fold_in(_rk, 511), 0.3 * jnp.ones((16,), jnp.float32), (1, 8192))
        _ctx_1024t = jnp.einsum('bsk,bkd->bsd', _ctx_1024c, _ctx_1024P)
        _ctx_1024t = _ctx_1024t * jax.lax.rsqrt(jnp.mean(jnp.square(_ctx_1024t)) + 1e-12) * 0.953939
        ctx_1024 = -1.39393e-06 + 0.999914 * (_ctx_1024t + 0.3 * jax.random.normal(jax.random.fold_in(_rk, 611), (1, 8192, 512), jnp.float32))
        return (x, ctx_1024)
    x, ctx_1024 = _rec_inputs()

    def _L0_xattn_setup():
        import jax, jax.numpy as jnp
        import numpy as np
        D_MODEL = 512
        NUM_HEADS = 16
        HEAD_DIM = D_MODEL // NUM_HEADS
        key = jax.random.key(seed)
        ks = jax.random.split(key, 11)
        B, S = (2, 1024)
        scale = 1.0 / np.sqrt(D_MODEL)
        inp = {'query': jax.random.normal(ks[0], (B, S, D_MODEL), jnp.float32), 'key': jax.random.normal(ks[1], (B, S, D_MODEL), jnp.float32), 'value': jax.random.normal(ks[2], (B, S, D_MODEL), jnp.float32), 'Wq': jax.random.normal(ks[3], (D_MODEL, D_MODEL), jnp.float32) * scale, 'bq': jnp.zeros((D_MODEL,), jnp.float32), 'Wk': jax.random.normal(ks[4], (D_MODEL, D_MODEL), jnp.float32) * scale, 'bk': jnp.zeros((D_MODEL,), jnp.float32), 'Wv': jax.random.normal(ks[5], (D_MODEL, D_MODEL), jnp.float32) * scale, 'bv': jnp.zeros((D_MODEL,), jnp.float32), 'Wo': jax.random.normal(ks[6], (D_MODEL, D_MODEL), jnp.float32) * scale, 'bo': jnp.zeros((D_MODEL,), jnp.float32)}
        return inp
    _L0_xattn_all = _L0_xattn_setup()
    _L0_xattn_in = {k: v for k, v in _L0_xattn_all.items() if k in ('Wq', 'bq', 'Wk', 'bk', 'Wv', 'bv', 'Wo', 'bo')}
    del _L0_xattn_all

    def _L0_attn_setup():
        import jax, jax.numpy as jnp
        import numpy as np
        NUM_HEADS = 16
        EMBED_DIM = 512

        def _linear_attention(x, Wq, bq, Wk, bk, Wv, bv, Wo, bo):
            B, S, D = x.shape
            H = NUM_HEADS
            hd = D // H
            v = (x @ Wv + bv).reshape(B, S, H, hd)
            q = (x @ Wq + bq).reshape(B, S, H, hd)
            k = (x @ Wk + bk).reshape(B, S, H, hd)
            q = jax.nn.elu(q) + 1.0
            k = jax.nn.elu(k) + 1.0
            qT = q.transpose(1, 0, 2, 3)
            kT = k.transpose(1, 0, 2, 3)
            vT = v.transpose(1, 0, 2, 3)
            s0 = jnp.zeros((B, H, hd, hd), dtype=x.dtype)
            z0 = jnp.zeros((B, H, hd), dtype=x.dtype)

            def step(carry, qkv):
                s, z = carry
                q_i, k_i, v_i = qkv
                s = s + jnp.einsum('bhd,bhm->bhdm', k_i, v_i)
                z = z + k_i
                qs = jnp.einsum('bhd,bhdm->bhm', q_i, s)
                qz = jnp.einsum('bhd,bhd->bh', q_i, z)[..., None]
                return ((s, z), qs / (qz + 1e-06))
            (_, _), values = jax.lax.scan(step, (s0, z0), (qT, kT, vT))
            values = values.transpose(1, 0, 2, 3).reshape(B, S, D)
            return values @ Wo + bo
        key = jax.random.key(seed)
        ks = jax.random.split(key, 6)
        B, S, D = (4, 1024, EMBED_DIM)
        sc = 1.0 / np.sqrt(D)
        return {'x': jax.random.normal(ks[0], (B, S, D), dtype=jnp.float32), 'mask': jnp.ones((B, S), dtype=jnp.int32), 'Wq': jax.random.normal(ks[1], (D, D), dtype=jnp.float32) * sc, 'bq': jnp.zeros((D,), dtype=jnp.float32), 'Wk': jax.random.normal(ks[2], (D, D), dtype=jnp.float32) * sc, 'bk': jnp.zeros((D,), dtype=jnp.float32), 'Wv': jax.random.normal(ks[3], (D, D), dtype=jnp.float32) * sc, 'bv': jnp.zeros((D,), dtype=jnp.float32), 'Wo': jax.random.normal(ks[4], (D, D), dtype=jnp.float32) * sc, 'bo': jnp.zeros((D,), dtype=jnp.float32)}
    _L0_attn_all = _L0_attn_setup()
    _L0_attn_in = {k: v for k, v in _L0_attn_all.items() if k in ('mask', 'Wq', 'bq', 'Wk', 'bk', 'Wv', 'bv', 'Wo', 'bo')}
    del _L0_attn_all

    def _L0_ffn_setup():
        import jax, jax.numpy as jnp
        import numpy as np
        TOP_K = 2
        EPS = 1e-10
        key = jax.random.key(seed)
        k1, k2, k3, k4 = jax.random.split(key, 4)
        B, S, H, E = (4, 1024, 512, 8)
        tokens = jax.random.normal(k1, (B, S, H), dtype=jnp.float32)
        router_w = jax.random.normal(k2, (E, H), dtype=jnp.float32) * (1.0 / np.sqrt(H))
        router_b = jax.random.normal(k3, (E,), dtype=jnp.float32) * 0.01
        expert_weights = jax.random.normal(k4, (E, H, H), dtype=jnp.float32) * (1.0 / np.sqrt(H))
        return {'tokens': tokens, 'router_w': router_w, 'router_b': router_b, 'expert_weights': expert_weights}
    _L0_ffn_all = _L0_ffn_setup()
    _L0_ffn_in = {k: v for k, v in _L0_ffn_all.items() if k in ('router_w', 'router_b', 'expert_weights')}
    del _L0_ffn_all
    return {'x': x, 'ctx_1024': ctx_1024, 'L0_xattn_Wq': _L0_xattn_in['Wq'], 'L0_xattn_bq': _L0_xattn_in['bq'], 'L0_xattn_Wk': _L0_xattn_in['Wk'], 'L0_xattn_bk': _L0_xattn_in['bk'], 'L0_xattn_Wv': _L0_xattn_in['Wv'], 'L0_xattn_bv': _L0_xattn_in['bv'], 'L0_xattn_Wo': _L0_xattn_in['Wo'], 'L0_xattn_bo': _L0_xattn_in['bo'], 'L0_attn_mask': _L0_attn_in['mask'], 'L0_attn_Wq': _L0_attn_in['Wq'], 'L0_attn_bq': _L0_attn_in['bq'], 'L0_attn_Wk': _L0_attn_in['Wk'], 'L0_attn_bk': _L0_attn_in['bk'], 'L0_attn_Wv': _L0_attn_in['Wv'], 'L0_attn_bv': _L0_attn_in['bv'], 'L0_attn_Wo': _L0_attn_in['Wo'], 'L0_attn_bo': _L0_attn_in['bo'], 'L0_ffn_router_w': _L0_ffn_in['router_w'], 'L0_ffn_router_b': _L0_ffn_in['router_b'], 'L0_ffn_expert_weights': _L0_ffn_in['expert_weights']}

def reference(x, ctx_1024, L0_xattn_Wq, L0_xattn_bq, L0_xattn_Wk, L0_xattn_bk, L0_xattn_Wv, L0_xattn_bv, L0_xattn_Wo, L0_xattn_bo, L0_attn_mask, L0_attn_Wq, L0_attn_bq, L0_attn_Wk, L0_attn_bk, L0_attn_Wv, L0_attn_bv, L0_attn_Wo, L0_attn_bo, L0_ffn_router_w, L0_ffn_router_b, L0_ffn_expert_weights):
    import jax
    import jax.numpy as jnp

    def _L0_xattn_ref(query, key, value, Wq, bq, Wk, bk, Wv, bv, Wo, bo):
        import jax, jax.numpy as jnp
        import numpy as np
        D_MODEL = 512
        NUM_HEADS = 16
        HEAD_DIM = D_MODEL // NUM_HEADS
        B, S, _ = query.shape
        q = query @ Wq + bq
        k = key @ Wk + bk
        v = value @ Wv + bv
        q = q.reshape(B, S, NUM_HEADS, HEAD_DIM).transpose(0, 2, 1, 3)
        k = k.reshape(B, -1, NUM_HEADS, HEAD_DIM).transpose(0, 2, 1, 3)
        v = v.reshape(B, -1, NUM_HEADS, HEAD_DIM).transpose(0, 2, 1, 3)
        scores = jnp.einsum('bhqd,bhkd->bhqk', q, k) / jnp.sqrt(jnp.asarray(HEAD_DIM, q.dtype))
        attn = jax.nn.softmax(scores, axis=-1)
        out = jnp.einsum('bhqk,bhkd->bhqd', attn, v)
        out = out.transpose(0, 2, 1, 3).reshape(B, S, D_MODEL)
        return out @ Wo + bo

    def _L0_attn_ref(x, mask, Wq, bq, Wk, bk, Wv, bv, Wo, bo):
        import jax, jax.numpy as jnp
        import numpy as np
        NUM_HEADS = 16
        EMBED_DIM = 512

        def _linear_attention(x, Wq, bq, Wk, bk, Wv, bv, Wo, bo):
            B, S, D = x.shape
            H = NUM_HEADS
            hd = D // H
            v = (x @ Wv + bv).reshape(B, S, H, hd)
            q = (x @ Wq + bq).reshape(B, S, H, hd)
            k = (x @ Wk + bk).reshape(B, S, H, hd)
            q = jax.nn.elu(q) + 1.0
            k = jax.nn.elu(k) + 1.0
            qT = q.transpose(1, 0, 2, 3)
            kT = k.transpose(1, 0, 2, 3)
            vT = v.transpose(1, 0, 2, 3)
            s0 = jnp.zeros((B, H, hd, hd), dtype=x.dtype)
            z0 = jnp.zeros((B, H, hd), dtype=x.dtype)

            def step(carry, qkv):
                s, z = carry
                q_i, k_i, v_i = qkv
                s = s + jnp.einsum('bhd,bhm->bhdm', k_i, v_i)
                z = z + k_i
                qs = jnp.einsum('bhd,bhdm->bhm', q_i, s)
                qz = jnp.einsum('bhd,bhd->bh', q_i, z)[..., None]
                return ((s, z), qs / (qz + 1e-06))
            (_, _), values = jax.lax.scan(step, (s0, z0), (qT, kT, vT))
            values = values.transpose(1, 0, 2, 3).reshape(B, S, D)
            return values @ Wo + bo
        return _linear_attention(x, Wq, bq, Wk, bk, Wv, bv, Wo, bo)

    def _L0_ffn_ref(tokens, router_w, router_b, expert_weights):
        import jax, jax.numpy as jnp
        import numpy as np
        TOP_K = 2
        EPS = 1e-10
        B, S, H = tokens.shape
        E = expert_weights.shape[0]
        logits = jnp.einsum('bsh,eh->bse', tokens, router_w) + router_b
        probs = jax.nn.softmax(logits, axis=-1)
        top_p, top_i = jax.lax.top_k(probs, TOP_K)
        w = top_p / (jnp.sum(top_p, axis=-1, keepdims=True) + EPS)
        x = tokens.reshape(-1, H)
        idx = top_i.reshape(-1, TOP_K)
        wf = w.reshape(-1, TOP_K)
        y_all = jnp.einsum('nh,ehd->ned', x, expert_weights)
        y_k = jnp.take_along_axis(y_all, idx[:, :, None], axis=1)
        out = jnp.einsum('nk,nkh->nh', wf, y_k)
        acc = jnp.clip(jnp.sum(wf, axis=-1), EPS, None)
        out = (out / acc[:, None]).reshape(B, S, H)
        scale = 1.0 + jnp.sum(w, axis=-1, keepdims=True) * EPS
        return out * scale
    x = x + _L0_xattn_ref(_layernorm(x, axis=-1), ctx_1024, ctx_1024, L0_xattn_Wq, L0_xattn_bq, L0_xattn_Wk, L0_xattn_bk, L0_xattn_Wv, L0_xattn_bv, L0_xattn_Wo, L0_xattn_bo)
    x = x + _L0_attn_ref(_layernorm(x, axis=-1), L0_attn_mask, L0_attn_Wq, L0_attn_bq, L0_attn_Wk, L0_attn_bk, L0_attn_Wv, L0_attn_bv, L0_attn_Wo, L0_attn_bo)
    x = x + _L0_ffn_ref(_layernorm(x, axis=-1), L0_ffn_router_w, L0_ffn_router_b, L0_ffn_expert_weights)
    return x

_drawn_inputs = setup_inputs


def setup_inputs(seed=0):
    import zlib

    import numpy as np

    out = dict(_drawn_inputs(seed))
    spreads = {'L0_xattn_bq': (0.0, 0.1),
     'L0_xattn_bk': (0.0, 0.8),
     'L0_xattn_bv': (0.0, 0.1),
     'L0_xattn_bo': (0.0, 0.1),
     'L0_attn_bq': (0.0, 0.8),
     'L0_attn_bk': (0.0, 0.8),
     'L0_attn_bv': (0.0, 0.1),
     'L0_attn_bo': (0.0, 0.1)}
    factors = {'L0_attn_Wq': 3.738}
    for name, (base, spread) in spreads.items():
        noise = np.random.default_rng([zlib.crc32(name.encode()), seed]).standard_normal(out[name].shape)
        drawn = base * np.exp(spread * noise) if base else spread * noise
        out[name] = jnp.asarray(drawn.astype(out[name].dtype))
    for name, factor in factors.items():
        out[name] = (out[name] * factor).astype(out[name].dtype)
    return out
```

```python
import math
from contextlib import ExitStack

import numpy as np

import concourse.bass as bass
from concourse import mybir

F32 = mybir.dt.float32
F32R = mybir.dt.float32r
U32 = mybir.dt.uint32
ACT = mybir.ActivationFunctionType
ALU = mybir.AluOpType
AX = mybir.AxisListType

P = 128
S = 512
D = 512
C = D // P
KEYS = 8192
H = 16
HD = D // H
KB = 512
BLOCKS = KEYS // KB
KT = KEYS // P
EPS = 1e-5


class Chain:

    def __init__(self, eng, sem):
        self.eng, self.sem, self.n = eng, sem, 0

    def __call__(self, instruction):
        self.n += 1
        instruction.then_inc(self.sem, 1)
        self.eng.wait_ge(self.sem, self.n)


def norm_on_vector(dve, link, x4, xn, stats, mv, rstd, var_ready, std_ready, xn_ready, n):
    for t in range(C):
        link(dve.bn_stats(stats[:, t, :], x4[:, t, :]))
    for t in range(C):
        link(dve.bn_aggr(mv[:, t, :], stats[:, t, :]))
    dve.tensor_scalar(rstd[:, 0:C], mv[:, :, 1], EPS, None, ALU.add).then_inc(var_ready, 1)
    dve.wait_ge(std_ready, n)
    link(dve.reciprocal(rstd[:, 2 * C:3 * C], rstd[:, C:2 * C]))
    for t in range(C):
        dve.tensor_scalar(xn[:, t, :], x4[:, t, :], mv[:, t, 0:1],
                          rstd[:, 2 * C + t:2 * C + t + 1], ALU.subtract, ALU.mult).then_inc(xn_ready, 1)


def project_context(nc, ins, scratch, ident, ones):
    khi_d, klo_d, qhi_d, qlo_d, v_d = scratch
    with ExitStack() as ctx:
        def sb(name, shape, dt=F32):
            return ctx.enter_context(nc.sbuf_tensor(name, shape, dt))

        def sem(name):
            return ctx.enter_context(nc.semaphore(name))

        x4 = sb("x4", [P, C, D])
        xn = sb("xn", [P, C, D])
        xnT = sb("xnT", [P, C, S])
        wq = sb("wq", [P, C, D])
        wraw = sb("wraw", [P, 2, C, D])
        whi = sb("whi", [P, 2, C, D], F32R)
        wlo = sb("wlo", [P, 2, C, D], F32R)
        craw = sb("craw", [P, 2, C, KB])
        chi = sb("chi", [P, 2, C, KB], F32R)
        clo = sb("clo", [P, 2, C, KB], F32R)
        khi = sb("khi", [P, 2, C, KB], F32R)
        klo = sb("klo", [P, 2, C, KB], F32R)
        vout = sb("vout", [P, 2, H, C, HD])
        bq = sb("bq_sb", [P, C])
        bk = sb("bk_sb", [P, C])
        stats = sb("stats", [P, C, 6])
        mv = sb("mv", [P, C, 2])
        rstd = sb("rstd", [P, 3 * C])
        bank = [ctx.enter_context(nc.psum_tensor(f"proj{j}", [P, 512], F32)) for j in range(8)]

        x_in, wq_in, w_in, bias_in, ident_done = sem("x_in"), sem("wq_in"), [sem("wk_in"), sem("wv_in")], sem("bias_in"), sem("ident_done")
        ctx_in = [sem("ctx_in0"), sem("ctx_in1")]
        whi_done, wlo_done, chi_done, clo_done = sem("whi_done"), sem("wlo_done"), sem("chi_done"), sem("clo_done")
        var_ready, std_ready, xn_ready, xnT_psum, xnT_ready = sem("var_ready"), sem("std_ready"), sem("xn_ready"), sem("xnT_psum"), sem("xnT_ready")
        q_psum, qhi_done, qlo_done, q_stored = sem("q_psum"), sem("qhi_done"), sem("qlo_done"), sem("q_stored")
        proj_done = sem("proj_done")
        khi_done, klo_done = sem("khi_done"), sem("klo_done")
        va_done, vv_done = sem("va_done"), sem("vv_done")
        k_stored, v_stored = ([sem(f"{n}_stored{u}") for u in range(2)] for n in "kv")
        vec = sem("vec_chain")

        ctxT = ins["ctxT"].rearrange("(c p) n -> p c n", p=P)
        khi_v = khi_d.rearrange("(c p) n -> p c n", p=P)
        klo_v = klo_d.rearrange("(c p) n -> p c n", p=P)
        qhi_v = qhi_d.rearrange("(c p) n -> p c n", p=P)
        qlo_v = qlo_d.rearrange("(c p) n -> p c n", p=P)
        v_v = v_d.rearrange("h p b n -> p h b n")

        qhi, qlo = khi[:, 1], klo[:, 1]

        def w_v(name):
            return ins[name].rearrange("(c p) n -> p c n", p=P)

        block = ctx.enter_context(nc.Block())

        @block.sync
        def _(sp):
            sp.dma_start(x4[:, :, :], ins["x"].rearrange("(c p) n -> p c n", p=P)).then_inc(x_in, 16)
            sp.dma_start(wraw[:, 0], w_v("xWk")).then_inc(w_in[0], 16)
            sp.dma_start(bq[:, :], ins["xbq_col"]).then_inc(bias_in, 16)
            sp.dma_start(bk[:, :], ins["xbk_col"]).then_inc(bias_in, 16)
            sp.dma_start(craw[:, 0], ctxT[:, :, 0:KB]).then_inc(ctx_in[0], 16)
            sp.dma_start(wraw[:, 1], w_v("xWv")).then_inc(w_in[1], 16)
            sp.dma_start(wq[:, :, :], w_v("xWq")).then_inc(wq_in, 16)
            sp.dma_start(craw[:, 1], ctxT[:, :, KB:2 * KB]).then_inc(ctx_in[1], 16)

            def load(i, u):
                b = 2 * i + u
                sp.wait_ge(chi_done, b + 1)
                sp.wait_ge(clo_done, b + 1)
                sp.dma_start(craw[:, u], ctxT[:, :, bass.ds((b + 2) * KB, KB)]).then_inc(ctx_in[u], 16)

            def store(i, u):
                b = 2 * i + u
                sp.wait_ge(khi_done, C * (b + 1))
                sp.wait_ge(klo_done, C * (b + 1))
                sp.dma_start(khi_v[:, :, bass.ds(b * KB, KB)], khi[:, u].bitcast(F32)).then_inc(k_stored[u], 16)
                sp.dma_start(klo_v[:, :, bass.ds(b * KB, KB)], klo[:, u].bitcast(F32)).then_inc(k_stored[u], 16)
                sp.wait_ge(va_done, 2 * (b + 1))
                sp.wait_ge(vv_done, 2 * (b + 1))
                sp.dma_start(v_v[:, :, bass.ds(b, 1), :].rearrange("p h b n -> p h (b n)"),
                             vout[:, u].rearrange("p h k d -> p h (k d)")).then_inc(v_stored[u], 16)

            sp.wait_ge(qhi_done, C)
            sp.dma_start(qhi_v, qhi.bitcast(F32)).then_inc(q_stored, 16)
            sp.wait_ge(qlo_done, C)
            sp.dma_start(qlo_v, qlo.bitcast(F32)).then_inc(q_stored, 16)
            with sp.Fori(0, BLOCKS // 2 - 1) as i:
                for u in range(2):
                    load(i, u)
                    store(i, u)
            for u in range(2):
                store(BLOCKS // 2 - 1, u)
            for u in range(2):
                sp.wait_ge(k_stored[u], 16 * BLOCKS)
                sp.wait_ge(v_stored[u], 8 * BLOCKS)
            sp.wait_ge(q_stored, 32)

        @block.gpsimd
        def _(pool):
            pool.memset(ident[:, :], 0.0).then_inc(ident_done, 1)
            pool.memset(ones[:, :], 1.0)
            pool.wait_ge(ident_done, 1)
            pool.affine_select(out=ident[:, :], in_=ident[:, :], compare_op=ALU.not_equal, fill=1.0,
                               base=0, pattern=[[-1, P]], channel_multiplier=1).then_inc(ident_done, 1)

        @block.scalar
        def _(act):
            def split(u):
                act.activation(chi[:, u], craw[:, u], ACT.Copy).then_inc(chi_done, 1)

            act.wait_ge(w_in[0], 16)
            act.activation(whi[:, 0], wraw[:, 0], ACT.Copy).then_inc(whi_done, 1)
            act.wait_ge(var_ready, 1)
            act.activation(rstd[:, C:2 * C], rstd[:, 0:C], ACT.Sqrt).then_inc(std_ready, 1)
            act.wait_ge(ctx_in[0], 16)
            split(0)
            act.wait_ge(w_in[1], 16)
            act.activation(whi[:, 1], wraw[:, 1], ACT.Copy).then_inc(whi_done, 1)
            act.wait_ge(ctx_in[1], 16)
            split(1)
            for c in range(C):
                act.wait_ge(xnT_psum, c + 1)
                act.activation(xnT[:, c, :], bank[c][:, :], ACT.Copy).then_inc(xnT_ready, 1)
            act.wait_ge(bias_in, 32)
            for g in range(C):
                act.wait_ge(q_psum, g + 1)
                act.activation(qhi[:, g, :], bank[4 + g][:, :], ACT.Identity, bias=bq[:, g:g + 1]).then_inc(qhi_done, 1)

            def evacuate(i, u, first):
                b = 2 * i + u
                if first and u == 1:
                    act.wait_ge(q_stored, 32)
                if not first:
                    act.wait_ge(k_stored[u], 32 * i)
                for g in range(C):
                    act.wait_ge(proj_done, 8 * b + g + 1)
                    act.activation(khi[:, u, g, :], bank[g][:, :], ACT.Identity, bias=bk[:, g:g + 1]).then_inc(khi_done, 1)
                if not first:
                    act.wait_ge(v_stored[u], 16 * i)
                for t in range(2):
                    act.wait_ge(proj_done, 8 * b + 4 + t + 1)
                    act.activation(vout[:, u, :, t, :], bank[4 + t][:, :].rearrange("p (h d) -> p h d", d=HD),
                                   ACT.Copy).then_inc(va_done, 1)

            def step(i, u, first, last):
                evacuate(i, u, first)
                if not last:
                    b = 2 * i + u
                    act.wait_ge(proj_done, 8 * (b + 1))
                    act.wait_ge(ctx_in[u], 16 * (i + 2))
                    split(u)

            for u in range(2):
                step(0, u, True, False)
            with act.Fori(1, BLOCKS // 2 - 1) as i:
                for u in range(2):
                    step(i, u, False, False)
            for u in range(2):
                step(BLOCKS // 2 - 1, u, False, True)

        @block.vector
        def _(dve):
            link = Chain(dve, vec)

            def split(u, b):
                dve.wait_ge(chi_done, b + 1)
                dve.tensor_tensor(clo[:, u], craw[:, u], chi[:, u].bitcast(F32), ALU.subtract).then_inc(clo_done, 1)

            dve.wait_ge(x_in, 16)
            norm_on_vector(dve, link, x4, xn, stats, mv, rstd, var_ready, std_ready, xn_ready, 1)
            for w in range(2):
                dve.wait_ge(whi_done, w + 1)
                dve.tensor_tensor(wlo[:, w], wraw[:, w], whi[:, w].bitcast(F32), ALU.subtract).then_inc(wlo_done, 1)
                split(w, w)
            dve.wait_ge(bias_in, 32)
            for g in range(C):
                dve.wait_ge(qhi_done, g + 1)
                dve.scalar_tensor_tensor(qlo[:, g, :], bank[4 + g][:, :], bq[:, g:g + 1],
                                         qhi[:, g, :].bitcast(F32), ALU.add, ALU.subtract).then_inc(qlo_done, 1)

            def step(i, u, first, last):
                b = 2 * i + u
                if first and u == 1:
                    dve.wait_ge(q_stored, 32)
                if not first:
                    dve.wait_ge(k_stored[u], 32 * i)
                for g in range(C):
                    dve.wait_ge(khi_done, C * b + g + 1)
                    dve.scalar_tensor_tensor(klo[:, u, g, :], bank[g][:, :], bk[:, g:g + 1],
                                             khi[:, u, g, :].bitcast(F32), ALU.add, ALU.subtract).then_inc(klo_done, 1)
                if not first:
                    dve.wait_ge(v_stored[u], 16 * i)
                for t in range(2, C):
                    dve.wait_ge(proj_done, 8 * b + 4 + t + 1)
                    dve.tensor_copy(vout[:, u, :, t, :], bank[4 + t][:, :].rearrange("p (h d) -> p h d", d=HD)).then_inc(vv_done, 1)
                if not last:
                    dve.wait_ge(proj_done, 8 * (b + 1))
                    split(u, b + 2)

            for u in range(2):
                step(0, u, True, False)
            with dve.Fori(1, BLOCKS // 2 - 1) as i:
                for u in range(2):
                    step(i, u, False, False)
            for u in range(2):
                step(BLOCKS // 2 - 1, u, False, True)

        @block.tensor
        def _(pe):
            pe.wait_ge(ident_done, 2)
            pe.wait_ge(xn_ready, C)
            for c in range(C):
                for t in range(C):
                    m = pe.transpose(bank[c][:, t * P:(t + 1) * P], xn[:, t, c * P:(c + 1) * P], ident[:, :])
                m.then_inc(xnT_psum, 1)
            pe.wait_ge(xnT_ready, C)
            pe.wait_ge(wq_in, 16)
            for g in range(C):
                for c in range(C):
                    m = pe.matmul(bank[4 + g][:, :], wq[:, c, g * P:(g + 1) * P], xnT[:, c, :], start=c == 0, stop=c == C - 1)
                m.then_inc(q_psum, 1)

            def step(i, u, first):
                b = 2 * i + u
                pe.wait_ge(chi_done, b + 1)
                pe.wait_ge(clo_done, b + 1)
                if first and u == 0:
                    pe.wait_ge(wlo_done, 2)
                    pe.wait_ge(qlo_done, C)
                for g in range(C):
                    if not (first and u == 0):
                        pe.wait_ge(klo_done, C * (b - 1) + g + 1)
                    for c in range(C):
                        for w, x, n in ((whi, chi, 0), (wlo, chi, 1), (whi, clo, 2)):
                            m = pe.matmul(bank[g][:, :], w[:, 0, c, g * P:(g + 1) * P], x[:, u, c, :],
                                          start=c == 0 and n == 0, stop=c == C - 1 and n == 2)
                    m.then_inc(proj_done, 1)
                for t in range(C):
                    if not (first and u == 0):
                        pe.wait_ge(*((va_done, 2 * (b - 1) + t + 1) if t < 2 else (vv_done, 2 * (b - 1) + t - 1)))
                    for c in range(C):
                        for x, w, n in ((chi, whi, 0), (chi, wlo, 1), (clo, whi, 2)):
                            m = pe.matmul(bank[4 + t][:, :], x[:, u, c, t * P:(t + 1) * P], w[:, 1, c, :],
                                          start=c == 0 and n == 0, stop=c == C - 1 and n == 2)
                    m.then_inc(proj_done, 1)

            for u in range(2):
                step(0, u, True)
            with pe.Fori(1, BLOCKS // 2) as i:
                for u in range(2):
                    step(i, u, False)


QUADS = KT // 4
SLOTS = 16
PV_LAG = 2
PASSES = 2 * C * (KEYS // 2048)
LOADS = 4
OWNER = "BABAPBABAPBAPBAP"
POOL_QUADS = [q for q in range(QUADS) if OWNER[q] in "AB"]
VEC_QUADS = [q for q in range(QUADS) if OWNER[q] == "A"]
PE_QUADS = [q for q in range(QUADS) if OWNER[q] == "P"]


def pool_adds(q):
    return sum(1 + (OWNER[k] == "B") for k in POOL_QUADS if k <= q) - 1


def vec_adds(q):
    return sum(2 for k in VEC_QUADS if k <= q) - 1


def attend(nc, scratch, ident, ones, o_part, den_d):
    khi_d, klo_d, qhi_d, qlo_d, v_d = scratch
    with ExitStack() as ctx:
        def sb(name, shape, dt=F32):
            return ctx.enter_context(nc.sbuf_tensor(name, shape, dt))

        def ps(name, shape):
            return ctx.enter_context(nc.psum_tensor(name, shape, F32))

        def sem(name):
            return ctx.enter_context(nc.semaphore(name))

        KS, KM = 3 * HD, 3 * HD + 1
        keys = sb("keys", [P, 2, KEYS], F32R)
        q1 = sb("q1", [P, 2, S], F32R)
        q2 = sb("q2", [P, 2, S], F32R)
        vh = sb("vh", [P, 2, KT, HD])
        prob = sb("prob", [P, SLOTS, S])
        pool_sum = sb("pool_sum", [P, 2, 2 * S])
        vec_sum = sb("vec_sum", [P, 2, S])
        den_sb = sb("den_sb", [P, 2, S])
        parts = sb("parts", [P, C, PASSES // C])
        mx = sb("mx", [P, C])
        score = [ps(f"score{j}", [P, 512]) for j in range(2)]
        pass1 = [ps(f"pass1{j}", [P, 1024]) for j in range(2)]
        out_ps = ps("out_ps", [P, 512])
        den_ps = ps("den_ps", [P, 512])

        keys_in = [[sem(f"keys_in{u}{c}") for c in range(LOADS)] for u in range(2)]
        q1_in, q2_in, v_in = ([sem(f"{n}_in{u}") for u in range(2)] for n in ("q1", "q2", "v"))
        one_row = sem("one_row")
        p1_ready, part_done, mx_ready, turned, turn_copied = sem("p1_ready"), sem("part_done"), sem("mx_ready"), sem("turned"), sem("turn_copied")
        score_ready, exp_done, pv_done = sem("score_ready"), sem("exp_done"), sem("pv_done")
        pool_added, vec_added = sem("pool_added"), sem("vec_added")
        den_done, o_evac, den_evac, den_stored = sem("den_done"), sem("o_evac"), sem("den_evac"), sem("den_stored")

        block = ctx.enter_context(nc.Block())

        @block.sync
        def _(sp):
            def rows(h):
                return bass.ds(h * HD, HD)

            def load_q(q, q_in, h, u):
                for k, src in enumerate((qhi_d, qhi_d, qlo_d)):
                    sp.dma_start(q[k * HD:(k + 1) * HD, u, :].bitcast(F32), src[rows(h), :]).then_inc(q_in[u], 16)

            def load_keys(h, u, c):
                n = KEYS // LOADS
                for k, src in enumerate((khi_d, klo_d, khi_d)):
                    sp.dma_start(keys[k * HD:(k + 1) * HD, u, c * n:(c + 1) * n].bitcast(F32),
                                 src[rows(h), c * n:(c + 1) * n]).then_inc(keys_in[u][c], 16)

            def load_v(h, u):
                sp.dma_start(vh[:, u].rearrange("p k d -> p (k d)"),
                             v_d[bass.ds(h, 1)].rearrange("h p b n -> p (h b n)")).then_inc(v_in[u], 16)

            def store_den(h, u):
                sp.wait_ge(den_evac, h + 1)
                sp.dma_start(den_d[:, bass.ds(h, 1), :].rearrange("j h n -> j (h n)"),
                             den_sb[0:P:HD, u, :]).then_inc(den_stored, 16)

            for u in range(2):
                load_q(q1, q1_in, u, u)
                for c in range(LOADS):
                    load_keys(u, u, c)
            for u in range(2):
                load_q(q2, q2_in, u, u)
                load_v(u, u)
            with sp.Fori(0, H // 2 - 1) as i:
                for u in range(2):
                    h = 2 * i + u
                    sp.wait_ge(p1_ready, PASSES * (h + 1))
                    load_q(q1, q1_in, h + 2, u)
                    for c in range(LOADS):
                        sp.wait_ge(score_ready, KT * h + (c + 1) * KT // LOADS)
                        load_keys(h + 2, u, c)
                    load_q(q2, q2_in, h + 2, u)
                    sp.wait_ge(pv_done, QUADS * (h + 1))
                    load_v(h + 2, u)
                    store_den(h, u)
            for h in (H - 2, H - 1):
                store_den(h, h % 2)
            sp.wait_ge(den_stored, 16 * H)

        def maxima_slots(h, q):
            return [(1 + (2 * q + j + 2 * PV_LAG) // PASSES, (2 * q + j + 2 * PV_LAG) % PASSES) for j in range(2)]

        @block.tensor
        def _(pe):
            def slot(i, u, h, s, first, halves=(0, 1)):
                c, t = s // C, s % C
                if 0 in halves:
                    slot_waits(i, u, h, s, first)
                for j in halves:
                    m = pe.matmul(pass1[s % 2][:, j * 512:(j + 1) * 512], q1[0:KS, u, t * P:(t + 1) * P],
                                  keys[0:KS, u, c * 1024 + j * 512:c * 1024 + (j + 1) * 512], start=True, stop=True)
                if 1 in halves:
                    m.then_inc(p1_ready, 1)

            def slot_waits(i, u, h, s, first):
                if s % (PASSES // LOADS) == 0:
                    pe.wait_ge(keys_in[u][s // (PASSES // LOADS)], 48 * (i + 1))
                if s == 0:
                    pe.wait_ge(q1_in[u], 48 * (i + 1))
                if not (first and s < 2):
                    pe.wait_ge(part_done, PASSES * h + s - 1)
                if s == 1 and not first:
                    pe.wait_ge(turn_copied, h)

            def turn(h):
                pe.wait_ge(mx_ready, h + 1)
                for t in range(C):
                    m = pe.matmul(pass1[1][0:1, t * P:(t + 1) * P], mx[:, t:t + 1], ident[:, :], start=True, stop=True)
                m.then_inc(turned, 1)

            def scores(i, u, h, k, first):
                if not (first and u == 0 and k < 2):
                    pe.wait_ge(exp_done, KT * h + k - 1)
                if k == 0:
                    pe.wait_ge(q2_in[u], 48 * (i + 1))
                    pe.wait_ge(turn_copied, h + 1)
                pe.matmul(score[k % 2][:, :], keys[0:KM, u, k * P:(k + 1) * P], q2[0:KM, u, :],
                          start=True, stop=True).then_inc(score_ready, 1)

            def values(i, u, h, q, first):
                pe.wait_ge(exp_done, KT * h + 4 * q + 4)
                if q == 0:
                    pe.wait_ge(v_in[u], 16 * (i + 1))
                    if not first:
                        pe.wait_ge(o_evac, h)
                if q == PE_QUADS[0] and not first:
                    pe.wait_ge(den_evac, h)
                if q in PE_QUADS:
                    for j in range(4):
                        pe.matmul(den_ps[j * HD:(j + 1) * HD, :], ones[:, 0:HD], prob[:, (4 * q + j) % SLOTS, :],
                                  start=q == PE_QUADS[0], stop=j == 3 and q == PE_QUADS[-1])
                for j in range(4):
                    m = pe.matmul(out_ps[j * HD:(j + 1) * HD, :], vh[:, u, 4 * q + j, :], prob[:, (4 * q + j) % SLOTS, :],
                                  start=q == 0, stop=q == QUADS - 1)
                m.then_inc(pv_done, 1)
                if q == QUADS - 1:
                    pe.wait_ge(pool_added, pool_adds(QUADS) * (h + 1))
                    pe.wait_ge(vec_added, vec_adds(QUADS) * (h + 1))
                    for j, part in enumerate((pool_sum[:, u, 0:S], pool_sum[:, u, S:2 * S], vec_sum[:, u, :])):
                        m = pe.matmul(den_ps[j * HD:(j + 1) * HD, :], ones[:, 0:HD], part, start=False, stop=True)
                    m.then_inc(den_done, 1)

            def pair(i, first, last):
                for u in range(2):
                    h = 2 * i + u
                    for q in range(QUADS):
                        (da, sa), (db, sb_) = maxima_slots(h, q)
                        run = not last or u + da < 2
                        scores(i, u, h, 4 * q, first)
                        if run:
                            slot(i + (u + da) // 2, (u + da) % 2, h + da, sa, False)
                        scores(i, u, h, 4 * q + 1, first)
                        if sa == 0 and not (last and u == 1):
                            turn(h + da - 1)
                        if q >= PV_LAG:
                            values(i, u, h, q - PV_LAG, first and u == 0)
                        elif u == 1:
                            values(i, 0, h - 1, q + QUADS - PV_LAG, first)
                        elif not first:
                            values(i - 1, 1, h - 1, q + QUADS - PV_LAG, False)
                        scores(i, u, h, 4 * q + 2, first)
                        if run:
                            slot(i + (u + db) // 2, (u + db) % 2, h + db, sb_, False, (0,))
                        scores(i, u, h, 4 * q + 3, first)
                        if run:
                            slot(i + (u + db) // 2, (u + db) % 2, h + db, sb_, False, (1,))

            for s in range(PASSES):
                slot(0, 0, 0, s, True)
            for s in range(2 * PV_LAG):
                slot(0, 1, 1, s, False)
                if s == 0:
                    pe.wait_ge(one_row, 2)
                    turn(0)
            pair(0, True, False)
            with pe.Fori(1, H // 2 - 1) as i:
                pair(i, False, False)
            pair(H // 2 - 1, False, True)
            for q in range(QUADS - PV_LAG, QUADS):
                values(H // 2 - 1, 1, H - 1, q, False)

        @block.vector
        def _(dve):
            def slot(h, s, first):
                dve.wait_ge(p1_ready, PASSES * h + s + 1)
                if s == 0 and not first:
                    dve.wait_ge(mx_ready, h)
                dve.tensor_reduce(parts[:, s % C, s // C:s // C + 1], pass1[s % 2][:, :], AX.X, ALU.max).then_inc(part_done, 1)
                if s == PASSES - 1:
                    dve.wait_ge(part_done, PASSES * (h + 1))
                    if not first:
                        dve.wait_ge(turned, h)
                    dve.tensor_reduce(mx[:, :], parts[:, :, :], AX.X, ALU.max).then_inc(mx_ready, 1)

            def add(u, h, q, j, first):
                total, done = vec_adds(QUADS), vec_adds(q) - 2 + j - 2
                tiles = [prob[:, (4 * q + k) % SLOTS, :] for k in range(4)]
                if q == VEC_QUADS[0]:
                    if j == 2:
                        dve.wait_ge(exp_done, KT * h + 4 * q + 4)
                        if not first:
                            dve.wait_ge(den_done, h - 1)
                        dve.tensor_tensor(vec_sum[:, u, :], tiles[2], tiles[3], ALU.add).then_inc(vec_added, 1)
                    return
                dve.wait_ge(exp_done, KT * h + 4 * q + j + 1)
                dve.wait_ge(vec_added, total * h + done)
                dve.tensor_tensor(vec_sum[:, u, :], tiles[j], vec_sum[:, u, :], ALU.add).then_inc(vec_added, 1)

            def pair(i, first, last):
                for u in range(2):
                    h = 2 * i + u
                    for q in range(QUADS):
                        for (d, s), j in zip(maxima_slots(h, q), (2, 3)):
                            if not last or u + d < 2:
                                slot(h + d, s, False)
                            if q - 1 in VEC_QUADS:
                                add(u, h, q - 1, j, first)

            for s in range(PASSES):
                slot(0, s, True)
            for s in range(2 * PV_LAG):
                slot(1, s, False)
            pair(0, True, False)
            with dve.Fori(1, H // 2 - 1) as i:
                pair(i, False, False)
            pair(H // 2 - 1, False, True)

        @block.gpsimd
        def _(pool):
            def add(u, h, q, first):
                total, done = pool_adds(QUADS), pool_adds(q) - 1 - (OWNER[q] == "B")
                two = prob[:, (4 * q) % SLOTS:(4 * q) % SLOTS + 4, :].rearrange("p (a b) n -> p a (b n)", a=2)
                if q == POOL_QUADS[0]:
                    pool.wait_ge(exp_done, KT * h + 4 * q + 4)
                    if not first:
                        pool.wait_ge(den_done, h - 1)
                    pool.tensor_tensor(pool_sum[:, u, :], two[:, 0], two[:, 1], ALU.add).then_inc(pool_added, 1)
                else:
                    for a in range(1 + (OWNER[q] == "B")):
                        pool.wait_ge(exp_done, KT * h + 4 * q + 2 * a + 2)
                        pool.wait_ge(pool_added, total * h + done + a)
                        pool.tensor_tensor(pool_sum[:, u, :], two[:, a], pool_sum[:, u, :], ALU.add).then_inc(pool_added, 1)

            pool.memset(keys[KS:KM, 0, :].bitcast(F32), 1.0).then_inc(one_row, 1)
            pool.memset(keys[KS:KM, 1, :].bitcast(F32), 1.0).then_inc(one_row, 1)
            for u in range(2):
                for q in POOL_QUADS:
                    add(u, u, q, True)
            with pool.Fori(1, H // 2) as i:
                for u in range(2):
                    for q in POOL_QUADS:
                        add(u, 2 * i + u, q, False)

        @block.scalar
        def _(act):
            def exponentials(u, h, q, js, first):
                for j in js:
                    k = 4 * q + j
                    if j == 0:
                        back, at = (0, q - 4) if q >= 4 else (1, q - 4 + QUADS)
                        if not (first and u == 0 and back):
                            act.wait_ge(pv_done, QUADS * (h - back) + at + 1)
                            if at in POOL_QUADS:
                                act.wait_ge(pool_added, pool_adds(QUADS) * (h - back) + pool_adds(at))
                            if at in VEC_QUADS:
                                act.wait_ge(vec_added, vec_adds(QUADS) * (h - back) + vec_adds(at))
                    act.wait_ge(score_ready, KT * h + k + 1)
                    act.activation(prob[:, k % SLOTS, :], score[k % 2][:, :], ACT.Exp, scale=1.0 / math.sqrt(HD)).then_inc(exp_done, 1)

            def copy_turn(u, h):
                act.wait_ge(turned, h + 1)
                act.activation(q2[KS:KM, u, :], pass1[1][0:1, 0:S], ACT.Copy, scale=-1.0).then_inc(turn_copied, 1)

            def evacuate(u, h, first):
                act.wait_ge(pv_done, QUADS * (h + 1))
                act.activation(o_part[:, bass.ds(h, 1), :].rearrange("p h n -> p (h n)"), out_ps[:, :], ACT.Copy).then_inc(o_evac, 1)
                act.wait_ge(den_done, h + 1)
                if not (first and h == 0):
                    act.wait_ge(den_stored, 16 * h)
                act.activation(den_sb[:, u, :], den_ps[:, :], ACT.Copy).then_inc(den_evac, 1)

            def pair(i, first, last):
                for u in range(2):
                    h = 2 * i + u
                    for q in range(QUADS):
                        exponentials(u, h, q, (0, 1), first)
                        (da, sa), _ = maxima_slots(h, q)
                        if sa == 0 and not (last and u == 1):
                            copy_turn((u + da - 1) % 2, h + da - 1)
                        exponentials(u, h, q, (2, 3), first)
                        if q == PV_LAG - 1 and not (first and u == 0):
                            evacuate((u + 1) % 2, h - 1, first)

            copy_turn(0, 0)
            pair(0, True, False)
            with act.Fori(1, H // 2 - 1) as i:
                pair(i, False, False)
            pair(H // 2 - 1, False, True)
            evacuate(1, H - 1, False)


def finish(nc, ins, out, ident, ones, o_part, den_d):
    E = ins["experts"].shape[0]
    with ExitStack() as ctx:
        def sb(name, shape, dt=F32):
            return ctx.enter_context(nc.sbuf_tensor(name, shape, dt))

        def sem(name):
            return ctx.enter_context(nc.semaphore(name))

        W = sb("w_small", [P, 4, C, D])
        RING = 4
        ex = sb("experts_sb", [P, RING, C, D])
        x4 = sb("res", [P, C, D])
        xn = sb("xn3", [P, C, D])
        xnT = sb("xnT3", [P, C, S])
        attT = sb("attT", [P, C, S])
        qT = sb("qT", [P, C, S])
        kT = sb("kT", [P, C, S])
        v = sb("v_lin", [P, C, D])
        widths = [S - t * P for t in range(C)]
        starts = [sum(widths[:t]) for t in range(C)]
        A = sb("masked", [P, 4, sum(widths)])
        tmp = sb("tmp", [P, 2, S])
        tmp2 = sb("tmp2", [P, 2, S])
        den64 = sb("den64", [4 * H, S])
        rden = sb("rden", [H, S])
        sel16 = sb("sel16", [4 * H, H])
        sel32 = sb("sel32", [P, HD])
        spread = sb("spread", [H, C, P])
        mask = sb("mask", [P, S])
        cols = sb("bias_cols", [P, 3, C])
        rows = sb("bias_rows", [1, 3, D])
        rw = sb("router", [P, C, E])
        rbias = sb("router_bias", [1, E])
        iota = sb("iota", [P, E])
        stats = sb("stats3", [P, C, 6])
        mv = sb("mv3", [P, C, 2])
        rstd = sb("rstd3", [P, 3 * C])
        pr = sb("pr", [P, C, E])
        top = sb("top", [P, C, 8])
        topi = sb("topi", [P, C, 8], U32)
        topf = sb("topf", [P, C, 8])
        small = sb("small", [P, 8, C])
        coef = sb("coef", [P, C, E])
        coef2 = sb("coef2", [P, C, E])
        bank = [ctx.enter_context(nc.psum_tensor(f"fin{j}", [P, 512], F32)) for j in range(8)]

        consts, den_in, x_in, biases_in = sem("consts"), sem("den_in"), sem("x3_in"), sem("biases_in")
        w_in = [sem(f"w3_in{j}") for j in range(5)]
        ex_in = [sem(f"ex_in{j}") for j in range(RING)]
        pe_done, act_done, vec = sem("pe_done"), sem("act_done"), sem("vec_chain3")
        den16_ps, rden_ready, spread_ps, spread_sb, o_sum, att_mul, att_ready = (sem(n) for n in (
            "den16_ps", "rden_ready", "spread_ps", "spread_sb", "o_sum", "att_mul", "att_ready"))
        wo_ps, res_ready = sem("wo_ps"), sem("res_ready")
        var_ready, std_ready, xn_ready, xnT_ps, xnT_ready = (sem(n) for n in ("var3", "std3", "xn3_ready", "xnT3_ps", "xnT3_ready"))
        qk_ps, neg_ready, elu_parts, qk_ready, v_ps, v_ready = (sem(n) for n in ("qk_ps", "neg_ready", "elu_parts", "qk_ready", "v_ps", "v3_ready"))
        a_ps, a_ready, lin_ps, den_plus, lin_ready = (sem(n) for n in ("a_ps", "a_ready", "lin_ps", "den_plus", "lin_ready"))
        logit_ps, negmax, exps, coef_ready, y_ps, y_added, stored = (sem(n) for n in (
            "logit_ps", "negmax", "exps", "coef_ready", "y_ps", "y_added", "stored"))

        CONSTS = 1 + 4 + 1 + 4 + 1 + 1 + 1 + 1 + 1

        block = ctx.enter_context(nc.Block())

        def chunks(a):
            return a.rearrange("(c p) n -> p c n", p=P)

        @block.sync
        def _(sp):
            sp.dma_start(den64[:, :], den_d.rearrange("j h n -> (j h) n")).then_inc(den_in, 16)
            sp.dma_start(W[:, 0], chunks(ins["xWo"])).then_inc(w_in[0], 16)
            sp.dma_start(x4[:, :, :], chunks(ins["x"])).then_inc(x_in, 16)
            sp.dma_start(cols[:, :, :], ins["bias_cols"]).then_inc(biases_in, 16)
            sp.dma_start(rows[:, :, :], ins["bias_rows"]).then_inc(biases_in, 16)
            sp.dma_start(rbias[:, :], ins["router_b"]).then_inc(biases_in, 16)
            sp.dma_start(rw[:, :, :], chunks(ins["router_wT"])).then_inc(biases_in, 16)
            for j, name in enumerate(("aWq", "aWk", "aWv")):
                sp.dma_start(W[:, 1 + j], chunks(ins[name])).then_inc(w_in[1 + j], 16)
            for e in range(RING):
                sp.dma_start(ex[:, e], chunks(ins["experts"][e])).then_inc(ex_in[e], 16)
            sp.wait_ge(wo_ps, C)
            sp.dma_start(W[:, 0], chunks(ins["aWo"])).then_inc(w_in[4], 16)
            for e in range(RING, E):
                sp.wait_ge(y_ps, C * (e - RING + 1))
                sp.dma_start(ex[:, e % RING], chunks(ins["experts"][e])).then_inc(ex_in[e % RING], 16)
            for t in range(C):
                sp.wait_ge(y_added, C * (E - 1) + t + 1)
                sp.dma_start(out[t * P:(t + 1) * P, :], x4[:, t, :]).then_inc(stored, 16)
            sp.wait_ge(stored, 16 * C)

        @block.gpsimd
        def _(pool):
            link = Chain(pool, consts)
            link(pool.memset(sel16[:, :], 0.0))
            for j in range(4):
                link(pool.affine_select(out=sel16[:, :], in_=sel16[:, :], compare_op=ALU.not_equal, fill=1.0,
                                        base=-H * j, pattern=[[-1, H]], channel_multiplier=1))
            link(pool.memset(sel32[:, :], 0.0))
            for j in range(4):
                link(pool.affine_select(out=sel32[:, :], in_=sel32[:, :], compare_op=ALU.not_equal, fill=1.0,
                                        base=-HD * j, pattern=[[-1, HD]], channel_multiplier=1))
            link(pool.memset(spread[:, :, :], 0.0))
            sp_v = spread[:, :, :].rearrange("h c (l d) -> h c l d", d=HD)
            link(pool.affine_select(out=sp_v, in_=sp_v, compare_op=ALU.not_equal, fill=1.0,
                                    base=0, pattern=[[-4, C], [-1, 4], [0, HD]], channel_multiplier=1))
            link(pool.memset(mask[:, :], 1.0))
            link(pool.affine_select(out=mask[:, :], in_=mask[:, :], compare_op=ALU.is_ge, fill=0.0,
                                    base=0, pattern=[[1, S]], channel_multiplier=-1))
            link(pool.iota(iota[:, :], pattern=[[1, E]], base=0, channel_multiplier=0,
                           allow_small_or_imprecise_dtypes=True))

        def norm_transpose(pe, n):
            for c in range(C):
                pe.wait_ge(xn_ready, C * n)
                for t in range(C):
                    m = pe.transpose(bank[c][:, t * P:(t + 1) * P], xn[:, t, c * P:(c + 1) * P], ident[:, :])
                m.then_inc(xnT_ps, 1)
            pe.wait_ge(xnT_ready, C * n)

        def out_projection(pe, n):
            for t in range(C):
                for c in range(C):
                    pe.matmul(bank[4 + t][:, :], attT[:, c, t * P:(t + 1) * P], W[:, 0, c, :], start=c == 0, stop=False)
                pe.matmul(bank[4 + t][:, :], ones[0:1, :], rows[0:1, 2 * n, :], start=False, stop=True).then_inc(wo_ps, 1)

        @block.tensor
        def _(pe):
            pe.wait_ge(consts, CONSTS)
            pe.wait_ge(den_in, 16)
            pe.matmul(bank[0][0:H, :], sel16[:, :], den64[:, :], start=True, stop=True).then_inc(den16_ps, 1)
            for g in range(C):
                for l in range(4):
                    m = pe.matmul(bank[4 + g][l * HD:(l + 1) * HD, :], sel32[:, :], o_part[:, 4 * g + l, :], start=True, stop=True)
                m.then_inc(o_sum, 1)
            pe.wait_ge(rden_ready, 1)
            for g in range(C):
                pe.matmul(bank[g][:, :], spread[:, g, :], rden[:, :], start=True, stop=True).then_inc(spread_ps, 1)
            pe.wait_ge(att_ready, C)
            pe.wait_ge(w_in[0], 16)
            pe.wait_ge(biases_in, 64)
            out_projection(pe, 0)
            norm_transpose(pe, 1)
            for k in range(2):
                pe.wait_ge(w_in[1 + k], 16)
                for g in range(C):
                    b = 4 * (1 - k) + g
                    for c in range(C):
                        m = pe.matmul(bank[b][:, :], W[:, 1 + k, c, g * P:(g + 1) * P], xnT[:, c, :], start=c == 0, stop=c == C - 1)
                    m.then_inc(qk_ps, 1)
            pe.wait_ge(w_in[3], 16)
            for t in range(C):
                pe.wait_ge(elu_parts, t + 1)
                for c in range(C):
                    pe.matmul(bank[4 + t][:, :], xnT[:, c, t * P:(t + 1) * P], W[:, 3, c, :], start=c == 0, stop=False)
                pe.matmul(bank[4 + t][:, :], ones[0:1, :], rows[0:1, 1, :], start=False, stop=True).then_inc(v_ps, 1)
            pe.wait_ge(qk_ready, 2 * C)
            n = 0
            for g in range(C):
                for l in range(4):
                    r = slice(l * HD, (l + 1) * HD)
                    for t in range(C):
                        if n >= 4:
                            pe.wait_ge(a_ready, n - 3)
                        pe.matmul(bank[n % 4][:, 0:widths[t]], kT[r, g, t * P:(t + 1) * P], qT[r, g, t * P:],
                                  start=True, stop=True).then_inc(a_ps, 1)
                        n += 1
                pe.wait_ge(v_ready, C)
                pe.wait_ge(a_ready, 16 * (g + 1))
                if g >= 2:
                    pe.wait_ge(lin_ready, g - 1)
                up, down = bank[4 + 2 * (g % 2)], bank[5 + 2 * (g % 2)]
                for t in range(C):
                    for ps, w in ((up, v), (down, None)):
                        for l in range(4):
                            lhs = ones[:, 0:HD] if w is None else w[:, t, (4 * g + l) * HD:(4 * g + l + 1) * HD]
                            m = pe.matmul(ps[l * HD:(l + 1) * HD, t * P:], lhs, A[:, l, starts[t]:starts[t] + widths[t]],
                                          start=t == 0, stop=t == C - 1)
                m.then_inc(lin_ps, 1)
            pe.wait_ge(lin_ready, C)
            pe.wait_ge(w_in[4], 16)
            out_projection(pe, 1)
            norm_transpose(pe, 2)
            for t in range(C):
                for c in range(C):
                    pe.matmul(bank[7][:, t * E:(t + 1) * E], xnT[:, c, t * P:(t + 1) * P], rw[:, c, :],
                              start=t == 0 and c == 0, stop=False, skip_group_check=True)
                m = pe.matmul(bank[7][:, t * E:(t + 1) * E], ones[0:1, :], rbias[0:1, :], start=False, stop=t == C - 1, skip_group_check=True)
            m.then_inc(logit_ps, 1)
            n = 0
            for e in range(E):
                pe.wait_ge(ex_in[e % RING], 16 * (e // RING + 1))
                for t in range(C):
                    if n >= 7:
                        pe.wait_ge(y_added, n - 6)
                    for c in range(C):
                        m = pe.matmul(bank[n % 7][:, :], xnT[:, c, t * P:(t + 1) * P], ex[:, e % RING, c, :], start=c == 0, stop=c == C - 1)
                    m.then_inc(y_ps, 1)
                    n += 1

        @block.scalar
        def _(act):
            def norm_scalar(n):
                act.wait_ge(var_ready, n)
                act.activation(rstd[:, C:2 * C], rstd[:, 0:C], ACT.Sqrt).then_inc(std_ready, 1)
                for c in range(C):
                    act.wait_ge(xnT_ps, C * (n - 1) + c + 1)
                    act.activation(xnT[:, c, :], bank[c][:, :], ACT.Copy).then_inc(xnT_ready, 1)

            act.wait_ge(biases_in, 64)
            for g in range(C):
                act.wait_ge(spread_ps, g + 1)
                if g >= 2:
                    act.wait_ge(att_mul, g - 1)
                act.activation(tmp[:, g % 2, :], bank[g][:, :], ACT.Copy).then_inc(spread_sb, 1)
            for g in range(C):
                act.wait_ge(att_mul, g + 1)
                act.activation(attT[:, g, :], attT[:, g, :], ACT.Identity, bias=cols[:, 0, g:g + 1]).then_inc(att_ready, 1)
            norm_scalar(1)
            for n in range(2 * C):
                k, g = n // C, n % C
                act.wait_ge(neg_ready, n + 1)
                act.activation(tmp[:, n % 2, :], tmp[:, n % 2, :], ACT.Exp).then_inc(act_done, 1)
                act.wait_ge(qk_ps, n + 1)
                act.activation((qT, kT)[k][:, g, :], bank[4 * (1 - k) + g][:, :], ACT.Relu, bias=cols[:, 1 + k, g:g + 1]).then_inc(elu_parts, 1)
            for t in range(C):
                act.wait_ge(v_ps, t + 1)
                act.activation(v[:, t, :], bank[4 + t][:, :], ACT.Copy).then_inc(v_ready, 1)
            for g in range(C):
                act.wait_ge(lin_ps, g + 1)
                if g >= 2:
                    act.wait_ge(lin_ready, g - 1)
                act.activation(tmp[:, g % 2, :], bank[5 + 2 * (g % 2)][:, :], ACT.Copy, bias=1e-6).then_inc(den_plus, 1)
            norm_scalar(2)
            act.wait_ge(negmax, 1)
            for t in range(C):
                act.activation(pr[:, t, :], bank[7][:, t * E:(t + 1) * E], ACT.Exp, bias=small[:, 0, t:t + 1],
                               accum_out=small[:, 1, t:t + 1]).then_inc(exps, 1)

        @block.vector
        def _(dve):
            link = Chain(dve, vec)
            dve.wait_ge(den16_ps, 1)
            dve.reciprocal(rden[:, :], bank[0][0:H, :]).then_inc(rden_ready, 1)
            for g in range(C):
                dve.wait_ge(spread_sb, g + 1)
                dve.wait_ge(o_sum, g + 1)
                dve.tensor_tensor(attT[:, g, :], bank[4 + g][:, :], tmp[:, g % 2, :], ALU.mult).then_inc(att_mul, 1)

            def residual(n):
                for t in range(C):
                    dve.wait_ge(wo_ps, C * n + t + 1)
                    link(dve.tensor_tensor(x4[:, t, :], bank[4 + t][:, :], x4[:, t, :], ALU.add))
                norm_on_vector(dve, link, x4, xn, stats, mv, rstd, var_ready, std_ready, xn_ready, n + 1)

            dve.wait_ge(x_in, 16)
            residual(0)
            for n in range(2 * C):
                k, g = n // C, n % C
                dve.wait_ge(qk_ps, n + 1)
                if n >= 2:
                    dve.wait_ge(qk_ready, n - 1)
                dve.tensor_scalar(tmp[:, n % 2, :], bank[4 * (1 - k) + g][:, :], cols[:, 1 + k, g:g + 1], 0.0, ALU.add, ALU.min).then_inc(neg_ready, 1)
                dve.wait_ge(act_done, n + 1)
                dve.wait_ge(elu_parts, n + 1)
                dst = (qT, kT)[k][:, g, :]
                dve.tensor_tensor(dst, dst, tmp[:, n % 2, :], ALU.add).then_inc(qk_ready, 1)
            n = 0
            for g in range(C):
                for l in range(4):
                    for t in range(C):
                        dve.wait_ge(a_ps, n + 1)
                        if g >= 1:
                            dve.wait_ge(lin_ps, g)
                        dve.tensor_tensor(A[:, l, starts[t]:starts[t] + widths[t]], bank[n % 4][:, 0:widths[t]],
                                          mask[:, 0:widths[t]], ALU.mult).then_inc(a_ready, 1)
                        n += 1
                dve.wait_ge(den_plus, g + 1)
                link(dve.reciprocal(tmp2[:, g % 2, :], tmp[:, g % 2, :]))
                dve.tensor_tensor(attT[:, g, :], bank[4 + 2 * (g % 2)][:, :], tmp2[:, g % 2, :], ALU.mult).then_inc(lin_ready, 1)
            residual(1)
            dve.wait_ge(logit_ps, 1)
            logits = bank[7][:, 0:C * E].rearrange("p (t e) -> p t e", e=E)
            dve.tensor_reduce(small[:, 0, :], logits, AX.X, ALU.max, negate=True).then_inc(negmax, 1)
            dve.wait_ge(exps, C)
            link(dve.reciprocal(small[:, 2, :], small[:, 1, :]))
            for t in range(C):
                link(dve.tensor_scalar(pr[:, t, :], pr[:, t, :], small[:, 2, t:t + 1], None, ALU.mult))
            for t in range(C):
                link(dve.max(top[:, t, :], pr[:, t, :]))
            for t in range(C):
                link(dve.max_index(topi[:, t, :], top[:, t, :], pr[:, t, :]))
            link(dve.tensor_copy(topf[:, :, :], topi[:, :, :]))
            p1, p2 = top[:, :, 0], top[:, :, 1]
            link(dve.tensor_tensor(small[:, 3, :], p1, p2, ALU.add))
            link(dve.tensor_scalar(small[:, 3, :], small[:, 3, :], 1e-10, None, ALU.add))
            link(dve.reciprocal(small[:, 3, :], small[:, 3, :]))
            link(dve.tensor_tensor(small[:, 4, :], p1, small[:, 3, :], ALU.mult))
            link(dve.tensor_tensor(small[:, 5, :], p2, small[:, 3, :], ALU.mult))
            link(dve.tensor_tensor(small[:, 6, :], small[:, 4, :], small[:, 5, :], ALU.add))
            link(dve.tensor_scalar(small[:, 7, :], small[:, 6, :], 1e-10, None, ALU.max))
            link(dve.reciprocal(small[:, 7, :], small[:, 7, :]))
            link(dve.tensor_scalar(small[:, 6, :], small[:, 6, :], 1e-10, 1.0, ALU.mult, ALU.add))
            link(dve.tensor_tensor(small[:, 7, :], small[:, 7, :], small[:, 6, :], ALU.mult))
            link(dve.tensor_tensor(small[:, 4, :], small[:, 4, :], small[:, 7, :], ALU.mult))
            link(dve.tensor_tensor(small[:, 5, :], small[:, 5, :], small[:, 7, :], ALU.mult))
            for t in range(C):
                link(dve.tensor_scalar(coef[:, t, :], iota[:, :], topf[:, t, 0:1], small[:, 4, t:t + 1], ALU.is_equal, ALU.mult))
                link(dve.tensor_scalar(coef2[:, t, :], iota[:, :], topf[:, t, 1:2], small[:, 5, t:t + 1], ALU.is_equal, ALU.mult))
            link(dve.tensor_tensor(coef[:, :, :], coef[:, :, :], coef2[:, :, :], ALU.add))
            n = 0
            for e in range(E):
                for t in range(C):
                    dve.wait_ge(y_ps, n + 1)
                    if e:
                        dve.wait_ge(y_added, n - C + 1)
                    dve.scalar_tensor_tensor(x4[:, t, :], bank[n % 7][:, :], coef[:, t, e:e + 1], x4[:, t, :],
                                             ALU.mult, ALU.add).then_inc(y_added, 1)
                    n += 1


def perceiver(nc, ins, out):
    khi_d = nc.dram_tensor("keys_high", (D, KEYS), F32, kind="Internal").ap()
    klo_d = nc.dram_tensor("keys_low", (D, KEYS), F32, kind="Internal").ap()
    qhi_d = nc.dram_tensor("queries_high", (D, S), F32, kind="Internal").ap()
    qlo_d = nc.dram_tensor("queries_low", (D, S), F32, kind="Internal").ap()
    v_d = nc.dram_tensor("values", (H, P, BLOCKS, C * HD), F32, kind="Internal").ap()
    den_d = nc.dram_tensor("denominators", (4, H, S), F32, kind="Internal").ap()
    scratch = (khi_d, klo_d, qhi_d, qlo_d, v_d)
    with ExitStack() as ctx:
        ident = ctx.enter_context(nc.sbuf_tensor("ident", [P, P], F32))
        ones = ctx.enter_context(nc.sbuf_tensor("ones", [P, P], F32))
        project_context(nc, ins, scratch, ident, ones)
        o_part = ctx.enter_context(nc.sbuf_tensor("o_part", [P, H, S], F32))
        attend(nc, scratch, ident, ones, o_part, den_d)
        finish(nc, ins, out, ident, ones, o_part, den_d)


def kernel(**inputs):
    import concourse.bacc as bacc
    from concourse.bass_utils import run_bass_kernel_spmd

    a = {k: np.asarray(v) for k, v in inputs.items()}

    def column(b):
        return b.reshape(C, P).T

    arrays = {
        "x": a["x"][0], "ctxT": a["ctx_1024"][0].T,
        "xWq": a["L0_xattn_Wq"], "xWk": a["L0_xattn_Wk"], "xWv": a["L0_xattn_Wv"], "xWo": a["L0_xattn_Wo"],
        "xbq_col": column(a["L0_xattn_bq"]), "xbk_col": column(a["L0_xattn_bk"]),
        "aWq": a["L0_attn_Wq"], "aWk": a["L0_attn_Wk"], "aWv": a["L0_attn_Wv"], "aWo": a["L0_attn_Wo"],
        "bias_cols": np.stack([column(a[n]) for n in ("L0_xattn_bv", "L0_attn_bq", "L0_attn_bk")], axis=1),
        "bias_rows": np.stack([a[n] for n in ("L0_xattn_bo", "L0_attn_bv", "L0_attn_bo")])[None],
        "router_wT": a["L0_ffn_router_w"].T, "router_b": a["L0_ffn_router_b"][None],
        "experts": a["L0_ffn_expert_weights"],
    }
    nc = bacc.Bacc("TRN2", target_bir_lowering=False, num_devices=1)
    arrays = {f"in_{k}": np.ascontiguousarray(v) for k, v in arrays.items()}
    ins = {k[3:]: nc.dram_tensor(k, v.shape, mybir.dt.from_np(v.dtype), kind="ExternalInput").ap() for k, v in arrays.items()}
    out = nc.dram_tensor("out", (S, D), F32, kind="ExternalOutput").ap()
    perceiver(nc, ins, out)
    r = run_bass_kernel_spmd(nc, [arrays], core_ids=[0])
    return r.results[0]["out"].reshape(1, S, D)
```

```python
import math
from contextlib import ExitStack

import numpy as np

import concourse.bass as bass
from concourse import mybir

F32 = mybir.dt.float32
F32R = mybir.dt.float32r
U32 = mybir.dt.uint32
ACT = mybir.ActivationFunctionType
ALU = mybir.AluOpType
AX = mybir.AxisListType

P = 128
S = 512
D = 512
C = D // P
KEYS = 8192
H = 16
HD = D // H
KB = 512
BLOCKS = KEYS // KB
KT = KEYS // P
EPS = 1e-5

QUADS = KT // 4
SLOTS = 16
AHEAD = 8
PV_LAG = 2
UNITS = C * (KEYS // 512)
PARTS = UNITS + 1
BANKS = 3
LOADS = 4
OWNER = "BABAPBABAPBAPBAP"
POOL_QUADS = [q for q in range(QUADS) if OWNER[q] in "AB"]
VEC_QUADS = [q for q in range(QUADS) if OWNER[q] == "A"]
PE_QUADS = [q for q in range(QUADS) if OWNER[q] == "P"]


class Chain:

    def __init__(self, eng, sem):
        self.eng, self.sem, self.n = eng, sem, 0

    def __call__(self, instruction):
        self.n += 1
        instruction.then_inc(self.sem, 1)
        self.eng.wait_ge(self.sem, self.n)


def norm_on_vector(dve, link, x4, xn, stats, mv, rstd, var_ready, std_ready, xn_ready, n):
    for t in range(C):
        link(dve.bn_stats(stats[:, t, :], x4[:, t, :]))
    for t in range(C):
        link(dve.bn_aggr(mv[:, t, :], stats[:, t, :]))
    dve.tensor_scalar(rstd[:, 0:C], mv[:, :, 1], EPS, None, ALU.add).then_inc(var_ready, 1)
    dve.wait_ge(std_ready, n)
    link(dve.reciprocal(rstd[:, 2 * C:3 * C], rstd[:, C:2 * C]))
    for t in range(C):
        dve.tensor_scalar(xn[:, t, :], x4[:, t, :], mv[:, t, 0:1],
                          rstd[:, 2 * C + t:2 * C + t + 1], ALU.subtract, ALU.mult).then_inc(xn_ready, 1)


def project_context(nc, ins, scratch, ident, ones, stacks, maxima, room):
    khi_d, klo_d, qhi_d, qlo_d, v_d = scratch
    keys, q1, q2 = stacks
    parts, mx, p1_ready, part_done, turned, turn_copied = maxima
    with ExitStack() as ctx:
        def sb(name, shape, dt=F32):
            return ctx.enter_context(nc.sbuf_tensor(name, shape, dt))

        def sem(name):
            return ctx.enter_context(nc.semaphore(name))

        whi = sb("whi", [P, 2, C, D], F32R)
        wlo = sb("wlo", [P, 2, C, D], F32R)
        chi = sb("chi", [P, 2, C, KB], F32R)
        clo = sb("clo", [P, 2, C, KB], F32R)
        khi = sb("khi", [P, 2, C, KB], F32R)
        klo = sb("klo", [P, 2, C, KB], F32R)
        craw, vrows, xs, wraw = (room[:, j * C:(j + 1) * C, :] for j in range(4))
        vout = vrows.rearrange("p c (h n) -> p (c h n)", n=C * HD).rearrange("p (h k d) -> p h k d", h=H, k=C)
        bq = sb("bq_sb", [P, C])
        bk = sb("bk_sb", [P, C])
        stats = sb("stats", [P, C, 6])
        mv = sb("mv", [P, C, 2])
        rstd = sb("rstd", [P, 3 * C])
        bank = [ctx.enter_context(nc.psum_tensor(f"proj{j}", [P, 512], F32)) for j in range(8)]

        first_in = [sem(f"first_in{c}") for c in range(C)]
        first_hi, first_lo = sem("first_hi"), sem("first_lo")
        x_in, wv_in, wq_in, bias_in, ident_done = sem("x_in"), sem("wv_in"), sem("wq_in"), sem("bias_in"), sem("ident_done")
        ctx_in = sem("ctx_in")
        wv_hi, wv_lo, chi_done, clo_done = sem("wv_hi"), sem("wv_lo"), sem("chi_done"), sem("clo_done")
        var_ready, std_ready, xn_ready, xnT_psum, xnT_ready = sem("var_ready"), sem("std_ready"), sem("xn_ready"), sem("xnT_psum"), sem("xnT_ready")
        q_psum, qhi_done, qlo_done, q_stored = sem("q_psum"), sem("qhi_done"), sem("qlo_done"), sem("q_stored")
        proj_done = sem("proj_done")
        khi_done, klo_done = sem("khi_done"), sem("klo_done")
        va_done, vv_done = sem("va_done"), sem("vv_done")
        k_stored, v_stored = [sem("k_stored0"), sem("k_stored1")], sem("v_stored")
        k_stacked, q_stacked = [sem("k_stacked0"), sem("k_stacked1")], sem("q_stacked")
        vec = sem("vec_chain")

        ctxT = ins["ctxT"].rearrange("(c p) n -> p c n", p=P)
        khi_v = khi_d.rearrange("(c p) n -> p c n", p=P)
        klo_v = klo_d.rearrange("(c p) n -> p c n", p=P)
        qhi_v = qhi_d.rearrange("(c p) n -> p c n", p=P)
        qlo_v = qlo_d.rearrange("(c p) n -> p c n", p=P)
        v_v = v_d.rearrange("h p b n -> p h b n")

        qhi, qlo = khi[:, 1], klo[:, 1]
        wk_raw = vrows

        def w_v(name):
            return ins[name].rearrange("(c p) n -> p c n", p=P)

        block = ctx.enter_context(nc.Block())

        @block.sync
        def _(sp):
            for c in range(C):
                sp.dma_start(wk_raw[:, c, :], w_v("xWk")[:, c, :]).then_inc(first_in[c], 16)
                sp.dma_start(craw[:, c, :], ctxT[:, c, 0:KB]).then_inc(first_in[c], 16)
            sp.dma_start(bk[:, :], ins["xbk_col"]).then_inc(bias_in, 16)
            sp.dma_start(bq[:, :], ins["xbq_col"]).then_inc(bias_in, 16)
            sp.dma_start(wraw[:, :, :], w_v("xWv")).then_inc(wv_in, 16)
            sp.dma_start(xs[:, :, :], ins["x"].rearrange("(c p) n -> p c n", p=P)).then_inc(x_in, 16)
            sp.wait_ge(first_lo, 2 * C)
            sp.dma_start(craw[:, :, :], ctxT[:, :, KB:2 * KB]).then_inc(ctx_in, 16)
            sp.wait_ge(wv_lo, 1)
            sp.dma_start(wraw[:, :, :], w_v("xWq")).then_inc(wq_in, 16)

            def store_keys(u, b):
                sp.wait_ge(khi_done, C * (b + 1))
                sp.wait_ge(klo_done, C * (b + 1))
                for h in range(2):
                    for k, part in enumerate((khi, klo, khi)):
                        sp.dma_start(keys[k * HD:(k + 1) * HD, h, bass.ds(b * KB, KB)].bitcast(F32),
                                     part[h * HD:(h + 1) * HD, u, 0, :].bitcast(F32)).then_inc(k_stacked[u], 16)
                sp.dma_start(khi_v[:, :, bass.ds(b * KB, KB)], khi[:, u].bitcast(F32)).then_inc(k_stored[u], 16)
                sp.dma_start(klo_v[:, :, bass.ds(b * KB, KB)], klo[:, u].bitcast(F32)).then_inc(k_stored[u], 16)

            def load_ctx(b):
                sp.wait_ge(chi_done, b - 1)
                sp.wait_ge(clo_done, b - 1)
                sp.dma_start(craw[:, :, :], ctxT[:, :, bass.ds(b * KB, KB)]).then_inc(ctx_in, 16)

            def store_values(b):
                sp.wait_ge(va_done, 2 * (b + 1))
                sp.wait_ge(vv_done, 2 * (b + 1))
                sp.dma_start(v_v[:, :, bass.ds(b, 1), :].rearrange("p h b n -> p h (b n)"),
                             vout[:, :, :, :].rearrange("p h k d -> p h (k d)")).then_inc(v_stored, 16)

            def step(i, u, last):
                b = 2 * i + u
                store_keys(u, b)
                if not last:
                    load_ctx(b + 2)
                store_values(b)

            step(0, 0, False)
            sp.wait_ge(qhi_done, C)
            sp.wait_ge(qlo_done, C)
            for h in range(2):
                for q in (q1, q2):
                    for k, part in enumerate((qhi, qhi, qlo)):
                        sp.dma_start(q[k * HD:(k + 1) * HD, h, :].bitcast(F32),
                                     part[h * HD:(h + 1) * HD, 0, :].bitcast(F32)).then_inc(q_stacked, 16)
            sp.dma_start(qhi_v, qhi.bitcast(F32)).then_inc(q_stored, 16)
            sp.dma_start(qlo_v, qlo.bitcast(F32)).then_inc(q_stored, 16)
            step(0, 1, False)
            with sp.Fori(1, BLOCKS // 2 - 1) as i:
                for u in range(2):
                    step(i, u, False)
            for u in range(2):
                step(BLOCKS // 2 - 1, u, True)
            for u in range(2):
                sp.wait_ge(k_stored[u], 16 * BLOCKS)
                sp.wait_ge(k_stacked[u], 48 * BLOCKS)
            sp.wait_ge(v_stored, 16 * BLOCKS)
            sp.wait_ge(q_stored, 32)

        @block.gpsimd
        def _(pool):
            pool.memset(ident[:, :], 0.0).then_inc(ident_done, 1)
            pool.memset(ones[:, :], 1.0)
            pool.wait_ge(ident_done, 1)
            pool.affine_select(out=ident[:, :], in_=ident[:, :], compare_op=ALU.not_equal, fill=1.0,
                               base=0, pattern=[[-1, P]], channel_multiplier=1).then_inc(ident_done, 1)
            for h in range(2):
                pool.wait_ge(ident_done, 2 + h)
                pool.memset(keys[3 * HD:3 * HD + 1, h, :].bitcast(F32), 1.0).then_inc(ident_done, 1)

        @block.scalar
        def _(act):
            for c in range(C):
                act.wait_ge(first_in[c], 32)
                act.activation(whi[:, 0, c, :], wk_raw[:, c, :], ACT.Copy).then_inc(first_hi, 1)
                act.activation(chi[:, 0, c, :], craw[:, c, :], ACT.Copy).then_inc(first_hi, 1)
            act.wait_ge(wv_in, 16)
            act.activation(whi[:, 1], wraw[:, :, :], ACT.Copy).then_inc(wv_hi, 1)
            act.wait_ge(bias_in, 32)

            def keys_out(i, u, b, done):
                if isinstance(b, int) and b == 1:
                    act.wait_ge(q_stored, 32)
                    act.wait_ge(q_stacked, 16 * 12)
                elif not isinstance(b, int) or b > 1:
                    act.wait_ge(k_stored[u], 32 * i)
                    act.wait_ge(k_stacked[u], 96 * i)
                for g in range(C):
                    act.wait_ge(proj_done, done + g + 1)
                    act.activation(khi[:, u, g, :], bank[g][:, :], ACT.Identity, bias=bk[:, g:g + 1]).then_inc(khi_done, 1)

            def values_out(b, done, first):
                if not first:
                    act.wait_ge(v_stored, 16 * b)
                for t in range(2):
                    act.wait_ge(proj_done, done + t + 1)
                    act.activation(vout[:, :, t, :], bank[4 + t][:, :].rearrange("p (h d) -> p h d", d=HD),
                                   ACT.Copy).then_inc(va_done, 1)

            def split_next(b, u):
                act.wait_ge(ctx_in, 16 * (b + 1))
                act.activation(chi[:, 1 - u], craw[:, :, :], ACT.Copy).then_inc(chi_done, 1)

            def step(i, u, first, last):
                b = 2 * i + u
                keys_out(i, u, b, 8 * b)
                if not last:
                    split_next(b, u)
                values_out(b, 8 * b + 4, first)

            step(0, 0, True, False)
            act.wait_ge(var_ready, 1)
            act.activation(rstd[:, C:2 * C], rstd[:, 0:C], ACT.Sqrt).then_inc(std_ready, 1)
            act.wait_ge(xnT_psum, C)
            for c in range(C):
                act.activation(xs[:, c, :], bank[c][:, :], ACT.Copy).then_inc(xnT_ready, 1)
            for g in range(C):
                act.wait_ge(q_psum, g + 1)
                act.activation(qhi[:, g, :], bank[4 + g][:, :], ACT.Identity, bias=bq[:, g:g + 1]).then_inc(qhi_done, 1)
            split_next(1, 1)
            values_out(1, 8, False)
            keys_out(0, 1, 1, 10)
            with act.Fori(1, BLOCKS // 2 - 1) as i:
                for u in range(2):
                    step(i, u, False, False)
            for u in range(2):
                step(BLOCKS // 2 - 1, u, False, u == 1)
            act.wait_ge(turned, 1)
            act.activation(q2[3 * HD:3 * HD + 1, 0, :], bank[0][0:1, :], ACT.Copy, scale=-1.0).then_inc(turn_copied, 1)

        @block.vector
        def _(dve):
            link = Chain(dve, vec)
            for c in range(C):
                dve.wait_ge(first_hi, 2 * c + 2)
                dve.tensor_tensor(wlo[:, 0, c, :], wk_raw[:, c, :], whi[:, 0, c, :].bitcast(F32), ALU.subtract).then_inc(first_lo, 1)
                dve.tensor_tensor(clo[:, 0, c, :], craw[:, c, :], chi[:, 0, c, :].bitcast(F32), ALU.subtract).then_inc(first_lo, 1)
            dve.wait_ge(wv_hi, 1)
            dve.tensor_tensor(wlo[:, 1], wraw[:, :, :], whi[:, 1].bitcast(F32), ALU.subtract).then_inc(wv_lo, 1)
            dve.wait_ge(bias_in, 32)

            def maximum(b, t):
                n = C * b + t
                dve.wait_ge(p1_ready, n + 1)
                dve.tensor_reduce(parts[:, t, bass.ds(b, 1)], bank[6 + t % 2][:, :], AX.X, ALU.max).then_inc(part_done, 1)

            def keys_out(i, u, b):
                if isinstance(b, int) and b == 1:
                    dve.wait_ge(q_stored, 32)
                    dve.wait_ge(q_stacked, 16 * 12)
                elif not isinstance(b, int) or b > 1:
                    dve.wait_ge(k_stored[u], 32 * i)
                    dve.wait_ge(k_stacked[u], 96 * i)
                for g in range(C):
                    dve.wait_ge(khi_done, C * b + g + 1)
                    dve.scalar_tensor_tensor(klo[:, u, g, :], bank[g][:, :], bk[:, g:g + 1],
                                             khi[:, u, g, :].bitcast(F32), ALU.add, ALU.subtract).then_inc(klo_done, 1)
                    if not isinstance(b, int) or b > 0:
                        maximum(b - 1, g)

            def values_out(b, done, first):
                if not first:
                    dve.wait_ge(v_stored, 16 * b)
                for t in range(2, C):
                    dve.wait_ge(proj_done, done + t + 1)
                    dve.tensor_copy(vout[:, :, t, :], bank[2 + t][:, :].rearrange("p (h d) -> p h d", d=HD)).then_inc(vv_done, 1)

            def split_next(b, u):
                dve.wait_ge(chi_done, b + 1)
                dve.tensor_tensor(clo[:, 1 - u], craw[:, :, :], chi[:, 1 - u].bitcast(F32), ALU.subtract).then_inc(clo_done, 1)

            def step(i, u, last):
                b = 2 * i + u
                keys_out(i, u, b)
                if not last:
                    split_next(b, u)
                values_out(b, 8 * b + 4, False)

            keys_out(0, 0, 0)
            split_next(0, 0)
            dve.wait_ge(x_in, 16)
            norm_on_vector(dve, link, xs, xs, stats, mv, rstd, var_ready, std_ready, xn_ready, 1)
            values_out(0, 4, True)
            for g in range(C):
                dve.wait_ge(qhi_done, g + 1)
                dve.scalar_tensor_tensor(qlo[:, g, :], bank[4 + g][:, :], bq[:, g:g + 1],
                                         qhi[:, g, :].bitcast(F32), ALU.add, ALU.subtract).then_inc(qlo_done, 1)
            split_next(1, 1)
            keys_out(0, 1, 1)
            values_out(1, 12, False)
            with dve.Fori(1, BLOCKS // 2 - 1) as i:
                for u in range(2):
                    step(i, u, False)
            for u in range(2):
                step(BLOCKS // 2 - 1, u, u == 1)
            for t in range(C):
                maximum(BLOCKS - 1, t)
            dve.wait_ge(part_done, UNITS)
            dve.tensor_reduce(mx[:, :], parts[:, :, :], AX.X, ALU.max).then_inc(part_done, 1)
            dve.wait_ge(part_done, PARTS)
            for n in range(AHEAD):
                dve.wait_ge(p1_ready, UNITS + n + 1)
                dve.tensor_reduce(parts[:, n % C, n // C:n // C + 1], bank[6 + n % 2][:, :], AX.X, ALU.max).then_inc(part_done, 1)

        @block.tensor
        def _(pe):
            def unit(i, u, t, first):
                b = 2 * i + u
                n = C * b + t
                if t == 0:
                    pe.wait_ge(k_stacked[u], 96 * (i + 1))
                    if first:
                        pe.wait_ge(q_stacked, 16 * 12)
                if not (first and u == 0 and t < 2):
                    pe.wait_ge(part_done, n - 1)
                pe.matmul(bank[6 + t % 2][:, :], q1[0:3 * HD, 0, t * P:(t + 1) * P],
                          keys[0:3 * HD, 0, bass.ds(b * KB, KB)], start=True, stop=True).then_inc(p1_ready, 1)

            def key_products(u, g, c):
                for w, x, n in ((whi, chi, 0), (wlo, chi, 1), (whi, clo, 2)):
                    m = pe.matmul(bank[g][:, :], w[:, 0, c, g * P:(g + 1) * P], x[:, u, c, :],
                                  start=c == 0 and n == 0, stop=c == C - 1 and n == 2)
                return m

            def values(b, u, first, tiles=range(C)):
                for t in tiles:
                    if t >= 2:
                        pe.wait_ge(va_done, 2 * b + t - 1)
                    elif not first:
                        pe.wait_ge(vv_done, 2 * (b - 1) + t + 1)
                    for c in range(C):
                        for x, w, n in ((chi, whi, 0), (chi, wlo, 1), (clo, whi, 2)):
                            m = pe.matmul(bank[4 + t % 2][:, :], x[:, u, c, t * P:(t + 1) * P], w[:, 1, c, :],
                                          start=c == 0 and n == 0, stop=c == C - 1 and n == 2)
                    m.then_inc(proj_done, 1)

            for c in range(C):
                pe.wait_ge(first_lo, 2 * c + 2)
                for g in range(C):
                    m = key_products(0, g, c)
                    if c == C - 1:
                        m.then_inc(proj_done, 1)
            pe.wait_ge(wv_lo, 1)
            values(0, 0, True)
            pe.wait_ge(ident_done, 2)
            pe.wait_ge(xn_ready, C)
            for c in range(C):
                pe.wait_ge(klo_done, c + 1)
                for t in range(C):
                    m = pe.transpose(bank[c][:, t * P:(t + 1) * P], xs[:, t, c * P:(c + 1) * P], ident[:, :])
                m.then_inc(xnT_psum, 1)
            pe.wait_ge(xnT_ready, C)
            pe.wait_ge(wq_in, 16)
            pe.wait_ge(vv_done, 2)
            for g in range(C):
                for c in range(C):
                    m = pe.matmul(bank[4 + g][:, :], wraw[:, c, g * P:(g + 1) * P], xs[:, c, :], start=c == 0, stop=c == C - 1)
                m.then_inc(q_psum, 1)

            def step(i, u, first):
                b = 2 * i + u
                pe.wait_ge(chi_done, b)
                pe.wait_ge(clo_done, b)
                if first:
                    pe.wait_ge(qlo_done, C)
                    values(b, u, False, (0, 1))
                for g in range(C):
                    if not first:
                        pe.wait_ge(klo_done, C * (b - 1) + g + 1)
                    for c in range(C):
                        m = key_products(u, g, c)
                    m.then_inc(proj_done, 1)
                    unit(i if u else i - 1, 1 - u, g, first)
                values(b, u, False, (2, 3) if first else range(C))

            step(0, 1, True)
            with pe.Fori(1, BLOCKS // 2) as i:
                for u in range(2):
                    step(i, u, False)
            for t in range(C):
                unit(BLOCKS // 2 - 1, 1, t, False)
            for n in range(AHEAD):
                c, t = n // C, n % C
                pe.wait_ge(part_done, UNITS + n - 1 + (n >= 2))
                pe.matmul(bank[6 + n % 2][:, :], q1[0:3 * HD, 1, t * P:(t + 1) * P],
                          keys[0:3 * HD, 1, c * KB:(c + 1) * KB], start=True, stop=True).then_inc(p1_ready, 1)
                if n == 1:
                    pe.wait_ge(part_done, PARTS)
                    for t in range(C):
                        m = pe.matmul(bank[0][0:1, t * P:(t + 1) * P], mx[:, t:t + 1], ident[:, :], start=True, stop=True)
                    m.then_inc(turned, 1)


def pool_adds(q):
    return sum(1 + (OWNER[k] == "B") for k in POOL_QUADS if k <= q) - 1


def vec_adds(q):
    return sum(2 for k in VEC_QUADS if k <= q) - 1


def attend(nc, scratch, ident, ones, stacks, maxima, o_part, den_d):
    khi_d, klo_d, qhi_d, qlo_d, v_d = scratch
    keys, q1, q2 = stacks
    parts, mx, p1_ready, part_done, turned, turn_copied = maxima
    with ExitStack() as ctx:
        def sb(name, shape, dt=F32):
            return ctx.enter_context(nc.sbuf_tensor(name, shape, dt))

        def ps(name, shape):
            return ctx.enter_context(nc.psum_tensor(name, shape, F32))

        def sem(name):
            return ctx.enter_context(nc.semaphore(name))

        KS, KM = 3 * HD, 3 * HD + 1
        vh = sb("vh", [P, 2, KT, HD])
        prob = sb("prob", [P, SLOTS, S])
        pool_sum = sb("pool_sum", [P, 2, 2 * S])
        vec_sum = sb("vec_sum", [P, 2, S])
        den_sb = sb("den_sb", [P, 2, S])
        score = [ps(f"score{j}", [P, 512]) for j in range(BANKS)]
        pass1 = [ps(f"pass1{j}", [P, 512]) for j in range(BANKS)]
        out_ps = ps("out_ps", [P, 512])
        den_ps = ps("den_ps", [P, 512])

        keys_in = [[sem(f"keys_in{u}{c}") for c in range(LOADS)] for u in range(2)]
        q1_in, q2_in, v_in = ([sem(f"{n}_in{u}") for u in range(2)] for n in ("q1", "q2", "v"))
        score_ready, exp_done, pv_done = sem("score_ready"), sem("exp_done"), sem("pv_done")
        pool_added, vec_added = sem("pool_added"), sem("vec_added")
        den_done, o_evac, den_evac, den_stored = sem("den_done"), sem("o_evac"), sem("den_evac"), sem("den_stored")

        block = ctx.enter_context(nc.Block())

        @block.sync
        def _(sp):
            def rows(h):
                return bass.ds(h * HD, HD)

            def load_q(q, q_in, h, u):
                for k, src in enumerate((qhi_d, qhi_d, qlo_d)):
                    sp.dma_start(q[k * HD:(k + 1) * HD, u, :].bitcast(F32), src[rows(h), :]).then_inc(q_in[u], 16)

            def load_keys(h, u, c):
                n = KEYS // LOADS
                for k, src in enumerate((khi_d, klo_d, khi_d)):
                    sp.dma_start(keys[k * HD:(k + 1) * HD, u, c * n:(c + 1) * n].bitcast(F32),
                                 src[rows(h), c * n:(c + 1) * n]).then_inc(keys_in[u][c], 16)

            def load_v(h, u):
                sp.dma_start(vh[:, u].rearrange("p k d -> p (k d)"),
                             v_d[bass.ds(h, 1)].rearrange("h p b n -> p (h b n)")).then_inc(v_in[u], 16)

            def store_den(h, u):
                sp.wait_ge(den_evac, h + 1)
                sp.dma_start(den_d[:, bass.ds(h, 1), :].rearrange("j h n -> j (h n)"),
                             den_sb[0:P:HD, u, :]).then_inc(den_stored, 16)

            for u in range(2):
                load_v(u, u)
            with sp.Fori(0, H // 2 - 1) as i:
                for u in range(2):
                    h = 2 * i + u
                    sp.wait_ge(p1_ready, UNITS * (h + 1))
                    load_q(q1, q1_in, h + 2, u)
                    for c in range(LOADS):
                        sp.wait_ge(score_ready, KT * h + (c + 1) * KT // LOADS)
                        load_keys(h + 2, u, c)
                    load_q(q2, q2_in, h + 2, u)
                    sp.wait_ge(pv_done, QUADS * (h + 1))
                    load_v(h + 2, u)
                    store_den(h, u)
            for h in (H - 2, H - 1):
                store_den(h, h % 2)
            sp.wait_ge(den_stored, 16 * H)

        def bank_of(u, n):
            return (n + u) % BANKS

        def free_at(u, n):
            return 1 if u == 0 and n < 2 else 2

        def units_beside(q):
            return [(1 + (4 * q + j + AHEAD) // UNITS, (4 * q + j + AHEAD) % UNITS) for j in range(4)]

        def first_pair(i):
            return isinstance(i, int) and i == 0

        @block.tensor
        def _(pe):
            def unit(i, u, h, base, n):
                c, t = n // C, n % C
                per = UNITS // LOADS
                if n % per == 0 and not first_pair(i):
                    pe.wait_ge(keys_in[u][n // per], 48 * i)
                if n == 0:
                    pe.wait_ge(q1_in[u], 48 * i)
                freed = n - free_at(u, n)
                pe.wait_ge(part_done, base + freed - (freed <= 0))
                if n == 2:
                    pe.wait_ge(turn_copied, h)
                pe.matmul(pass1[bank_of(u, n)][:, :], q1[0:KS, u, t * P:(t + 1) * P],
                          keys[0:KS, u, c * 512:(c + 1) * 512], start=True, stop=True).then_inc(p1_ready, 1)

            def turn(u, h):
                pe.wait_ge(part_done, PARTS * (h + 1))
                for t in range(C):
                    m = pe.matmul(pass1[bank_of(1 - u, 2)][0:1, t * P:(t + 1) * P], mx[:, t:t + 1], ident[:, :], start=True, stop=True)
                m.then_inc(turned, 1)

            def scores(i, u, h, base, k, first):
                if not (first and u == 0 and k < BANKS):
                    pe.wait_ge(exp_done, base + k - free_at(u, k))
                if k == 0:
                    if not first:
                        pe.wait_ge(q2_in[u], 48 * i)
                    pe.wait_ge(turn_copied, h + 1)
                pe.matmul(score[bank_of(u, k)][:, :], keys[0:KM, u, k * P:(k + 1) * P], q2[0:KM, u, :],
                          start=True, stop=True).then_inc(score_ready, 1)

            def values(i, u, h, q, first):
                if q == 0:
                    pe.wait_ge(v_in[u], 16 * (i + 1))
                    if not first:
                        pe.wait_ge(o_evac, h)
                if q == PE_QUADS[0] and not first:
                    pe.wait_ge(den_evac, h)
                if q in PE_QUADS:
                    for j in range(4):
                        pe.matmul(den_ps[j * HD:(j + 1) * HD, :], ones[:, 0:HD], prob[:, (4 * q + j) % SLOTS, :],
                                  start=q == PE_QUADS[0], stop=j == 3 and q == PE_QUADS[-1])
                for j in range(4):
                    m = pe.matmul(out_ps[j * HD:(j + 1) * HD, :], vh[:, u, 4 * q + j, :], prob[:, (4 * q + j) % SLOTS, :],
                                  start=q == 0, stop=q == QUADS - 1)
                m.then_inc(pv_done, 1)
                if q == QUADS - 1:
                    pe.wait_ge(pool_added, pool_adds(QUADS) * (h + 1))
                    pe.wait_ge(vec_added, vec_adds(QUADS) * (h + 1))
                    for j, part in enumerate((pool_sum[:, u, 0:S], pool_sum[:, u, S:2 * S], vec_sum[:, u, :])):
                        m = pe.matmul(den_ps[j * HD:(j + 1) * HD, :], ones[:, 0:HD], part, start=False, stop=True)
                    m.then_inc(den_done, 1)

            def pair(i, first, last):
                for u in range(2):
                    h = 2 * i + u
                    exps, parts_done = KT * h, [PARTS * (h + d) for d in (1, 2)]
                    for q in range(QUADS):
                        for j, (d, n) in enumerate(units_beside(q)):
                            scores(i, u, h, exps, 4 * q + j, first)
                            if not last or u + d < 2:
                                unit(i + (u + d) // 2, (u + d) % 2, h + d, parts_done[d - 1], n)
                            if n == 1 and not (last and u == 1):
                                turn((u + d - 1) % 2, h + d - 1)
                            if j != 1:
                                continue
                            if q >= PV_LAG:
                                values(i, u, h, q - PV_LAG, first and u == 0)
                            elif u == 1:
                                values(i, 0, h - 1, q + QUADS - PV_LAG, first)
                            elif not first:
                                values(i - 1, 1, h - 1, q + QUADS - PV_LAG, False)

            pair(0, True, False)
            with pe.Fori(1, H // 2 - 1) as i:
                pair(i, False, False)
            pair(H // 2 - 1, False, True)
            pe.wait_ge(exp_done, KT * H)
            for q in range(QUADS - PV_LAG, QUADS):
                values(H // 2 - 1, 1, H - 1, q, False)

        @block.vector
        def _(dve):
            def unit(u, h, base, n):
                dve.wait_ge(p1_ready, base + n + 1)
                if n == 0:
                    dve.wait_ge(part_done, PARTS * h)
                dve.tensor_reduce(parts[:, n % C, n // C:n // C + 1], pass1[bank_of(u, n)][:, :], AX.X, ALU.max).then_inc(part_done, 1)
                if n == UNITS - 1:
                    dve.wait_ge(part_done, PARTS * h + UNITS)
                    dve.wait_ge(turned, h)
                    dve.tensor_reduce(mx[:, :], parts[:, :, :], AX.X, ALU.max).then_inc(part_done, 1)

            def add(u, h, q, j, first):
                total, done = vec_adds(QUADS), vec_adds(q) - 2 + j - 2
                tiles = [prob[:, (4 * q + k) % SLOTS, :] for k in range(4)]
                if q == VEC_QUADS[0]:
                    if j == 2:
                        dve.wait_ge(exp_done, KT * h + 4 * q + 4)
                        if not first:
                            dve.wait_ge(den_done, h - 1)
                        dve.tensor_tensor(vec_sum[:, u, :], tiles[2], tiles[3], ALU.add).then_inc(vec_added, 1)
                    return
                dve.wait_ge(exp_done, KT * h + 4 * q + j + 1)
                dve.wait_ge(vec_added, total * h + done)
                dve.tensor_tensor(vec_sum[:, u, :], tiles[j], vec_sum[:, u, :], ALU.add).then_inc(vec_added, 1)

            def pair(i, first, last):
                for u in range(2):
                    h = 2 * i + u
                    ready = [UNITS * (h + d) for d in (1, 2)]
                    for q in range(QUADS):
                        for j, (d, n) in enumerate(units_beside(q)):
                            if not last or u + d < 2:
                                unit((u + d) % 2, h + d, ready[d - 1], n)
                            if j % 2 and q - 1 in VEC_QUADS:
                                add(u, h, q - 1, 2 + j // 2, first)

            pair(0, True, False)
            with dve.Fori(1, H // 2 - 1) as i:
                pair(i, False, False)
            pair(H // 2 - 1, False, True)

        @block.gpsimd
        def _(pool):
            def add(u, h, q, first):
                total, done = pool_adds(QUADS), pool_adds(q) - 1 - (OWNER[q] == "B")
                two = prob[:, (4 * q) % SLOTS:(4 * q) % SLOTS + 4, :].rearrange("p (a b) n -> p a (b n)", a=2)
                if q == POOL_QUADS[0]:
                    pool.wait_ge(exp_done, KT * h + 4 * q + 4)
                    if not first:
                        pool.wait_ge(den_done, h - 1)
                    pool.tensor_tensor(pool_sum[:, u, :], two[:, 0], two[:, 1], ALU.add).then_inc(pool_added, 1)
                else:
                    for a in range(1 + (OWNER[q] == "B")):
                        pool.wait_ge(exp_done, KT * h + 4 * q + 2 * a + 2)
                        pool.wait_ge(pool_added, total * h + done + a)
                        pool.tensor_tensor(pool_sum[:, u, :], two[:, a], pool_sum[:, u, :], ALU.add).then_inc(pool_added, 1)

            for u in range(2):
                for q in POOL_QUADS:
                    add(u, u, q, True)
            with pool.Fori(1, H // 2) as i:
                for u in range(2):
                    for q in POOL_QUADS:
                        add(u, 2 * i + u, q, False)

        @block.scalar
        def _(act):
            def exponentials(u, h, q, js, first):
                for j in js:
                    k = 4 * q + j
                    if j == 0:
                        back, at = (0, q - 4) if q >= 4 else (1, q - 4 + QUADS)
                        if not (first and u == 0 and back):
                            act.wait_ge(pv_done, QUADS * (h - back) + at + 1)
                            if at in POOL_QUADS:
                                act.wait_ge(pool_added, pool_adds(QUADS) * (h - back) + pool_adds(at))
                            if at in VEC_QUADS:
                                act.wait_ge(vec_added, vec_adds(QUADS) * (h - back) + vec_adds(at))
                    act.wait_ge(score_ready, KT * h + k + 1)
                    act.activation(prob[:, k % SLOTS, :], score[bank_of(u, k)][:, :], ACT.Exp, scale=1.0 / math.sqrt(HD)).then_inc(exp_done, 1)

            def copy_turn(u, h):
                act.wait_ge(turned, h + 1)
                act.activation(q2[KS:KM, u, :], pass1[bank_of(1 - u, 2)][0:1, 0:S], ACT.Copy, scale=-1.0).then_inc(turn_copied, 1)

            def evacuate(u, h, first):
                act.wait_ge(pv_done, QUADS * (h + 1))
                act.activation(o_part[:, bass.ds(h, 1), :].rearrange("p h n -> p (h n)"), out_ps[:, :], ACT.Copy).then_inc(o_evac, 1)
                act.wait_ge(den_done, h + 1)
                if not (first and h == 0):
                    act.wait_ge(den_stored, 16 * h)
                act.activation(den_sb[:, u, :], den_ps[:, :], ACT.Copy).then_inc(den_evac, 1)

            def pair(i, first, last):
                for u in range(2):
                    h = 2 * i + u
                    for q in range(QUADS):
                        exponentials(u, h, q, (0, 1), first)
                        d, n = units_beside(q)[1]
                        if n == 1 and not (last and u == 1):
                            copy_turn((u + d - 1) % 2, h + d - 1)
                        exponentials(u, h, q, (2, 3), first)
                        if q == PV_LAG - 1 and not (first and u == 0):
                            evacuate((u + 1) % 2, h - 1, first)

            pair(0, True, False)
            with act.Fori(1, H // 2 - 1) as i:
                pair(i, False, False)
            pair(H // 2 - 1, False, True)
            evacuate(1, H - 1, False)


def finish(nc, ins, out, ident, ones, o_part, den_d):
    E = ins["experts"].shape[0]
    LINEAR_Q, LINEAR_K, LINEAR_V, LINEAR_O, EXPERTS = 1, 2, 3, 4, 5
    WEIGHTS = EXPERTS + E
    RING = 3
    with ExitStack() as ctx:
        def sb(name, shape, dt=F32):
            return ctx.enter_context(nc.sbuf_tensor(name, shape, dt))

        def sem(name):
            return ctx.enter_context(nc.semaphore(name))

        raw = sb("w_raw", [P, RING, C, D])
        whi = sb("w_high", [P, 2, C, D], F32R)
        wlo = sb("w_low", [P, 2, C, D], F32R)
        x4 = sb("res", [P, C, D])
        xn = sb("xn3", [P, C, D])
        xhi = sb("xnT_high", [P, C, S], F32R)
        xlo = sb("xnT_low", [P, C, S], F32R)
        att = sb("att", [P, C, S])
        ahi = sb("att_high", [P, C, S], F32R)
        alo = sb("att_low", [P, C, S], F32R)
        qT, kT, v, kk = (o_part[:, j * C:(j + 1) * C, :] for j in range(4))
        masked = sb("masked", [P, 2, 4, S])
        state = sb("state", [P, 2, C, P])
        tmp = sb("tmp", [P, 2, S])
        up = sb("up", [P, 2, S])
        down = sb("down", [P, 2, S])
        rec = sb("rec", [P, 2, S])
        den64 = sb("den64", [4 * H, S])
        rden = sb("rden", [H, S])
        sel16 = sb("sel16", [4 * H, H])
        sel32 = sb("sel32", [P, HD])
        spread = sb("spread", [H, C, P])
        mask = sb("mask", [P, 4, P])
        diag = sb("diag", [P, 4, P])
        cols = sb("bias_cols", [P, 3, C])
        rows = sb("bias_rows", [1, 3, D])
        BR = HD + 1
        brow = sb("bias_split", [BR, 3, D], F32R)
        brow_ones = sb("bias_ones", [BR, P], F32R)
        rw = sb("router", [P, C, E])
        rwhi = sb("router_high", [P, C, E], F32R)
        rwlo = sb("router_low", [P, C, E], F32R)
        rbias = sb("router_bias", [E, 1])
        lgT = sb("logitsT", [E, S])
        iota = sb("iota", [P, E])
        stats = sb("stats3", [P, C, 6])
        mv = sb("mv3", [P, C, 2])
        rstd = sb("rstd3", [P, 3 * C])
        pr = sb("pr", [P, C, E])
        top = sb("top", [P, C, 8])
        topi = sb("topi", [P, C, 8], U32)
        topf = sb("topf", [P, C, 8])
        small = sb("small", [P, 8, C])
        coef = sb("coef", [P, C, E])
        coef2 = sb("coef2", [P, C, E])
        bank = [ctx.enter_context(nc.psum_tensor(f"fin{j}", [P, 512], F32)) for j in range(8)]

        consts, den_in, x_in, biases_in = sem("consts"), sem("den_in"), sem("x3_in"), sem("biases_in")
        raw_in = [sem(f"raw_in{j}") for j in range(RING)]
        w_hi, w_lo = sem("w_hi"), sem("w_lo")
        rows_hi, rows_lo, router_hi, router_lo = sem("rows_hi"), sem("rows_lo"), sem("router_hi"), sem("router_lo")
        vec, pool_vec, act_done = sem("vec_chain3"), sem("pool_chain3"), sem("act_done")
        den16_ps, rden_ready, spread_ps, spread_sb, o_sum, att_mul, ahi_ready, alo_ready = (sem(n) for n in (
            "den16_ps", "rden_ready", "spread_ps", "spread_sb", "o_sum", "att_mul", "ahi_ready", "alo_ready"))
        alo_first = sem("alo_first")
        wo_ps, added = sem("wo_ps"), sem("added")
        var_ready, std_ready, xn_ready, xT_ps, xhi_ready, xlo_ready = (sem(n) for n in ("var3", "std3", "xn3_ready", "xT_ps", "xhi_ready", "xlo_ready"))
        qk_ps, neg_ready, elu_parts, qk_ready, v_ps, v_ready, kk_ps, kk_ready = (sem(n) for n in (
            "qk_ps", "neg_ready", "elu_parts", "qk_ready", "v_ps", "v3_ready", "kk_ps", "kk_ready"))
        a_ps, a_ready, lin_ps, lin_out, rec_ready, state_ps, state_ready = (sem(n) for n in (
            "a_ps", "a_ready", "lin_ps", "lin_out", "rec_ready", "state_ps", "state_ready"))
        rt_ps, lgT_ready, logit_ps, negmax, exps, y_ps, y_added, stored = (sem(n) for n in (
            "rt_ps", "lgT_ready", "logit_ps", "negmax", "exps", "y_ps", "y_added", "stored"))

        CONSTS = 1 + 4 + 1 + 4 + 1 + 1 + 3 + 2 + 1 + 2

        block = ctx.enter_context(nc.Block())

        def chunks(a):
            return a.rearrange("(c p) n -> p c n", p=P)

        def tokens(t):
            return slice(t * P, (t + 1) * P)

        @block.sync
        def _(sp):
            weights = [ins[n] for n in ("xWo", "aWq", "aWk", "aWv", "aWo")] + [ins["experts"][e] for e in range(E)]

            def load(w):
                if w >= RING:
                    sp.wait_ge(w_lo, w - RING + 1)
                sp.dma_start(raw[:, w % RING], chunks(weights[w])).then_inc(raw_in[w % RING], 16)

            sp.dma_start(den64[:, :], den_d.rearrange("j h n -> (j h) n")).then_inc(den_in, 16)
            load(0)
            sp.dma_start(cols[:, :, :], ins["bias_cols"]).then_inc(biases_in, 16)
            sp.dma_start(rows[:, :, :], ins["bias_rows"]).then_inc(biases_in, 16)
            sp.dma_start(rbias[:, :], ins["router_b"]).then_inc(biases_in, 16)
            sp.dma_start(rw[:, :, :], chunks(ins["router_wT"])).then_inc(biases_in, 16)
            sp.dma_start(x4[:, :, :], chunks(ins["x"])).then_inc(x_in, 16)
            for w in range(1, WEIGHTS):
                load(w)
            for t in range(C):
                sp.wait_ge(y_added, C * (E - 1) + t + 1)
                sp.dma_start(out[tokens(t), :], x4[:, t, :]).then_inc(stored, 16)
            sp.wait_ge(stored, 16 * C)

        @block.gpsimd
        def _(pool):
            link = Chain(pool, consts)
            link(pool.memset(sel32[:, :], 0.0))
            for j in range(4):
                link(pool.affine_select(out=sel32[:, :], in_=sel32[:, :], compare_op=ALU.not_equal, fill=1.0,
                                        base=-HD * j, pattern=[[-1, HD]], channel_multiplier=1))
            link(pool.memset(sel16[:, :], 0.0))
            for j in range(4):
                link(pool.affine_select(out=sel16[:, :], in_=sel16[:, :], compare_op=ALU.not_equal, fill=1.0,
                                        base=-H * j, pattern=[[-1, H]], channel_multiplier=1))
            link(pool.memset(spread[:, :, :], 0.0))
            sp_v = spread[:, :, :].rearrange("h c (l d) -> h c l d", d=HD)
            link(pool.affine_select(out=sp_v, in_=sp_v, compare_op=ALU.not_equal, fill=1.0,
                                    base=0, pattern=[[-4, C], [-1, 4], [0, HD]], channel_multiplier=1))
            link(pool.memset(brow[:, :, :].bitcast(F32), 0.0))
            link(pool.memset(brow_ones[:, :].bitcast(F32), 1.0))
            link(pool.memset(diag[:, :, :], 1.0))
            d_v = diag[:, :, :].rearrange("p a (j d) -> p a j d", d=HD)
            link(pool.affine_select(out=d_v, in_=d_v, compare_op=ALU.is_ge, fill=0.0,
                                    base=0, pattern=[[0, 4], [-HD, 4], [0, HD]], channel_multiplier=1))
            link(pool.affine_select(out=d_v, in_=d_v, compare_op=ALU.is_ge, fill=0.0,
                                    base=HD - 1, pattern=[[0, 4], [HD, 4], [0, HD]], channel_multiplier=-1))
            link(pool.memset(mask[:, :, :], 1.0))
            link(pool.affine_select(out=mask[:, :, :], in_=mask[:, :, :], compare_op=ALU.is_ge, fill=0.0,
                                    base=0, pattern=[[0, 4], [1, P]], channel_multiplier=-1))
            link(pool.iota(iota[:, :], pattern=[[1, E]], base=0, channel_multiplier=0,
                           allow_small_or_imprecise_dtypes=True))

            def split_low(w):
                pool.wait_ge(w_hi, w + 1)
                pool.tensor_tensor(wlo[:, w % 2], raw[:, w % RING], whi[:, w % 2].bitcast(F32), ALU.subtract).then_inc(w_lo, 1)

            for w in range(EXPERTS + 1):
                split_low(w)
            vlink = Chain(pool, pool_vec)
            for c in range(C):
                pool.wait_ge(lin_out, c + 1)
                pool.wait_ge(rec_ready, c + 1)
                a = att[:, :, tokens(c)]
                vlink(pool.tensor_tensor(a, up[:, c % 2, :].rearrange("p (g n) -> p g n", g=C),
                                         rec[:, c % 2, :].rearrange("p (g n) -> p g n", g=C), ALU.mult))
                pool.wait_ge(ahi_ready, C + c + 1)
                pool.tensor_tensor(alo[:, :, tokens(c)], a, ahi[:, :, tokens(c)].bitcast(F32), ALU.subtract).then_inc(alo_ready, 1)
            for w in range(EXPERTS + 1, WEIGHTS):
                split_low(w)

        @block.tensor
        def _(pe):
            TERMS = ((0, 0), (0, 1), (1, 0))

            def out_projection(t, b, w, row):
                for c in range(C):
                    for n, (i, j) in enumerate(TERMS):
                        pe.matmul(bank[b][:, :], (ahi, alo)[i][:, c, tokens(t)], (whi, wlo)[j][:, w % 2, c, :],
                                  start=c == 0 and n == 0, stop=False)
                pe.matmul(bank[b][:, :], brow_ones[:, :], brow[:, row, :], start=False, stop=True).then_inc(wo_ps, 1)

            def transpose(t, b, n):
                pe.wait_ge(xn_ready, C * n + t + 1)
                for c in range(C):
                    m = pe.transpose(bank[b][:, tokens(c)], xn[:, t, tokens(c)], ident[:, :])
                m.then_inc(xT_ps, 1)

            pe.wait_ge(consts, 5)
            for g in range(C):
                for l in range(4):
                    m = pe.matmul(bank[4 + g][l * HD:(l + 1) * HD, :], sel32[:, :], o_part[:, 4 * g + l, :], start=True, stop=True)
                m.then_inc(o_sum, 1)
            pe.wait_ge(consts, CONSTS)
            pe.wait_ge(den_in, 16)
            pe.matmul(bank[0][0:H, :], sel16[:, :], den64[:, :], start=True, stop=True).then_inc(den16_ps, 1)
            pe.wait_ge(rden_ready, 1)
            for g in range(C):
                pe.matmul(bank[g][:, :], spread[:, g, :], rden[:, :], start=True, stop=True).then_inc(spread_ps, 1)
            pe.wait_ge(rows_lo, 1)
            pe.wait_ge(alo_first, C)
            pe.wait_ge(w_lo, 1)
            out_projection(0, 4, 0, 0)
            out_projection(1, 5, 0, 0)
            transpose(0, 0, 0)
            out_projection(2, 6, 0, 0)
            transpose(1, 1, 0)
            out_projection(3, 7, 0, 0)
            transpose(2, 2, 0)
            transpose(3, 3, 0)

            pe.wait_ge(xlo_ready, C)
            for k in range(2):
                w = LINEAR_Q + k
                pe.wait_ge(w_lo, w + 1)
                for g in range(C):
                    for c in range(C):
                        for n, (i, j) in enumerate(TERMS):
                            m = pe.matmul(bank[4 * k + g][:, :], (whi, wlo)[j][:, w % 2, c, tokens(g)], (xhi, xlo)[i][:, c, :],
                                          start=c == 0 and n == 0, stop=c == C - 1 and n == 2)
                    m.then_inc(qk_ps, 1)
            pe.wait_ge(w_lo, LINEAR_V + 1)
            for t in range(C):
                pe.wait_ge(elu_parts, t + 1)
                for c in range(C):
                    for n, (i, j) in enumerate(TERMS):
                        pe.matmul(bank[t][:, :], (xhi, xlo)[i][:, c, tokens(t)], (whi, wlo)[j][:, LINEAR_V % 2, c, :],
                                  start=c == 0 and n == 0, stop=False)
                pe.matmul(bank[t][:, :], brow_ones[:, :], brow[:, 1, :], start=False, stop=True).then_inc(v_ps, 1)
            pe.wait_ge(qk_ready, 2 * C)
            for t in range(C):
                for g in range(C):
                    m = pe.transpose(bank[4 + t][:, tokens(g)], kT[:, g, tokens(t)], ident[:, :])
                m.then_inc(kk_ps, 1)

            def causal_scores(c):
                for l in range(4):
                    r = slice(l * HD, (l + 1) * HD)
                    if c == 0:
                        pe.wait_ge(v_ready, l + 1)
                    else:
                        pe.wait_ge(a_ready, 4 * (c - 1) + l + 1)
                    for g in range(C):
                        m = pe.matmul(bank[l][:, tokens(g)], kT[r, g, tokens(c)], qT[r, g, tokens(c)], start=True, stop=True)
                    m.then_inc(a_ps, 1)

            def sums(c):
                if c == 0:
                    pe.wait_ge(kk_ready, C)
                else:
                    pe.wait_ge(lin_out, c)
                    pe.wait_ge(state_ready, 2 * c)
                pe.wait_ge(a_ready, 4 * (c + 1))
                for g in range(C):
                    for b, w in ((4, v), (5, None)):
                        for l in range(4):
                            lhs = ones[:, 0:HD] if w is None else w[:, c, (4 * g + l) * HD:(4 * g + l + 1) * HD]
                            m = pe.matmul(bank[b][l * HD:(l + 1) * HD, tokens(g)], lhs, masked[:, c % 2, l, tokens(g)],
                                          start=True, stop=c == 0)
                    if c:
                        for j in range(2):
                            m = pe.matmul(bank[4 + j][:, tokens(g)], state[:, j, g, :], qT[:, g, tokens(c)], start=False, stop=True)
                m.then_inc(lin_ps, 1)
                if c < C - 1:
                    for j in range(2):
                        for g in range(C):
                            m = pe.matmul(bank[6 + j][:, tokens(g)], kk[:, c, tokens(g)], (v[:, c, tokens(g)], ones[:, :])[j],
                                          start=c == 0 and g == 0, stop=True, skip_group_check=True)
                        m.then_inc(state_ps, 1)

            def linear_projection(t, b):
                pe.wait_ge(alo_ready, t + 1)
                pe.wait_ge(w_lo, LINEAR_O + 1)
                out_projection(t, b, LINEAR_O, 2)

            causal_scores(0)
            sums(0)
            causal_scores(1)
            sums(1)
            pe.wait_ge(a_ready, 4 * 2)
            linear_projection(0, 3)
            pe.wait_ge(added, C + 1)
            causal_scores(2)
            sums(2)
            linear_projection(1, 3)
            pe.wait_ge(added, C + 2)
            causal_scores(3)
            sums(3)
            pe.wait_ge(a_ready, 4 * C)
            transpose(0, 0, 1)
            linear_projection(2, 3)
            transpose(1, 1, 1)
            pe.wait_ge(state_ready, 2 * (C - 1))
            linear_projection(3, 6)
            transpose(2, 2, 1)
            transpose(3, 7, 1)
            pe.wait_ge(router_lo, 1)
            pe.wait_ge(xlo_ready, 2 * C)
            for c in range(C):
                for n, (i, j) in enumerate(TERMS):
                    m = pe.matmul(bank[7][0:E, :], (rwhi, rwlo)[j][:, c, :], (xhi, xlo)[i][:, c, :],
                                  start=c == 0 and n == 0, stop=c == C - 1 and n == 2)
            m.then_inc(rt_ps, 1)
            n = 0
            for e in range(E):
                w = EXPERTS + e
                pe.wait_ge(w_lo, w + 1)
                for t in range(C):
                    if n >= 7:
                        pe.wait_ge(y_added, n - 6)
                    elif n == 3:
                        pe.wait_ge(added, 2 * C)
                    for c in range(C):
                        for k, (i, j) in enumerate(TERMS):
                            m = pe.matmul(bank[n % 7][:, :], (xhi, xlo)[i][:, c, tokens(t)], (whi, wlo)[j][:, w % 2, c, :],
                                          start=c == 0 and k == 0, stop=c == C - 1 and k == 2)
                    m.then_inc(y_ps, 1)
                    n += 1
                    if n == 1:
                        pe.wait_ge(lgT_ready, 1)
                        for k in range(C):
                            m = pe.transpose(bank[7][:, k * E:(k + 1) * E], lgT[:, tokens(k)], ident[0:E, 0:E])
                        m.then_inc(logit_ps, 1)

        @block.scalar
        def _(act):
            def split_high(w, free=None, count=0):
                act.wait_ge(raw_in[w % RING], 16 * (w // RING + 1))
                if free is not None:
                    act.wait_ge(free, count)
                act.activation(whi[:, w % 2], raw[:, w % RING], ACT.Copy).then_inc(w_hi, 1)

            def root(t, n):
                act.wait_ge(var_ready, C * n + t + 1)
                act.activation(rstd[:, C + t:C + t + 1], rstd[:, t:t + 1], ACT.Sqrt).then_inc(std_ready, 1)

            def transposed(t, b, n):
                act.wait_ge(xT_ps, C * n + t + 1)
                act.activation(xhi[:, :, tokens(t)], bank[b][:, :].rearrange("p (c n) -> p c n", c=C), ACT.Copy).then_inc(xhi_ready, 1)

            split_high(0)
            act.wait_ge(biases_in, 64)
            act.wait_ge(consts, CONSTS)
            act.activation(brow[0:1, :, :], rows[:, :, :], ACT.Copy).then_inc(rows_hi, 1)
            act.activation(rwhi[:, :, :], rw[:, :, :], ACT.Copy).then_inc(router_hi, 1)
            for g in range(C):
                act.wait_ge(spread_ps, g + 1)
                if g >= 2:
                    act.wait_ge(att_mul, g - 1)
                act.activation(tmp[:, g % 2, :], bank[g][:, :], ACT.Copy).then_inc(spread_sb, 1)
            for g in range(C):
                act.wait_ge(att_mul, g + 1)
                act.activation(ahi[:, g, :], att[:, g, :], ACT.Identity, bias=cols[:, 0, g:g + 1]).then_inc(ahi_ready, 1)
            split_high(1)
            root(0, 0)
            root(1, 0)
            transposed(0, 0, 0)
            root(2, 0)
            transposed(1, 1, 0)
            root(3, 0)
            transposed(2, 2, 0)
            transposed(3, 3, 0)
            for n in range(2 * C):
                k, g = n // C, n % C
                if g == 0:
                    split_high(LINEAR_K + k, (wo_ps, qk_ps)[k], C)
                act.wait_ge(neg_ready, n + 1)
                act.activation(tmp[:, n % 2, :], tmp[:, n % 2, :], ACT.Exp).then_inc(act_done, 1)
                act.activation((qT, kT)[k][:, g, :], bank[n][:, :], ACT.Relu, bias=cols[:, 1 + k, g:g + 1]).then_inc(elu_parts, 1)
            split_high(LINEAR_O, qk_ps, 2 * C)
            for t in range(C):
                act.wait_ge(v_ps, t + 1)
                act.activation(v[:, t, :], bank[t][:, :], ACT.Copy).then_inc(v_ready, 1)
            for t in range(C):
                act.wait_ge(kk_ps, t + 1)
                act.activation(kk[:, t, :], bank[4 + t][:, :], ACT.Copy).then_inc(kk_ready, 1)
            split_high(EXPERTS, v_ps, C)

            def sums_out(c):
                act.wait_ge(lin_ps, c + 1)
                if c >= 2:
                    act.wait_ge(ahi_ready, C + c - 1)
                act.activation(down[:, c % 2, :], bank[5][:, :], ACT.Copy, bias=1e-6).then_inc(act_done, 1)
                act.activation(up[:, c % 2, :], bank[4][:, :], ACT.Copy).then_inc(lin_out, 1)

            def high(c):
                act.wait_ge(pool_vec, c + 1)
                act.activation(ahi[:, :, tokens(c)], att[:, :, tokens(c)], ACT.Copy).then_inc(ahi_ready, 1)

            sums_out(0)
            high(0)
            sums_out(1)
            high(1)
            root(0, 1)
            sums_out(2)
            high(2)
            root(1, 1)
            sums_out(3)
            high(3)
            transposed(0, 0, 1)
            root(2, 1)
            transposed(1, 1, 1)
            root(3, 1)
            transposed(2, 2, 1)
            transposed(3, 7, 1)
            split_high(EXPERTS + 1, wo_ps, 2 * C)
            act.wait_ge(rt_ps, 1)
            act.activation(lgT[:, :], bank[7][0:E, :], ACT.Identity, bias=rbias[:, 0:1]).then_inc(lgT_ready, 1)
            act.wait_ge(negmax, 1)
            for t in range(C):
                act.activation(pr[:, t, :], bank[7][:, t * E:(t + 1) * E], ACT.Exp, bias=small[:, 0, t:t + 1],
                               accum_out=small[:, 1, t:t + 1]).then_inc(exps, 1)
            for e in range(2, E):
                split_high(EXPERTS + e, y_ps, C * (e - 1))

        @block.vector
        def _(dve):
            link = Chain(dve, vec)

            def add(t, b, n):
                dve.wait_ge(wo_ps, C * n + t + 1)
                dve.tensor_tensor(x4[:, t, :], bank[b][:, :], x4[:, t, :], ALU.add).then_inc(added, 1)

            def norm(t, n):
                dve.wait_ge(added, C * n + t + 1)
                link(dve.bn_stats(stats[:, t, :], x4[:, t, :]))
                link(dve.bn_aggr(mv[:, t, :], stats[:, t, :]))
                dve.tensor_scalar(rstd[:, t:t + 1], mv[:, t, 1:2], EPS, None, ALU.add).then_inc(var_ready, 1)
                dve.wait_ge(std_ready, C * n + t + 1)
                link(dve.reciprocal(rstd[:, 2 * C + t:2 * C + t + 1], rstd[:, C + t:C + t + 1]))
                if n:
                    dve.wait_ge(xT_ps, C)
                dve.tensor_scalar(xn[:, t, :], x4[:, t, :], mv[:, t, 0:1], rstd[:, 2 * C + t:2 * C + t + 1],
                                  ALU.subtract, ALU.mult).then_inc(xn_ready, 1)

            def transposed_low(t, b, n):
                dve.wait_ge(xhi_ready, C * n + t + 1)
                dve.tensor_tensor(xlo[:, :, tokens(t)], bank[b][:, :].rearrange("p (c n) -> p c n", c=C),
                                  xhi[:, :, tokens(t)].bitcast(F32), ALU.subtract).then_inc(xlo_ready, 1)

            dve.wait_ge(den16_ps, 1)
            dve.reciprocal(rden[:, :], bank[0][0:H, :]).then_inc(rden_ready, 1)
            dve.wait_ge(rows_hi, 1)
            dve.tensor_tensor(brow[HD:BR, :, :], rows[:, :, :], brow[0:1, :, :].bitcast(F32), ALU.subtract).then_inc(rows_lo, 1)
            dve.wait_ge(router_hi, 1)
            dve.tensor_tensor(rwlo[:, :, :], rw[:, :, :], rwhi[:, :, :].bitcast(F32), ALU.subtract).then_inc(router_lo, 1)
            for g in range(C):
                dve.wait_ge(spread_sb, g + 1)
                dve.wait_ge(o_sum, g + 1)
                dve.tensor_tensor(att[:, g, :], bank[4 + g][:, :], tmp[:, g % 2, :], ALU.mult).then_inc(att_mul, 1)
            for g in range(C):
                dve.wait_ge(ahi_ready, g + 1)
                dve.scalar_tensor_tensor(alo[:, g, :], att[:, g, :], cols[:, 0, g:g + 1], ahi[:, g, :].bitcast(F32),
                                         ALU.add, ALU.subtract).then_inc(alo_first, 1)
            dve.wait_ge(x_in, 16)
            add(0, 4, 0)
            norm(0, 0)
            add(1, 5, 0)
            norm(1, 0)
            transposed_low(0, 0, 0)
            add(2, 6, 0)
            norm(2, 0)
            transposed_low(1, 1, 0)
            add(3, 7, 0)
            norm(3, 0)
            transposed_low(2, 2, 0)
            transposed_low(3, 3, 0)
            for n in range(2 * C):
                k, g = n // C, n % C
                dve.wait_ge(qk_ps, n + 1)
                if n >= 2:
                    dve.wait_ge(qk_ready, n - 1)
                dve.tensor_scalar(tmp[:, n % 2, :], bank[n][:, :], cols[:, 1 + k, g:g + 1], 0.0, ALU.add, ALU.min).then_inc(neg_ready, 1)
                dve.wait_ge(act_done, n + 1)
                dve.wait_ge(elu_parts, n + 1)
                dst = (qT, kT)[k][:, g, :]
                dve.tensor_tensor(dst, dst, tmp[:, n % 2, :], ALU.add).then_inc(qk_ready, 1)

            def apply_mask(c, l):
                dve.wait_ge(a_ps, 4 * c + l + 1)
                if c >= 2:
                    dve.wait_ge(lin_ps, c - 1)
                dve.tensor_tensor(masked[:, c % 2, l, :], bank[l][:, :], mask[:, :, :].rearrange("p a n -> p (a n)"),
                                  ALU.mult).then_inc(a_ready, 1)

            def invert(c, g):
                dve.wait_ge(act_done, 2 * C + c + 1)
                if c >= 2:
                    dve.wait_ge(pool_vec, c - 1)
                m = dve.reciprocal(rec[:, c % 2, tokens(g)], down[:, c % 2, tokens(g)])
                if g == C - 1:
                    m.then_inc(rec_ready, 1)

            def keep_state(c):
                for j in range(2):
                    dve.wait_ge(state_ps, 2 * c + j + 1)
                    dve.tensor_tensor(state[:, j], bank[6 + j][:, :].rearrange("p (g n) -> p g n", g=C), diag[:, :, :],
                                      ALU.mult).then_inc(state_ready, 1)

            for l in range(4):
                apply_mask(0, l)
            keep_state(0)
            for l in range(4):
                apply_mask(1, l)
                invert(0, l)
            keep_state(1)
            add(0, 3, 1)
            for l in range(4):
                apply_mask(2, l)
                invert(1, l)
            keep_state(2)
            norm(0, 1)
            add(1, 3, 1)
            for l in range(4):
                apply_mask(3, l)
                invert(2, l)
            norm(1, 1)
            for l in range(4):
                invert(3, l)
            transposed_low(0, 0, 1)
            add(2, 3, 1)
            norm(2, 1)
            transposed_low(1, 1, 1)
            add(3, 6, 1)
            norm(3, 1)
            transposed_low(2, 2, 1)
            transposed_low(3, 7, 1)
            dve.wait_ge(logit_ps, 1)
            logits = bank[7][:, 0:C * E].rearrange("p (t e) -> p t e", e=E)
            dve.tensor_reduce(small[:, 0, :], logits, AX.X, ALU.max, negate=True).then_inc(negmax, 1)
            dve.wait_ge(exps, C)
            link(dve.reciprocal(small[:, 2, :], small[:, 1, :]))
            for t in range(C):
                link(dve.tensor_scalar(pr[:, t, :], pr[:, t, :], small[:, 2, t:t + 1], None, ALU.mult))
            for t in range(C):
                link(dve.max(top[:, t, :], pr[:, t, :]))
            for t in range(C):
                link(dve.max_index(topi[:, t, :], top[:, t, :], pr[:, t, :]))
            link(dve.tensor_copy(topf[:, :, :], topi[:, :, :]))
            p1, p2 = top[:, :, 0], top[:, :, 1]
            link(dve.tensor_tensor(small[:, 3, :], p1, p2, ALU.add))
            link(dve.tensor_scalar(small[:, 3, :], small[:, 3, :], 1e-10, None, ALU.add))
            link(dve.reciprocal(small[:, 3, :], small[:, 3, :]))
            link(dve.tensor_tensor(small[:, 4, :], p1, small[:, 3, :], ALU.mult))
            link(dve.tensor_tensor(small[:, 5, :], p2, small[:, 3, :], ALU.mult))
            link(dve.tensor_tensor(small[:, 6, :], small[:, 4, :], small[:, 5, :], ALU.add))
            link(dve.tensor_scalar(small[:, 7, :], small[:, 6, :], 1e-10, None, ALU.max))
            link(dve.reciprocal(small[:, 7, :], small[:, 7, :]))
            link(dve.tensor_scalar(small[:, 6, :], small[:, 6, :], 1e-10, 1.0, ALU.mult, ALU.add))
            link(dve.tensor_tensor(small[:, 7, :], small[:, 7, :], small[:, 6, :], ALU.mult))
            link(dve.tensor_tensor(small[:, 4, :], small[:, 4, :], small[:, 7, :], ALU.mult))
            link(dve.tensor_tensor(small[:, 5, :], small[:, 5, :], small[:, 7, :], ALU.mult))
            for t in range(C):
                link(dve.tensor_scalar(coef[:, t, :], iota[:, :], topf[:, t, 0:1], small[:, 4, t:t + 1], ALU.is_equal, ALU.mult))
                link(dve.tensor_scalar(coef2[:, t, :], iota[:, :], topf[:, t, 1:2], small[:, 5, t:t + 1], ALU.is_equal, ALU.mult))
            link(dve.tensor_tensor(coef[:, :, :], coef[:, :, :], coef2[:, :, :], ALU.add))
            n = 0
            for e in range(E):
                for t in range(C):
                    dve.wait_ge(y_ps, n + 1)
                    if e:
                        dve.wait_ge(y_added, n - C + 1)
                    dve.scalar_tensor_tensor(x4[:, t, :], bank[n % 7][:, :], coef[:, t, e:e + 1], x4[:, t, :],
                                             ALU.mult, ALU.add).then_inc(y_added, 1)
                    n += 1


def perceiver(nc, ins, out):
    khi_d = nc.dram_tensor("keys_high", (D, KEYS), F32, kind="Internal").ap()
    klo_d = nc.dram_tensor("keys_low", (D, KEYS), F32, kind="Internal").ap()
    qhi_d = nc.dram_tensor("queries_high", (D, S), F32, kind="Internal").ap()
    qlo_d = nc.dram_tensor("queries_low", (D, S), F32, kind="Internal").ap()
    v_d = nc.dram_tensor("values", (H, P, BLOCKS, C * HD), F32, kind="Internal").ap()
    den_d = nc.dram_tensor("denominators", (4, H, S), F32, kind="Internal").ap()
    scratch = (khi_d, klo_d, qhi_d, qlo_d, v_d)
    with ExitStack() as ctx:
        ident = ctx.enter_context(nc.sbuf_tensor("ident", [P, P], F32))
        ones = ctx.enter_context(nc.sbuf_tensor("ones", [P, P], F32))
        o_part = ctx.enter_context(nc.sbuf_tensor("o_part", [P, H, S], F32))
        with ExitStack() as shared:
            keys = shared.enter_context(nc.sbuf_tensor("keys", [P, 2, KEYS], F32R))
            q1 = shared.enter_context(nc.sbuf_tensor("q1", [P, 2, S], F32R))
            q2 = shared.enter_context(nc.sbuf_tensor("q2", [P, 2, S], F32R))
            parts = shared.enter_context(nc.sbuf_tensor("parts", [P, C, UNITS // C], F32))
            mx = shared.enter_context(nc.sbuf_tensor("mx", [P, C], F32))
            maxima = (parts, mx) + tuple(shared.enter_context(nc.semaphore(n)) for n in ("p1_ready", "part_done", "turned", "turn_copied"))
            project_context(nc, ins, scratch, ident, ones, (keys, q1, q2), maxima, o_part)
            attend(nc, scratch, ident, ones, (keys, q1, q2), maxima, o_part, den_d)
        finish(nc, ins, out, ident, ones, o_part, den_d)


def kernel(**inputs):
    import concourse.bacc as bacc
    from concourse.bass_utils import run_bass_kernel_spmd

    a = {k: np.asarray(v) for k, v in inputs.items()}

    def column(b):
        return b.reshape(C, P).T

    arrays = {
        "x": a["x"][0], "ctxT": a["ctx_1024"][0].T,
        "xWq": a["L0_xattn_Wq"], "xWk": a["L0_xattn_Wk"], "xWv": a["L0_xattn_Wv"], "xWo": a["L0_xattn_Wo"],
        "xbq_col": column(a["L0_xattn_bq"]), "xbk_col": column(a["L0_xattn_bk"]),
        "aWq": a["L0_attn_Wq"], "aWk": a["L0_attn_Wk"], "aWv": a["L0_attn_Wv"], "aWo": a["L0_attn_Wo"],
        "bias_cols": np.stack([column(a[n]) for n in ("L0_xattn_bv", "L0_attn_bq", "L0_attn_bk")], axis=1),
        "bias_rows": np.stack([a[n] for n in ("L0_xattn_bo", "L0_attn_bv", "L0_attn_bo")])[None],
        "router_wT": a["L0_ffn_router_w"].T, "router_b": a["L0_ffn_router_b"][:, None],
        "experts": a["L0_ffn_expert_weights"],
    }
    nc = bacc.Bacc("TRN2", target_bir_lowering=False, num_devices=1)
    arrays = {f"in_{k}": np.ascontiguousarray(v) for k, v in arrays.items()}
    ins = {k[3:]: nc.dram_tensor(k, v.shape, mybir.dt.from_np(v.dtype), kind="ExternalInput").ap() for k, v in arrays.items()}
    out = nc.dram_tensor("out", (S, D), F32, kind="ExternalOutput").ap()
    perceiver(nc, ins, out)
    r = run_bass_kernel_spmd(nc, [arrays], core_ids=[0])
    return r.results[0]["out"].reshape(1, S, D)
```

```python
import math
from contextlib import ExitStack

import numpy as np

import concourse.bass as bass
from concourse import mybir

F32 = mybir.dt.float32
F32R = mybir.dt.float32r
U32 = mybir.dt.uint32
ACT = mybir.ActivationFunctionType
ALU = mybir.AluOpType
AX = mybir.AxisListType

P = 128
S = 512
D = 512
C = D // P
KEYS = 8192
H = 16
HD = D // H
KB = 512
BLOCKS = KEYS // KB
KT = KEYS // P
EPS = 1e-5

QUADS = KT // 4
SLOTS = 32
AHEAD = 8
PV_LAG = 2
UNITS = C * (KEYS // 512)
PARTS = UNITS + 1
BANKS = 3
LOADS = 4
OWNER = "BABABABPBABBABAP"
LAST_OWNER = "BDAADAADAADAADAP"


class Chain:

    def __init__(self, eng, sem):
        self.eng, self.sem, self.n = eng, sem, 0

    def __call__(self, instruction):
        self.n += 1
        instruction.then_inc(self.sem, 1)
        self.eng.wait_ge(self.sem, self.n)


def norm_on_vector(dve, link, x4, xn, stats, mv, rstd, var_ready, std_ready, xn_ready, n):
    for t in range(C):
        link(dve.bn_stats(stats[:, t, :], x4[:, t, :]))
    for t in range(C):
        link(dve.bn_aggr(mv[:, t, :], stats[:, t, :]))
    dve.tensor_scalar(rstd[:, 0:C], mv[:, :, 1], EPS, None, ALU.add).then_inc(var_ready, 1)
    dve.wait_ge(std_ready, n)
    link(dve.reciprocal(rstd[:, 2 * C:3 * C], rstd[:, C:2 * C]))
    for t in range(C):
        dve.tensor_scalar(xn[:, t, :], x4[:, t, :], mv[:, t, 0:1],
                          rstd[:, 2 * C + t:2 * C + t + 1], ALU.subtract, ALU.mult).then_inc(xn_ready, 1)


def project_context(nc, ins, scratch, ident, ones, selectors, stacks, maxima, room):
    khi_d, klo_d, qhi_d, qlo_d, v_d = scratch
    keys, q1, q2 = stacks
    parts, mx, p1_ready, part_done, turned, turn_copied = maxima
    sel32, spread = selectors
    with ExitStack() as ctx:
        def sb(name, shape, dt=F32):
            return ctx.enter_context(nc.sbuf_tensor(name, shape, dt))

        def sem(name):
            return ctx.enter_context(nc.semaphore(name))

        whi = sb("whi", [P, 2, C, D], F32R)
        wlo = sb("wlo", [P, 2, C, D], F32R)
        chi = sb("chi", [P, 2, C, KB], F32R)
        clo = sb("clo", [P, 2, C, KB], F32R)
        khi = sb("khi", [P, 2, C, KB], F32R)
        klo = sb("klo", [P, 2, C, KB], F32R)
        craw, vrows, xs, wraw = (room[:, j * C:(j + 1) * C, :] for j in range(4))
        vout = vrows.rearrange("p c (h n) -> p (c h n)", n=C * HD).rearrange("p (h k d) -> p h k d", h=H, k=C)
        bq = sb("bq_sb", [P, C])
        bk = sb("bk_sb", [P, C])
        stats = sb("stats", [P, C, 6])
        mv = sb("mv", [P, C, 2])
        rstd = sb("rstd", [P, 3 * C])
        bank = [ctx.enter_context(nc.psum_tensor(f"proj{j}", [P, 512], F32)) for j in range(8)]

        first_in = [sem(f"first_in{c}") for c in range(C)]
        first_hi, first_lo = sem("first_hi"), sem("first_lo")
        consts = sem("early_consts")
        x_in, wv_in, wq_in, bias_in, ident_done = sem("x_in"), sem("wv_in"), sem("wq_in"), sem("bias_in"), sem("ident_done")
        ctx_in = sem("ctx_in")
        wv_hi, wv_lo, chi_done, clo_done = sem("wv_hi"), sem("wv_lo"), sem("chi_done"), sem("clo_done")
        var_ready, std_ready, xn_ready, xnT_psum, xnT_ready = sem("var_ready"), sem("std_ready"), sem("xn_ready"), sem("xnT_psum"), sem("xnT_ready")
        q_psum, qhi_done, qlo_done, q_stored = sem("q_psum"), sem("qhi_done"), sem("qlo_done"), sem("q_stored")
        proj_done = sem("proj_done")
        khi_done, klo_done = sem("khi_done"), sem("klo_done")
        va_done, vv_done = sem("va_done"), sem("vv_done")
        k_stored, v_stored = [sem("k_stored0"), sem("k_stored1")], sem("v_stored")
        k_stacked, q_stacked = [sem("k_stacked0"), sem("k_stacked1")], sem("q_stacked")
        vec = sem("vec_chain")

        ctxT = ins["ctxT"].rearrange("(c p) n -> p c n", p=P)
        khi_v = khi_d.rearrange("(c p) n -> p c n", p=P)
        klo_v = klo_d.rearrange("(c p) n -> p c n", p=P)
        qhi_v = qhi_d.rearrange("(c p) n -> p c n", p=P)
        qlo_v = qlo_d.rearrange("(c p) n -> p c n", p=P)
        v_v = v_d.rearrange("h p b n -> p h b n")

        qhi, qlo = khi[:, 1], klo[:, 1]
        wk_raw = vrows

        def w_v(name):
            return ins[name].rearrange("(c p) n -> p c n", p=P)

        block = ctx.enter_context(nc.Block())

        @block.sync
        def _(sp):
            for c in range(C):
                sp.dma_start(wk_raw[:, c, :], w_v("xWk")[:, c, :]).then_inc(first_in[c], 16)
                sp.dma_start(craw[:, c, :], ctxT[:, c, 0:KB]).then_inc(first_in[c], 16)
            sp.dma_start(bk[:, :], ins["xbk_col"]).then_inc(bias_in, 16)
            sp.dma_start(bq[:, :], ins["xbq_col"]).then_inc(bias_in, 16)
            sp.dma_start(wraw[:, :, :], w_v("xWv")).then_inc(wv_in, 16)
            sp.dma_start(xs[:, :, :], ins["x"].rearrange("(c p) n -> p c n", p=P)).then_inc(x_in, 16)
            sp.wait_ge(first_lo, 2 * C)
            sp.dma_start(craw[:, :, :], ctxT[:, :, KB:2 * KB]).then_inc(ctx_in, 16)
            sp.wait_ge(wv_lo, 1)
            sp.dma_start(wraw[:, :, :], w_v("xWq")).then_inc(wq_in, 16)

            def store_keys(u, b):
                sp.wait_ge(khi_done, C * (b + 1))
                sp.wait_ge(klo_done, C * (b + 1))
                for h in range(2):
                    for k, part in enumerate((khi, klo, khi)):
                        sp.dma_start(keys[k * HD:(k + 1) * HD, h, bass.ds(b * KB, KB)].bitcast(F32),
                                     part[h * HD:(h + 1) * HD, u, 0, :].bitcast(F32)).then_inc(k_stacked[u], 16)
                sp.dma_start(khi_v[:, :, bass.ds(b * KB, KB)], khi[:, u].bitcast(F32)).then_inc(k_stored[u], 16)
                sp.dma_start(klo_v[:, :, bass.ds(b * KB, KB)], klo[:, u].bitcast(F32)).then_inc(k_stored[u], 16)

            def load_ctx(b):
                sp.wait_ge(chi_done, b - 1)
                sp.wait_ge(clo_done, b - 1)
                sp.dma_start(craw[:, :, :], ctxT[:, :, bass.ds(b * KB, KB)]).then_inc(ctx_in, 16)

            def store_values(b):
                sp.wait_ge(va_done, 2 * (b + 1))
                sp.wait_ge(vv_done, 2 * (b + 1))
                sp.dma_start(v_v[:, :, bass.ds(b, 1), :].rearrange("p h b n -> p h (b n)"),
                             vout[:, :, :, :].rearrange("p h k d -> p h (k d)")).then_inc(v_stored, 16)

            def step(i, u, last):
                b = 2 * i + u
                store_keys(u, b)
                if not last:
                    load_ctx(b + 2)
                store_values(b)

            step(0, 0, False)
            sp.wait_ge(qhi_done, C)
            sp.wait_ge(qlo_done, C)
            for h in range(2):
                for q in (q1, q2):
                    for k, part in enumerate((qhi, qhi, qlo)):
                        sp.dma_start(q[k * HD:(k + 1) * HD, h, :].bitcast(F32),
                                     part[h * HD:(h + 1) * HD, 0, :].bitcast(F32)).then_inc(q_stacked, 16)
            sp.dma_start(qhi_v, qhi.bitcast(F32)).then_inc(q_stored, 16)
            sp.dma_start(qlo_v, qlo.bitcast(F32)).then_inc(q_stored, 16)
            step(0, 1, False)
            with sp.Fori(1, BLOCKS // 2 - 1) as i:
                for u in range(2):
                    step(i, u, False)
            for u in range(2):
                step(BLOCKS // 2 - 1, u, True)
            for u in range(2):
                sp.wait_ge(k_stored[u], 16 * BLOCKS)
                sp.wait_ge(k_stacked[u], 48 * BLOCKS)
            sp.wait_ge(v_stored, 16 * BLOCKS)
            sp.wait_ge(q_stored, 32)

        @block.gpsimd
        def _(pool):
            pool.memset(ident[:, :], 0.0).then_inc(ident_done, 1)
            pool.memset(ones[:, :], 1.0)
            pool.wait_ge(ident_done, 1)
            pool.affine_select(out=ident[:, :], in_=ident[:, :], compare_op=ALU.not_equal, fill=1.0,
                               base=0, pattern=[[-1, P]], channel_multiplier=1).then_inc(ident_done, 1)
            for h in range(2):
                pool.wait_ge(ident_done, 2 + h)
                pool.memset(keys[3 * HD:3 * HD + 1, h, :].bitcast(F32), 1.0).then_inc(ident_done, 1)
            pool.wait_ge(ident_done, 4)
            link = Chain(pool, consts)
            link(pool.memset(sel32[:, :], 0.0))
            for j in range(4):
                link(pool.affine_select(out=sel32[:, :], in_=sel32[:, :], compare_op=ALU.not_equal, fill=1.0,
                                        base=-HD * j, pattern=[[-1, HD]], channel_multiplier=1))
            link(pool.memset(spread[:, :, :], 0.0))
            sp_v = spread[:, :, :].rearrange("h c (l d) -> h c l d", d=HD)
            for j in range(4):
                link(pool.affine_select(out=sp_v, in_=sp_v, compare_op=ALU.not_equal, fill=1.0,
                                        base=-32 * j, pattern=[[-4, C], [-1, 4], [0, HD]], channel_multiplier=1))

        @block.scalar
        def _(act):
            for c in range(C):
                act.wait_ge(first_in[c], 32)
                act.activation(whi[:, 0, c, :], wk_raw[:, c, :], ACT.Copy).then_inc(first_hi, 1)
                act.activation(chi[:, 0, c, :], craw[:, c, :], ACT.Copy).then_inc(first_hi, 1)
            act.wait_ge(wv_in, 16)
            act.activation(whi[:, 1], wraw[:, :, :], ACT.Copy).then_inc(wv_hi, 1)
            act.wait_ge(bias_in, 32)

            def keys_out(i, u, b, done):
                if isinstance(b, int) and b == 1:
                    act.wait_ge(q_stored, 32)
                    act.wait_ge(q_stacked, 16 * 12)
                elif not isinstance(b, int) or b > 1:
                    act.wait_ge(k_stored[u], 32 * i)
                    act.wait_ge(k_stacked[u], 96 * i)
                for g in range(C):
                    act.wait_ge(proj_done, done + g + 1)
                    act.activation(khi[:, u, g, :], bank[g][:, :], ACT.Identity, bias=bk[:, g:g + 1]).then_inc(khi_done, 1)

            def values_out(b, done, first):
                if not first:
                    act.wait_ge(v_stored, 16 * b)
                for t in range(2):
                    act.wait_ge(proj_done, done + t + 1)
                    act.activation(vout[:, :, t, :], bank[4 + t][:, :].rearrange("p (h d) -> p h d", d=HD),
                                   ACT.Copy).then_inc(va_done, 1)

            def split_next(b, u):
                act.wait_ge(ctx_in, 16 * (b + 1))
                act.activation(chi[:, 1 - u], craw[:, :, :], ACT.Copy).then_inc(chi_done, 1)

            def step(i, u, first, last):
                b = 2 * i + u
                keys_out(i, u, b, 8 * b)
                if not last:
                    split_next(b, u)
                values_out(b, 8 * b + 4, first)

            step(0, 0, True, False)
            act.wait_ge(var_ready, 1)
            act.activation(rstd[:, C:2 * C], rstd[:, 0:C], ACT.Sqrt).then_inc(std_ready, 1)
            act.wait_ge(xnT_psum, C)
            for c in range(C):
                act.activation(xs[:, c, :], bank[c][:, :], ACT.Copy).then_inc(xnT_ready, 1)
            for g in range(C):
                act.wait_ge(q_psum, g + 1)
                act.activation(qhi[:, g, :], bank[4 + g][:, :], ACT.Identity, bias=bq[:, g:g + 1]).then_inc(qhi_done, 1)
            split_next(1, 1)
            values_out(1, 8, False)
            keys_out(0, 1, 1, 11)
            with act.Fori(1, BLOCKS // 2 - 1) as i:
                for u in range(2):
                    step(i, u, False, False)
            for u in range(2):
                step(BLOCKS // 2 - 1, u, False, u == 1)
            act.wait_ge(turned, 1)
            act.activation(q2[3 * HD:3 * HD + 1, 0, :], bank[0][0:1, :], ACT.Copy, scale=-1.0).then_inc(turn_copied, 1)

        @block.vector
        def _(dve):
            link = Chain(dve, vec)
            for c in range(C):
                dve.wait_ge(first_hi, 2 * c + 2)
                dve.tensor_tensor(wlo[:, 0, c, :], wk_raw[:, c, :], whi[:, 0, c, :].bitcast(F32), ALU.subtract).then_inc(first_lo, 1)
                dve.tensor_tensor(clo[:, 0, c, :], craw[:, c, :], chi[:, 0, c, :].bitcast(F32), ALU.subtract).then_inc(first_lo, 1)
            dve.wait_ge(wv_hi, 1)
            dve.tensor_tensor(wlo[:, 1], wraw[:, :, :], whi[:, 1].bitcast(F32), ALU.subtract).then_inc(wv_lo, 1)
            dve.wait_ge(bias_in, 32)

            def maximum(b, t):
                n = C * b + t
                dve.wait_ge(p1_ready, n + 1)
                dve.tensor_reduce(parts[:, t, bass.ds(b, 1)], bank[6 + t % 2][:, :], AX.X, ALU.max).then_inc(part_done, 1)

            def keys_out(i, u, b):
                if isinstance(b, int) and b == 1:
                    dve.wait_ge(q_stored, 32)
                    dve.wait_ge(q_stacked, 16 * 12)
                elif not isinstance(b, int) or b > 1:
                    dve.wait_ge(k_stored[u], 32 * i)
                    dve.wait_ge(k_stacked[u], 96 * i)
                for g in range(C):
                    dve.wait_ge(khi_done, C * b + g + 1)
                    dve.scalar_tensor_tensor(klo[:, u, g, :], bank[g][:, :], bk[:, g:g + 1],
                                             khi[:, u, g, :].bitcast(F32), ALU.add, ALU.subtract).then_inc(klo_done, 1)
                    if not isinstance(b, int) or b > 0:
                        maximum(b - 1, g)

            def values_out(b, done, first, tiles=range(2, C)):
                if not first:
                    dve.wait_ge(v_stored, 16 * b)
                for t in tiles:
                    dve.wait_ge(proj_done, done + t + 1)
                    dve.tensor_copy(vout[:, :, t, :], bank[2 + t][:, :].rearrange("p (h d) -> p h d", d=HD)).then_inc(vv_done, 1)

            def split_next(b, u):
                dve.wait_ge(chi_done, b + 1)
                dve.tensor_tensor(clo[:, 1 - u], craw[:, :, :], chi[:, 1 - u].bitcast(F32), ALU.subtract).then_inc(clo_done, 1)

            def step(i, u, last):
                b = 2 * i + u
                keys_out(i, u, b)
                if not last:
                    split_next(b, u)
                values_out(b, 8 * b + 4, False)

            keys_out(0, 0, 0)
            split_next(0, 0)
            dve.wait_ge(x_in, 16)
            norm_on_vector(dve, link, xs, xs, stats, mv, rstd, var_ready, std_ready, xn_ready, 1)
            values_out(0, 4, True)
            for g in range(C):
                dve.wait_ge(qhi_done, g + 1)
                dve.scalar_tensor_tensor(qlo[:, g, :], bank[4 + g][:, :], bq[:, g:g + 1],
                                         qhi[:, g, :].bitcast(F32), ALU.add, ALU.subtract).then_inc(qlo_done, 1)
            split_next(1, 1)
            values_out(1, 8, False, (2,))
            keys_out(0, 1, 1)
            values_out(1, 12, False, (3,))
            with dve.Fori(1, BLOCKS // 2 - 1) as i:
                for u in range(2):
                    step(i, u, False)
            for u in range(2):
                step(BLOCKS // 2 - 1, u, u == 1)
            for t in range(C):
                maximum(BLOCKS - 1, t)
            dve.wait_ge(part_done, UNITS)
            dve.tensor_reduce(mx[:, :], parts[:, :, :], AX.X, ALU.max).then_inc(part_done, 1)
            dve.wait_ge(part_done, PARTS)
            for n in range(AHEAD):
                dve.wait_ge(p1_ready, UNITS + n + 1)
                dve.tensor_reduce(parts[:, n % C, n // C:n // C + 1], bank[6 + n % 2][:, :], AX.X, ALU.max).then_inc(part_done, 1)

        @block.tensor
        def _(pe):
            def unit(i, u, t, first):
                b = 2 * i + u
                n = C * b + t
                if t == 0:
                    pe.wait_ge(k_stacked[u], 96 * (i + 1))
                    if first:
                        pe.wait_ge(q_stacked, 16 * 12)
                if not (first and u == 0 and t < 2):
                    pe.wait_ge(part_done, n - 1)
                pe.matmul(bank[6 + t % 2][:, :], q1[0:3 * HD, 0, t * P:(t + 1) * P],
                          keys[0:3 * HD, 0, bass.ds(b * KB, KB)], start=True, stop=True).then_inc(p1_ready, 1)

            def key_products(u, g, c):
                for w, x, n in ((whi, chi, 0), (wlo, chi, 1), (whi, clo, 2)):
                    m = pe.matmul(bank[g][:, :], w[:, 0, c, g * P:(g + 1) * P], x[:, u, c, :],
                                  start=c == 0 and n == 0, stop=c == C - 1 and n == 2)
                return m

            def values(b, u, first, tiles=range(C)):
                for t in tiles:
                    if t >= 2:
                        pe.wait_ge(va_done, 2 * b + t - 1)
                    elif not first:
                        pe.wait_ge(vv_done, 2 * (b - 1) + t + 1)
                    for c in range(C):
                        for x, w, n in ((chi, whi, 0), (chi, wlo, 1), (clo, whi, 2)):
                            m = pe.matmul(bank[4 + t % 2][:, :], x[:, u, c, t * P:(t + 1) * P], w[:, 1, c, :],
                                          start=c == 0 and n == 0, stop=c == C - 1 and n == 2)
                    m.then_inc(proj_done, 1)

            for c in range(C):
                pe.wait_ge(first_lo, 2 * c + 2)
                for g in range(C):
                    m = key_products(0, g, c)
                    if c == C - 1:
                        m.then_inc(proj_done, 1)
            pe.wait_ge(wv_lo, 1)
            values(0, 0, True)
            pe.wait_ge(ident_done, 2)
            pe.wait_ge(xn_ready, C)
            for c in range(C):
                pe.wait_ge(klo_done, c + 1)
                for t in range(C):
                    m = pe.transpose(bank[c][:, t * P:(t + 1) * P], xs[:, t, c * P:(c + 1) * P], ident[:, :])
                m.then_inc(xnT_psum, 1)
            pe.wait_ge(wq_in, 16)
            pe.wait_ge(vv_done, 2)
            for c in range(C):
                pe.wait_ge(xnT_ready, c + 1)
                for g in range(C):
                    m = pe.matmul(bank[4 + g][:, :], wraw[:, c, g * P:(g + 1) * P], xs[:, c, :], start=c == 0, stop=c == C - 1)
                    if c == C - 1:
                        m.then_inc(q_psum, 1)

            def step(i, u, first):
                b = 2 * i + u
                pe.wait_ge(chi_done, b)
                pe.wait_ge(clo_done, b)
                if first:
                    pe.wait_ge(qlo_done, 2)
                    values(b, u, False, (0, 1, 2))
                    pe.wait_ge(qlo_done, C)
                for g in range(C):
                    if not first:
                        pe.wait_ge(klo_done, C * (b - 1) + g + 1)
                    for c in range(C):
                        m = key_products(u, g, c)
                    m.then_inc(proj_done, 1)
                    unit(i if u else i - 1, 1 - u, g, first)
                values(b, u, False, (3,) if first else range(C))

            step(0, 1, True)
            with pe.Fori(1, BLOCKS // 2) as i:
                for u in range(2):
                    step(i, u, False)
            for t in range(C):
                unit(BLOCKS // 2 - 1, 1, t, False)
            for n in range(AHEAD):
                c, t = n // C, n % C
                pe.wait_ge(part_done, UNITS + n - 1 + (n >= 2))
                pe.matmul(bank[6 + n % 2][:, :], q1[0:3 * HD, 1, t * P:(t + 1) * P],
                          keys[0:3 * HD, 1, c * KB:(c + 1) * KB], start=True, stop=True).then_inc(p1_ready, 1)
                if n == 1:
                    pe.wait_ge(part_done, PARTS)
                    for t in range(C):
                        m = pe.matmul(bank[0][0:1, t * P:(t + 1) * P], mx[:, t:t + 1], ident[:, :], start=True, stop=True)
                    m.then_inc(turned, 1)


def owners(h):
    return LAST_OWNER if isinstance(h, int) and h == H - 1 else OWNER


def pool_quads(own):
    return [q for q in range(QUADS) if own[q] in "AB"]


def vec_tiles(own, q):
    return {"A": (2, 3), "D": (0, 1, 2, 3)}.get(own[q], ())


def pe_quads(own):
    return [q for q in range(QUADS) if own[q] == "P"]


def pool_adds(own, q=QUADS - 1):
    return sum(1 + (own[k] == "B") for k in pool_quads(own) if k <= q) - 1


def vec_adds(own, q=QUADS - 1):
    return sum(len(vec_tiles(own, k)) for k in range(q + 1)) - 1


def attend(nc, scratch, ident, ones, stacks, maxima, o_part, den_d):
    khi_d, klo_d, qhi_d, qlo_d, v_d = scratch
    keys, q1, q2 = stacks
    parts, mx, p1_ready, part_done, turned, turn_copied = maxima
    with ExitStack() as ctx:
        def sb(name, shape, dt=F32):
            return ctx.enter_context(nc.sbuf_tensor(name, shape, dt))

        def ps(name, shape):
            return ctx.enter_context(nc.psum_tensor(name, shape, F32))

        def sem(name):
            return ctx.enter_context(nc.semaphore(name))

        KS, KM = 3 * HD, 3 * HD + 1
        vh = sb("vh", [P, 2, KT, HD])
        prob = sb("prob", [P, SLOTS, S])
        pool_sum = sb("pool_sum", [P, 2, 2 * S])
        vec_sum = sb("vec_sum", [P, 2, S])
        den_sb = sb("den_sb", [P, 2, S])
        score = [ps(f"score{j}", [P, 512]) for j in range(BANKS)]
        pass1 = [ps(f"pass1{j}", [P, 512]) for j in range(BANKS)]
        out_ps = ps("out_ps", [P, 512])
        den_ps = ps("den_ps", [P, 512])

        keys_in = [[sem(f"keys_in{u}{c}") for c in range(LOADS)] for u in range(2)]
        q1_in, q2_in, v_in = ([sem(f"{n}_in{u}") for u in range(2)] for n in ("q1", "q2", "v"))
        score_ready, exp_done, pv_done = sem("score_ready"), sem("exp_done"), sem("pv_done")
        pool_added, vec_added = sem("pool_added"), sem("vec_added")
        den_done, o_evac, den_evac, den_stored = sem("den_done"), sem("o_evac"), sem("den_evac"), sem("den_stored")

        block = ctx.enter_context(nc.Block())

        @block.sync
        def _(sp):
            def rows(h):
                return bass.ds(h * HD, HD)

            def load_q(q, q_in, h, u):
                for k, src in enumerate((qhi_d, qhi_d, qlo_d)):
                    sp.dma_start(q[k * HD:(k + 1) * HD, u, :].bitcast(F32), src[rows(h), :]).then_inc(q_in[u], 16)

            def load_keys(h, u, c):
                n = KEYS // LOADS
                for k, src in enumerate((khi_d, klo_d, khi_d)):
                    sp.dma_start(keys[k * HD:(k + 1) * HD, u, c * n:(c + 1) * n].bitcast(F32),
                                 src[rows(h), c * n:(c + 1) * n]).then_inc(keys_in[u][c], 16)

            def load_v(h, u):
                sp.dma_start(vh[:, u].rearrange("p k d -> p (k d)"),
                             v_d[bass.ds(h, 1)].rearrange("h p b n -> p (h b n)")).then_inc(v_in[u], 16)

            def store_den(h, u):
                sp.wait_ge(den_evac, h + 1)
                sp.dma_start(den_d[:, bass.ds(h, 1), :].rearrange("j h n -> j (h n)"),
                             den_sb[0:P:HD, u, :]).then_inc(den_stored, 16)

            for u in range(2):
                load_v(u, u)
            with sp.Fori(0, H // 2 - 1) as i:
                for u in range(2):
                    h = 2 * i + u
                    sp.wait_ge(p1_ready, UNITS * (h + 1))
                    load_q(q1, q1_in, h + 2, u)
                    for c in range(LOADS):
                        sp.wait_ge(score_ready, KT * h + (c + 1) * KT // LOADS)
                        load_keys(h + 2, u, c)
                    load_q(q2, q2_in, h + 2, u)
                    sp.wait_ge(pv_done, QUADS * (h + 1))
                    load_v(h + 2, u)
                    store_den(h, u)
            for h in (H - 2, H - 1):
                store_den(h, h % 2)
            sp.wait_ge(den_stored, 16 * H)

        def bank_of(u, n):
            return (n + u) % BANKS

        def free_at(u, n):
            return 1 if u == 0 and n < 2 else 2

        def is_last(h):
            return isinstance(h, int) and h == H - 1

        def score_bank(u, h, k):
            n = (k + u) % (2 * BANKS)
            return pass1[n - BANKS] if is_last(h) and n >= BANKS else score[bank_of(u, k)]

        def units_beside(q):
            return [(1 + (4 * q + j + AHEAD) // UNITS, (4 * q + j + AHEAD) % UNITS) for j in range(4)]

        def first_pair(i):
            return isinstance(i, int) and i == 0

        @block.tensor
        def _(pe):
            def unit(i, u, h, base, n):
                c, t = n // C, n % C
                per = UNITS // LOADS
                if n % per == 0 and not first_pair(i):
                    pe.wait_ge(keys_in[u][n // per], 48 * i)
                if n == 0:
                    pe.wait_ge(q1_in[u], 48 * i)
                freed = n - free_at(u, n)
                pe.wait_ge(part_done, base + freed - (freed <= 0))
                if n == 2:
                    pe.wait_ge(turn_copied, h)
                pe.matmul(pass1[bank_of(u, n)][:, :], q1[0:KS, u, t * P:(t + 1) * P],
                          keys[0:KS, u, c * 512:(c + 1) * 512], start=True, stop=True).then_inc(p1_ready, 1)

            def turn(u, h):
                pe.wait_ge(part_done, PARTS * (h + 1))
                for t in range(C):
                    m = pe.matmul(pass1[bank_of(1 - u, 2)][0:1, t * P:(t + 1) * P], mx[:, t:t + 1], ident[:, :], start=True, stop=True)
                m.then_inc(turned, 1)

            def scores(i, u, h, base, k, first):
                if is_last(h):
                    ago = 2 if k < 2 else 5
                    if not 2 <= k < 5:
                        pe.wait_ge(exp_done, base + k - ago)
                elif not (first and u == 0 and k < BANKS):
                    pe.wait_ge(exp_done, base + k - free_at(u, k))
                if k == 0:
                    if not first:
                        pe.wait_ge(q2_in[u], 48 * i)
                    pe.wait_ge(turn_copied, h + 1)
                pe.matmul(score_bank(u, h, k)[:, :], keys[0:KM, u, k * P:(k + 1) * P], q2[0:KM, u, :],
                          start=True, stop=True).then_inc(score_ready, 1)

            def values(i, u, h, q, first):
                if q == 0:
                    pe.wait_ge(v_in[u], 16 * (i + 1))
                    if not first:
                        pe.wait_ge(o_evac, h)
                own = owners(h)
                if q == pe_quads(own)[0] and not first:
                    pe.wait_ge(den_evac, h)
                if q in pe_quads(own):
                    for j in range(4):
                        pe.matmul(den_ps[j * HD:(j + 1) * HD, :], ones[:, 0:HD], prob[:, (4 * q + j) % SLOTS, :],
                                  start=q == pe_quads(own)[0], stop=j == 3 and q == pe_quads(own)[-1])
                for j in range(4):
                    m = pe.matmul(out_ps[j * HD:(j + 1) * HD, :], vh[:, u, 4 * q + j, :], prob[:, (4 * q + j) % SLOTS, :],
                                  start=q == 0, stop=q == QUADS - 1)
                m.then_inc(pv_done, 1)
                if q == QUADS - 1:
                    pe.wait_ge(pool_added, pool_adds(OWNER) * h + pool_adds(own))
                    pe.wait_ge(vec_added, vec_adds(OWNER) * h + vec_adds(own))
                    for j, part in enumerate((pool_sum[:, u, 0:S], pool_sum[:, u, S:2 * S], vec_sum[:, u, :])):
                        m = pe.matmul(den_ps[j * HD:(j + 1) * HD, :], ones[:, 0:HD], part, start=False, stop=True)
                    m.then_inc(den_done, 1)

            def pair(i, first, last):
                for u in range(2):
                    h = 2 * i + u
                    exps, parts_done = KT * h, [PARTS * (h + d) for d in (1, 2)]
                    for q in range(QUADS):
                        for j, (d, n) in enumerate(units_beside(q)):
                            scores(i, u, h, exps, 4 * q + j, first)
                            if not last or u + d < 2:
                                unit(i + (u + d) // 2, (u + d) % 2, h + d, parts_done[d - 1], n)
                            if n == 1 and not (last and u == 1):
                                turn((u + d - 1) % 2, h + d - 1)
                            if j != 1:
                                continue
                            if q >= PV_LAG:
                                values(i, u, h, q - PV_LAG, first and u == 0)
                            elif u == 1:
                                values(i, 0, h - 1, q + QUADS - PV_LAG, first)
                            elif not first:
                                values(i - 1, 1, h - 1, q + QUADS - PV_LAG, False)

            pair(0, True, False)
            with pe.Fori(1, H // 2 - 1) as i:
                pair(i, False, False)
            pair(H // 2 - 1, False, True)
            pe.wait_ge(exp_done, KT * H)
            for q in range(QUADS - PV_LAG, QUADS):
                values(H // 2 - 1, 1, H - 1, q, False)

        @block.vector
        def _(dve):
            def unit(u, h, base, n):
                dve.wait_ge(p1_ready, base + n + 1)
                if n == 0:
                    dve.wait_ge(part_done, PARTS * h)
                dve.tensor_reduce(parts[:, n % C, n // C:n // C + 1], pass1[bank_of(u, n)][:, :], AX.X, ALU.max).then_inc(part_done, 1)
                if n == UNITS - 1:
                    dve.wait_ge(part_done, PARTS * h + UNITS)
                    dve.wait_ge(turned, h)
                    dve.tensor_reduce(mx[:, :], parts[:, :, :], AX.X, ALU.max).then_inc(part_done, 1)

            def add(u, h, q, j, first):
                own = owners(h)
                mine = vec_tiles(own, q)
                if j not in mine:
                    return
                before = vec_adds(own, q) - len(mine) + mine.index(j)
                if before < 0:
                    return
                tile = prob[:, (4 * q + j) % SLOTS, :]
                dve.wait_ge(exp_done, KT * h + 4 * q + j + 1)
                if before == 0:
                    if not first:
                        dve.wait_ge(den_done, h - 1)
                    dve.tensor_tensor(vec_sum[:, u, :], prob[:, (4 * q + j - 1) % SLOTS, :], tile, ALU.add).then_inc(vec_added, 1)
                    return
                dve.wait_ge(vec_added, vec_adds(OWNER) * h + before)
                dve.tensor_tensor(vec_sum[:, u, :], tile, vec_sum[:, u, :], ALU.add).then_inc(vec_added, 1)

            def pair(i, first, last):
                for u in range(2):
                    h = 2 * i + u
                    ready = [UNITS * (h + d) for d in (1, 2)]
                    for q in range(QUADS):
                        for j, (d, n) in enumerate(units_beside(q)):
                            if not last or u + d < 2:
                                unit((u + d) % 2, h + d, ready[d - 1], n)
                            if q == 0:
                                continue
                            if owners(h)[q - 1] == "D":
                                add(u, h, q - 1, j, first)
                            elif j % 2:
                                add(u, h, q - 1, 2 + j // 2, first)

            pair(0, True, False)
            with dve.Fori(1, H // 2 - 1) as i:
                pair(i, False, False)
            pair(H // 2 - 1, False, True)

        @block.gpsimd
        def _(pool):
            def add(u, h, q, first):
                own = owners(h)
                two = prob[:, (4 * q) % SLOTS:(4 * q) % SLOTS + 4, :].rearrange("p (a b) n -> p a (b n)", a=2)
                if q == pool_quads(own)[0]:
                    pool.wait_ge(exp_done, KT * h + 4 * q + 4)
                    if not first:
                        pool.wait_ge(den_done, h - 1)
                    pool.tensor_tensor(pool_sum[:, u, :], two[:, 0], two[:, 1], ALU.add).then_inc(pool_added, 1)
                else:
                    pairs = 1 + (own[q] == "B")
                    for a in range(pairs):
                        pool.wait_ge(exp_done, KT * h + 4 * q + 2 * a + 2)
                        pool.wait_ge(pool_added, pool_adds(OWNER) * h + pool_adds(own, q) - pairs + a)
                        pool.tensor_tensor(pool_sum[:, u, :], two[:, a], pool_sum[:, u, :], ALU.add).then_inc(pool_added, 1)

            for u in range(2):
                for q in pool_quads(OWNER):
                    add(u, u, q, True)
            with pool.Fori(1, H // 2 - 1) as i:
                for u in range(2):
                    for q in pool_quads(OWNER):
                        add(u, 2 * i + u, q, False)
            for h in (H - 2, H - 1):
                for q in pool_quads(owners(h)):
                    add(h % 2, h, q, False)

        @block.scalar
        def _(act):
            def exponentials(u, h, q, js, first):
                for j in js:
                    k = 4 * q + j
                    if j == 0:
                        ago = SLOTS // 4
                        back, at = (0, q - ago) if q >= ago else (1, q - ago + QUADS)
                        if not (first and u == 0 and back):
                            act.wait_ge(pv_done, QUADS * (h - back) + at + 1)
                            own = owners(h - back)
                            if at in pool_quads(own):
                                act.wait_ge(pool_added, pool_adds(OWNER) * (h - back) + pool_adds(own, at))
                            if vec_tiles(own, at):
                                act.wait_ge(vec_added, vec_adds(OWNER) * (h - back) + vec_adds(own, at))
                    act.wait_ge(score_ready, KT * h + k + 1)
                    act.activation(prob[:, k % SLOTS, :], score_bank(u, h, k)[:, :], ACT.Exp, scale=1.0 / math.sqrt(HD)).then_inc(exp_done, 1)

            def copy_turn(u, h):
                act.wait_ge(turned, h + 1)
                act.activation(q2[KS:KM, u, :], pass1[bank_of(1 - u, 2)][0:1, 0:S], ACT.Copy, scale=-1.0).then_inc(turn_copied, 1)

            def evacuate(u, h, first):
                act.wait_ge(pv_done, QUADS * (h + 1))
                act.activation(o_part[:, bass.ds(h, 1), :].rearrange("p h n -> p (h n)"), out_ps[:, :], ACT.Copy).then_inc(o_evac, 1)
                act.wait_ge(den_done, h + 1)
                if not (first and h == 0):
                    act.wait_ge(den_stored, 16 * h)
                act.activation(den_sb[:, u, :], den_ps[:, :], ACT.Copy).then_inc(den_evac, 1)

            def pair(i, first, last):
                for u in range(2):
                    h = 2 * i + u
                    for q in range(QUADS):
                        exponentials(u, h, q, (0, 1), first)
                        d, n = units_beside(q)[1]
                        if n == 1 and not (last and u == 1):
                            copy_turn((u + d - 1) % 2, h + d - 1)
                        exponentials(u, h, q, (2, 3), first)
                        if q == PV_LAG - 1 and not (first and u == 0):
                            evacuate((u + 1) % 2, h - 1, first)

            pair(0, True, False)
            with act.Fori(1, H // 2 - 1) as i:
                pair(i, False, False)
            pair(H // 2 - 1, False, True)
            evacuate(1, H - 1, False)


def finish(nc, ins, out, ident, ones, selectors, o_part, den_d):
    E = ins["experts"].shape[0]
    LINEAR_V, LINEAR_Q, LINEAR_K, LINEAR_O, EXPERTS = 1, 2, 3, 4, 5
    WEIGHTS = EXPERTS + E
    RING = 3
    with ExitStack() as ctx:
        def sb(name, shape, dt=F32):
            return ctx.enter_context(nc.sbuf_tensor(name, shape, dt))

        def sem(name):
            return ctx.enter_context(nc.semaphore(name))

        raw = sb("w_raw", [P, RING, C, D])
        whi = sb("w_high", [P, 2, C, D], F32R)
        wlo = sb("w_low", [P, 2, C, D], F32R)
        x4 = sb("res", [P, C, D])
        xn = sb("xn3", [P, C, D])
        xhi = sb("xnT_high", [P, C, S], F32R)
        xlo = sb("xnT_low", [P, C, S], F32R)
        att = sb("att", [P, C, S])
        ahi = sb("att_high", [P, C, S], F32R)
        alo = sb("att_low", [P, C, S], F32R)
        qT, kT, v, kk = (o_part[:, j * C:(j + 1) * C, :] for j in range(4))
        masked = sb("masked", [P, 2, 4, S])
        state = sb("state", [P, 2, C, P])
        tmp = sb("tmp", [P, 2, S])
        up = sb("up", [P, 2, S])
        down = sb("down", [P, 2, S])
        rec = sb("rec", [P, 2, S])
        sel32, spread = selectors
        den4 = sb("den4", [P, 4, P])
        den_sum = sb("den_sum", [P, P])
        den_inv = den4[:, 0, :]
        rden = sb("rden", [P, S])
        mask = sb("mask", [P, 4, P])
        diag = sb("diag", [P, 4, P])
        cols = sb("bias_cols", [P, 3, C])
        rows = sb("bias_rows", [1, 3, D])
        BR = HD + 1
        brow = sb("bias_split", [BR, 3, D], F32R)
        brow_ones = sb("bias_ones", [BR, P], F32R)
        rw = sb("router", [P, C, E])
        rwhi = sb("router_high", [P, C, E], F32R)
        rwlo = sb("router_low", [P, C, E], F32R)
        rbias = sb("router_bias", [E, 1])
        lgT = sb("logitsT", [E, S])
        iota = sb("iota", [P, E])
        stats = sb("stats3", [P, C, 6])
        mv = sb("mv3", [P, C, 2])
        rstd = sb("rstd3", [P, 3 * C])
        pr = sb("pr", [P, C, E])
        top = sb("top", [P, C, 8])
        topi = sb("topi", [P, C, 8], U32)
        topf = sb("topf", [P, C, 8])
        small = sb("small", [P, 8, C])
        coef = sb("coef", [P, C, E])
        coef2 = sb("coef2", [P, C, E])
        bank = [ctx.enter_context(nc.psum_tensor(f"fin{j}", [P, 512], F32)) for j in range(8)]

        consts, den_in, x_in, biases_in = sem("consts"), sem("den_in"), sem("x3_in"), sem("biases_in")
        raw_in = [sem(f"raw_in{j}") for j in range(RING)]
        w_hi, w_lo = sem("w_hi"), sem("w_lo")
        rows_hi, rows_lo, router_hi, router_lo = sem("rows_hi"), sem("rows_lo"), sem("router_hi"), sem("router_lo")
        vec_max = sem("vec_parallel")
        vec, pool_vec, act_done = sem("vec_chain3"), sem("pool_chain3"), sem("act_done")
        den_set, rden_ready, spread_ps, spread_sb, o_sum, att_mul, ahi_ready, alo_ready = (sem(n) for n in (
            "den_set", "rden_ready", "spread_ps", "spread_sb", "o_sum", "att_mul", "ahi_ready", "alo_ready"))
        alo_first = sem("alo_first")
        wo_ps, added = sem("wo_ps"), sem("added")
        var_ready, std_ready, xn_ready, xT_ps, xhi_ready, xlo_ready = (sem(n) for n in ("var3", "std3", "xn3_ready", "xT_ps", "xhi_ready", "xlo_ready"))
        qk_ps, neg_ready, elu_parts, qk_ready, v_ps, v_ready, kk_ps, kk_ready = (sem(n) for n in (
            "qk_ps", "neg_ready", "elu_parts", "qk_ready", "v_ps", "v3_ready", "kk_ps", "kk_ready"))
        a_ps, a_ready, lin_ps, lin_out, rec_ready, state_ps, state_ready = (sem(n) for n in (
            "a_ps", "a_ready", "lin_ps", "lin_out", "rec_ready", "state_ps", "state_ready"))
        rt_ps, lgT_ready, logit_ps, negmax, exps, y_ps, y_added, stored = (sem(n) for n in (
            "rt_ps", "lgT_ready", "logit_ps", "negmax", "exps", "y_ps", "y_added", "stored"))

        Y_BANKS = (4, 5, 0, 1, 2, 3, 6)
        CONSTS = 1 + 1 + 3 + 2 + 1

        block = ctx.enter_context(nc.Block())

        def chunks(a):
            return a.rearrange("(c p) n -> p c n", p=P)

        def tokens(t):
            return slice(t * P, (t + 1) * P)

        @block.sync
        def _(sp):
            weights = [ins[n] for n in ("xWo", "aWv", "aWq", "aWk", "aWo")] + [ins["experts"][e] for e in range(E)]

            def load(w):
                if w >= RING:
                    sp.wait_ge(w_lo, w - RING + 1)
                sp.dma_start(raw[:, w % RING], chunks(weights[w])).then_inc(raw_in[w % RING], 16)

            load(0)
            sp.wait_ge(den_set, 1)
            for t in range(C):
                sp.dma_start(den4[32 * t:32 * t + H, :, :], den_d[:, :, tokens(t)].rearrange("j h n -> h j n")).then_inc(den_in, 16)
            sp.dma_start(cols[:, :, :], ins["bias_cols"]).then_inc(biases_in, 16)
            sp.dma_start(rows[:, :, :], ins["bias_rows"]).then_inc(biases_in, 16)
            sp.dma_start(rbias[:, :], ins["router_b"]).then_inc(biases_in, 16)
            sp.dma_start(rw[:, :, :], chunks(ins["router_wT"])).then_inc(biases_in, 16)
            sp.dma_start(x4[:, :, :], chunks(ins["x"])).then_inc(x_in, 16)
            for w in range(1, WEIGHTS):
                load(w)
            for t in range(C):
                sp.wait_ge(y_added, C * (E - 1) + t + 1)
                sp.dma_start(out[tokens(t), :], x4[:, t, :]).then_inc(stored, 16)
            sp.wait_ge(stored, 16 * C)

        @block.gpsimd
        def _(pool):
            link = Chain(pool, consts)
            pool.memset(den4[:, :, :], 1.0).then_inc(den_set, 1)
            pool.wait_ge(den_set, 1)
            pool.memset(rden[:, :], 0.0).then_inc(den_set, 1)
            pool.wait_ge(den_set, 2)
            link(pool.memset(brow[:, :, :].bitcast(F32), 0.0))
            link(pool.memset(brow_ones[:, :].bitcast(F32), 1.0))
            link(pool.memset(diag[:, :, :], 1.0))
            d_v = diag[:, :, :].rearrange("p a (j d) -> p a j d", d=HD)
            link(pool.affine_select(out=d_v, in_=d_v, compare_op=ALU.is_ge, fill=0.0,
                                    base=0, pattern=[[0, 4], [-HD, 4], [0, HD]], channel_multiplier=1))
            link(pool.affine_select(out=d_v, in_=d_v, compare_op=ALU.is_ge, fill=0.0,
                                    base=HD - 1, pattern=[[0, 4], [HD, 4], [0, HD]], channel_multiplier=-1))
            link(pool.memset(mask[:, :, :], 1.0))
            link(pool.affine_select(out=mask[:, :, :], in_=mask[:, :, :], compare_op=ALU.is_ge, fill=0.0,
                                    base=0, pattern=[[0, 4], [1, P]], channel_multiplier=-1))
            link(pool.iota(iota[:, :], pattern=[[1, E]], base=0, channel_multiplier=0,
                           allow_small_or_imprecise_dtypes=True))

            def split_low(w):
                pool.wait_ge(w_hi, w + 1)
                pool.tensor_tensor(wlo[:, w % 2], raw[:, w % RING], whi[:, w % 2].bitcast(F32), ALU.subtract).then_inc(w_lo, 1)

            for w in range(EXPERTS + 1):
                split_low(w)
            vlink = Chain(pool, pool_vec)
            for c in range(C):
                pool.wait_ge(lin_out, c + 1)
                pool.wait_ge(rec_ready, c + 1)
                a = att[:, :, tokens(c)]
                vlink(pool.tensor_tensor(a, up[:, c % 2, :].rearrange("p (g n) -> p g n", g=C),
                                         rec[:, c % 2, :].rearrange("p (g n) -> p g n", g=C), ALU.mult))
                pool.wait_ge(ahi_ready, C + c + 1)
                pool.tensor_tensor(alo[:, :, tokens(c)], a, ahi[:, :, tokens(c)].bitcast(F32), ALU.subtract).then_inc(alo_ready, 1)
            for w in range(EXPERTS + 1, WEIGHTS):
                split_low(w)

        @block.tensor
        def _(pe):
            TERMS = ((0, 0), (0, 1), (1, 0))

            def out_projection(t, b, w, row):
                for c in range(C):
                    for n, (i, j) in enumerate(TERMS):
                        pe.matmul(bank[b][:, :], (ahi, alo)[i][:, c, tokens(t)], (whi, wlo)[j][:, w % 2, c, :],
                                  start=c == 0 and n == 0, stop=False)
                pe.wait_ge(rows_lo, 1)
                pe.matmul(bank[b][:, :], brow_ones[:, :], brow[:, row, :], start=False, stop=True).then_inc(wo_ps, 1)

            def transpose(t, b, n):
                pe.wait_ge(xn_ready, C * n + t + 1)
                for c in range(C):
                    m = pe.transpose(bank[b][:, tokens(c)], xn[:, t, tokens(c)], ident[:, :])
                m.then_inc(xT_ps, 1)

            for g in range(C):
                for l in range(4):
                    m = pe.matmul(bank[4 + g][l * HD:(l + 1) * HD, :], sel32[:, :], o_part[:, 4 * g + l, :], start=True, stop=True)
                m.then_inc(o_sum, 1)
            pe.wait_ge(rden_ready, C)
            for g in range(C):
                pe.matmul(bank[g][:, :], spread[:, g, :], rden[:, :], start=True, stop=True).then_inc(spread_ps, 1)
            pe.wait_ge(alo_first, C)
            pe.wait_ge(w_lo, 1)


            def linear_values(t):
                pe.wait_ge(w_lo, LINEAR_V + 1)
                pe.wait_ge(xlo_ready, t + 1)
                pe.wait_ge(added, t + 1)
                for c in range(C):
                    for n, (i, j) in enumerate(TERMS):
                        pe.matmul(bank[4 + t][:, :], (xhi, xlo)[i][:, c, tokens(t)], (whi, wlo)[j][:, LINEAR_V % 2, c, :],
                                  start=c == 0 and n == 0, stop=False)
                pe.matmul(bank[4 + t][:, :], brow_ones[:, :], brow[:, 1, :], start=False, stop=True).then_inc(v_ps, 1)

            out_projection(0, 4, 0, 0)
            out_projection(1, 5, 0, 0)
            transpose(0, 0, 0)
            out_projection(2, 6, 0, 0)
            transpose(1, 1, 0)
            linear_values(0)
            out_projection(3, 7, 0, 0)
            transpose(2, 2, 0)
            linear_values(1)
            transpose(3, 3, 0)
            linear_values(2)
            linear_values(3)

            pe.wait_ge(xlo_ready, C)
            for k in range(2):
                w = LINEAR_Q + k
                pe.wait_ge(w_lo, w + 1)
                for g in range(C):
                    if k:
                        pe.wait_ge(v_ready, g + 1)
                    for c in range(C):
                        for n, (i, j) in enumerate(TERMS):
                            m = pe.matmul(bank[4 * k + g][:, :], (whi, wlo)[j][:, w % 2, c, tokens(g)], (xhi, xlo)[i][:, c, :],
                                          start=c == 0 and n == 0, stop=c == C - 1 and n == 2)
                    m.then_inc(qk_ps, 1)
            for g in range(C):
                pe.wait_ge(qk_ready, C + g + 1)
                for t in range(C):
                    m = pe.transpose(bank[t][:, tokens(g)], kT[:, g, tokens(t)], ident[:, :])
            m.then_inc(kk_ps, 1)

            def causal_scores(c, heads=range(4)):
                for l in heads:
                    r = slice(l * HD, (l + 1) * HD)
                    if c == 0:
                        pe.wait_ge(kk_ready, l + 1)
                    else:
                        pe.wait_ge(a_ready, 4 * (c - 1) + l + 1)
                    for g in range(C):
                        m = pe.matmul(bank[l][:, tokens(g)], kT[r, g, tokens(c)], qT[r, g, tokens(c)], start=True, stop=True)
                    m.then_inc(a_ps, 1)

            def sums(c):
                if c:
                    pe.wait_ge(lin_out, c)
                    pe.wait_ge(state_ready, 2 * c)
                pe.wait_ge(a_ready, 4 * (c + 1))
                for g in range(C):
                    for b, w in ((4, v), (5, None)):
                        for l in range(4):
                            lhs = ones[:, 0:HD] if w is None else w[:, c, (4 * g + l) * HD:(4 * g + l + 1) * HD]
                            m = pe.matmul(bank[b][l * HD:(l + 1) * HD, tokens(g)], lhs, masked[:, c % 2, l, tokens(g)],
                                          start=True, stop=c == 0)
                    if c:
                        for j in range(2):
                            m = pe.matmul(bank[4 + j][:, tokens(g)], state[:, j, g, :], qT[:, g, tokens(c)], start=False, stop=True)
                m.then_inc(lin_ps, 1)
                if c < C - 1:
                    for j in range(2):
                        for g in range(C):
                            m = pe.matmul(bank[6 + j][:, tokens(g)], kk[:, c, tokens(g)], (v[:, c, tokens(g)], ones[:, :])[j],
                                          start=c == 0 and g == 0, stop=True, skip_group_check=True)
                        m.then_inc(state_ps, 1)

            def linear_projection(t, b):
                pe.wait_ge(alo_ready, t + 1)
                pe.wait_ge(w_lo, LINEAR_O + 1)
                out_projection(t, b, LINEAR_O, 2)

            causal_scores(0)
            sums(0)
            causal_scores(1)
            sums(1)
            for c in range(2, C):
                causal_scores(c, (0, 1, 2))
                pe.wait_ge(a_ready, 4 * c)
                linear_projection(c - 2, 3)
                pe.wait_ge(added, C + c - 1)
                causal_scores(c, (3,))
                if c == C - 1:
                    pe.wait_ge(a_ready, 4 * c + 1)
                    transpose(0, 0, 1)
                sums(c)

            def expert_tile(n):
                e, t = n // C, n % C
                w = EXPERTS + e
                pe.wait_ge(w_lo, w + 1)
                pe.wait_ge(xlo_ready, C + (t if e == 0 else C - 1) + 1)
                if n == 0:
                    pe.wait_ge(lin_out, C)
                elif n == 5:
                    pe.wait_ge(added, 2 * C)
                elif n >= 7:
                    pe.wait_ge(y_added, n - 6)
                for c in range(C):
                    for k, (i, j) in enumerate(TERMS):
                        m = pe.matmul(bank[Y_BANKS[n % 7]][:, :], (xhi, xlo)[i][:, c, tokens(t)], (whi, wlo)[j][:, w % 2, c, :],
                                      start=c == 0 and k == 0, stop=c == C - 1 and k == 2)
                m.then_inc(y_ps, 1)

            pe.wait_ge(a_ready, 4 * C)
            transpose(1, 1, 1)
            linear_projection(2, 3)
            expert_tile(0)
            expert_tile(1)
            pe.wait_ge(state_ready, 2 * (C - 1))
            linear_projection(3, 6)
            transpose(2, 2, 1)
            expert_tile(2)
            transpose(3, 7, 1)
            pe.wait_ge(router_lo, 1)
            pe.wait_ge(xlo_ready, 2 * C)
            for c in range(C):
                for n, (i, j) in enumerate(TERMS):
                    m = pe.matmul(bank[7][0:E, :], (rwhi, rwlo)[j][:, c, :], (xhi, xlo)[i][:, c, :],
                                  start=c == 0 and n == 0, stop=c == C - 1 and n == 2)
            m.then_inc(rt_ps, 1)
            for n in range(3, E * C):
                expert_tile(n)
                if n == 3:
                    pe.wait_ge(lgT_ready, 1)
                    for k in range(C):
                        m = pe.transpose(bank[7][:, k * E:(k + 1) * E], lgT[:, tokens(k)], ident[0:E, 0:E])
                    m.then_inc(logit_ps, 1)

        @block.scalar
        def _(act):
            def split_high(w, free=None, count=0):
                act.wait_ge(raw_in[w % RING], 16 * (w // RING + 1))
                if free is not None:
                    act.wait_ge(free, count)
                act.activation(whi[:, w % 2], raw[:, w % RING], ACT.Copy).then_inc(w_hi, 1)

            def root(t, n):
                act.wait_ge(var_ready, C * n + t + 1)
                act.activation(rstd[:, C + t:C + t + 1], rstd[:, t:t + 1], ACT.Sqrt).then_inc(std_ready, 1)

            def transposed(t, b, n):
                act.wait_ge(xT_ps, C * n + t + 1)
                act.activation(xhi[:, :, tokens(t)], bank[b][:, :].rearrange("p (c n) -> p c n", c=C), ACT.Copy).then_inc(xhi_ready, 1)

            split_high(0)
            act.wait_ge(biases_in, 64)
            for g in range(C):
                act.wait_ge(spread_ps, g + 1)
                if g >= 2:
                    act.wait_ge(att_mul, g - 1)
                act.activation(tmp[:, g % 2, :], bank[g][:, :], ACT.Copy).then_inc(spread_sb, 1)
            for g in range(C):
                act.wait_ge(att_mul, g + 1)
                act.activation(ahi[:, g, :], att[:, g, :], ACT.Identity, bias=cols[:, 0, g:g + 1]).then_inc(ahi_ready, 1)
            act.wait_ge(consts, CONSTS)
            act.activation(brow[0:1, :, :], rows[:, :, :], ACT.Copy).then_inc(rows_hi, 1)
            act.activation(rwhi[:, :, :], rw[:, :, :], ACT.Copy).then_inc(router_hi, 1)
            split_high(1)
            root(0, 0)
            root(1, 0)
            transposed(0, 0, 0)
            root(2, 0)
            transposed(1, 1, 0)

            def values_out(t):
                act.wait_ge(v_ps, t + 1)
                act.activation(v[:, t, :], bank[4 + t][:, :], ACT.Copy).then_inc(v_ready, 1)

            values_out(0)
            root(3, 0)
            transposed(2, 2, 0)
            values_out(1)
            transposed(3, 3, 0)
            split_high(LINEAR_Q, wo_ps, C)
            values_out(2)
            values_out(3)
            for n in range(2 * C):
                k, g = n // C, n % C
                if g == 0:
                    split_high(LINEAR_K + k, (v_ps, qk_ps)[k], C)
                act.wait_ge(neg_ready, n + 1)
                act.activation(tmp[:, n % 2, :], tmp[:, n % 2, :], ACT.Exp).then_inc(act_done, 1)
                act.activation((qT, kT)[k][:, g, :], bank[n][:, :], ACT.Relu, bias=cols[:, 1 + k, g:g + 1]).then_inc(elu_parts, 1)
            act.wait_ge(kk_ps, 1)
            for t in range(C):
                act.activation(kk[:, t, :], bank[t][:, :], ACT.Copy).then_inc(kk_ready, 1)
            split_high(EXPERTS, qk_ps, 2 * C)

            def sums_out(c):
                act.wait_ge(lin_ps, c + 1)
                if c >= 2:
                    act.wait_ge(ahi_ready, C + c - 1)
                act.activation(down[:, c % 2, :], bank[5][:, :], ACT.Copy, bias=1e-6).then_inc(act_done, 1)
                act.activation(up[:, c % 2, :], bank[4][:, :], ACT.Copy).then_inc(lin_out, 1)

            def high(c):
                act.wait_ge(pool_vec, c + 1)
                act.activation(ahi[:, :, tokens(c)], att[:, :, tokens(c)], ACT.Copy).then_inc(ahi_ready, 1)

            sums_out(0)
            high(0)
            sums_out(1)
            high(1)
            root(0, 1)
            sums_out(2)
            high(2)
            root(1, 1)
            transposed(0, 0, 1)
            sums_out(3)
            transposed(1, 1, 1)
            high(3)
            root(2, 1)
            root(3, 1)
            transposed(2, 2, 1)
            transposed(3, 7, 1)
            split_high(EXPERTS + 1, wo_ps, 2 * C)
            act.wait_ge(rt_ps, 1)
            act.activation(lgT[:, :], bank[7][0:E, :], ACT.Identity, bias=rbias[:, 0:1]).then_inc(lgT_ready, 1)
            act.wait_ge(negmax, 1)
            for t in range(C):
                act.activation(pr[:, t, :], bank[7][:, t * E:(t + 1) * E], ACT.Exp, bias=small[:, 0, t:t + 1],
                               accum_out=small[:, 1, t:t + 1]).then_inc(exps, 1)
            for e in range(2, E):
                split_high(EXPERTS + e, y_ps, C * (e - 1))

        @block.vector
        def _(dve):
            link = Chain(dve, vec)

            def add(t, b, n):
                dve.wait_ge(wo_ps, C * n + t + 1)
                dve.tensor_tensor(x4[:, t, :], bank[b][:, :], x4[:, t, :], ALU.add).then_inc(added, 1)

            def norm(t, n):
                dve.wait_ge(added, C * n + t + 1)
                link(dve.bn_stats(stats[:, t, :], x4[:, t, :]))
                link(dve.bn_aggr(mv[:, t, :], stats[:, t, :]))
                dve.tensor_scalar(rstd[:, t:t + 1], mv[:, t, 1:2], EPS, None, ALU.add).then_inc(var_ready, 1)
                dve.wait_ge(std_ready, C * n + t + 1)
                link(dve.reciprocal(rstd[:, 2 * C + t:2 * C + t + 1], rstd[:, C + t:C + t + 1]))
                if n:
                    dve.wait_ge(xT_ps, C)
                dve.tensor_scalar(xn[:, t, :], x4[:, t, :], mv[:, t, 0:1], rstd[:, 2 * C + t:2 * C + t + 1],
                                  ALU.subtract, ALU.mult).then_inc(xn_ready, 1)

            def transposed_low(t, b, n):
                dve.wait_ge(xhi_ready, C * n + t + 1)
                dve.tensor_tensor(xlo[:, :, tokens(t)], bank[b][:, :].rearrange("p (c n) -> p c n", c=C),
                                  xhi[:, :, tokens(t)].bitcast(F32), ALU.subtract).then_inc(xlo_ready, 1)

            dve.wait_ge(den_in, 16 * C)
            link(dve.tensor_reduce(den_sum[:, :], den4[:, :, :].rearrange("p j n -> p n j"), AX.X, ALU.add))
            link(dve.reciprocal(den_inv, den_sum[:, :]))
            dve.wait_ge(den_set, 2)
            for t in range(C):
                r = slice(32 * t, 32 * t + H)
                dve.tensor_copy(rden[r, tokens(t)], den_inv[r, :]).then_inc(rden_ready, 1)
            for g in range(C):
                dve.wait_ge(spread_sb, g + 1)
                dve.wait_ge(o_sum, g + 1)
                dve.tensor_tensor(att[:, g, :], bank[4 + g][:, :], tmp[:, g % 2, :], ALU.mult).then_inc(att_mul, 1)
            for g in range(C):
                dve.wait_ge(ahi_ready, g + 1)
                dve.scalar_tensor_tensor(alo[:, g, :], att[:, g, :], cols[:, 0, g:g + 1], ahi[:, g, :].bitcast(F32),
                                         ALU.add, ALU.subtract).then_inc(alo_first, 1)
            dve.wait_ge(rows_hi, 1)
            dve.tensor_tensor(brow[HD:BR, :, :], rows[:, :, :], brow[0:1, :, :].bitcast(F32), ALU.subtract).then_inc(rows_lo, 1)
            dve.wait_ge(router_hi, 1)
            dve.tensor_tensor(rwlo[:, :, :], rw[:, :, :], rwhi[:, :, :].bitcast(F32), ALU.subtract).then_inc(router_lo, 1)
            dve.wait_ge(x_in, 16)
            add(0, 4, 0)
            norm(0, 0)
            add(1, 5, 0)
            norm(1, 0)
            transposed_low(0, 0, 0)
            add(2, 6, 0)
            norm(2, 0)
            transposed_low(1, 1, 0)
            add(3, 7, 0)
            norm(3, 0)
            transposed_low(2, 2, 0)
            transposed_low(3, 3, 0)
            for n in range(2 * C):
                k, g = n // C, n % C
                dve.wait_ge(qk_ps, n + 1)
                if n >= 2:
                    dve.wait_ge(qk_ready, n - 1)
                dve.tensor_scalar(tmp[:, n % 2, :], bank[n][:, :], cols[:, 1 + k, g:g + 1], 0.0, ALU.add, ALU.min).then_inc(neg_ready, 1)
                dve.wait_ge(act_done, n + 1)
                dve.wait_ge(elu_parts, n + 1)
                dst = (qT, kT)[k][:, g, :]
                dve.tensor_tensor(dst, dst, tmp[:, n % 2, :], ALU.add).then_inc(qk_ready, 1)

            def apply_mask(c, l):
                dve.wait_ge(a_ps, 4 * c + l + 1)
                if c >= 2:
                    dve.wait_ge(lin_ps, c - 1)
                dve.tensor_tensor(masked[:, c % 2, l, :], bank[l][:, :], mask[:, :, :].rearrange("p a n -> p (a n)"),
                                  ALU.mult).then_inc(a_ready, 1)

            def invert(c):
                dve.wait_ge(act_done, 2 * C + c + 1)
                if c >= 2:
                    dve.wait_ge(pool_vec, c - 1)
                dve.reciprocal(rec[:, c % 2, :], down[:, c % 2, :]).then_inc(rec_ready, 1)

            def keep_state(c):
                for j in range(2):
                    dve.wait_ge(state_ps, 2 * c + j + 1)
                    dve.tensor_tensor(state[:, j], bank[6 + j][:, :].rearrange("p (g n) -> p g n", g=C), diag[:, :, :],
                                      ALU.mult).then_inc(state_ready, 1)

            for l in range(4):
                apply_mask(0, l)
            keep_state(0)
            for l in range(4):
                apply_mask(1, l)
            invert(0)
            keep_state(1)
            for l in range(4):
                if l == 3:
                    add(0, 3, 1)
                apply_mask(2, l)
            invert(1)
            keep_state(2)
            norm(0, 1)
            for l in range(4):
                if l == 3:
                    add(1, 3, 1)
                apply_mask(3, l)
            invert(2)
            norm(1, 1)
            transposed_low(0, 0, 1)
            invert(3)
            transposed_low(1, 1, 1)
            add(2, 3, 1)
            norm(2, 1)
            add(3, 6, 1)
            norm(3, 1)
            transposed_low(2, 2, 1)
            transposed_low(3, 7, 1)
            dve.wait_ge(logit_ps, 1)
            logits = bank[7][:, 0:C * E].rearrange("p (t e) -> p t e", e=E)
            dve.tensor_reduce(small[:, 0, :], logits, AX.X, ALU.max, negate=True).then_inc(negmax, 1)
            dve.wait_ge(exps, C)
            def everywhere(column):
                return column.unsqueeze(2).to_broadcast([P, C, E])

            link(dve.reciprocal(small[:, 2, :], small[:, 1, :]))
            link(dve.tensor_tensor(pr[:, :, :], pr[:, :, :], everywhere(small[:, 2, :]), ALU.mult))
            for t in range(C):
                m = dve.max(top[:, t, :], pr[:, t, :])
                if t < C - 1:
                    m.then_inc(vec_max, 1)
            link(m)
            dve.wait_ge(vec_max, C - 1)
            for t in range(C):
                m = dve.max_index(topi[:, t, :], top[:, t, :], pr[:, t, :])
                if t < C - 1:
                    m.then_inc(vec_max, 1)
            link(m)
            dve.wait_ge(vec_max, 2 * (C - 1))
            p1, p2 = top[:, :, 0], top[:, :, 1]
            dve.tensor_copy(topf[:, :, :], topi[:, :, :]).then_inc(vec_max, 1)
            link(dve.tensor_tensor(small[:, 3, :], p1, p2, ALU.add))
            link(dve.tensor_scalar(small[:, 3, :], small[:, 3, :], 1e-10, None, ALU.add))
            link(dve.reciprocal(small[:, 3, :], small[:, 3, :]))
            link(dve.tensor_tensor(small[:, 4:6, :], top[:, :, 0:2].rearrange("p t k -> p k t"),
                                   small[:, 3, :].unsqueeze(1).to_broadcast([P, 2, C]), ALU.mult))
            link(dve.tensor_tensor(small[:, 6, :], small[:, 4, :], small[:, 5, :], ALU.add))
            link(dve.tensor_scalar(small[:, 7, :], small[:, 6, :], 1e-10, None, ALU.max))
            dve.tensor_scalar(small[:, 6, :], small[:, 6, :], 1e-10, 1.0, ALU.mult, ALU.add).then_inc(vec_max, 1)
            link(dve.reciprocal(small[:, 7, :], small[:, 7, :]))
            dve.wait_ge(vec_max, 2 * C)
            link(dve.tensor_tensor(small[:, 7, :], small[:, 7, :], small[:, 6, :], ALU.mult))
            link(dve.tensor_tensor(small[:, 4:6, :], small[:, 4:6, :], small[:, 7, :].unsqueeze(1).to_broadcast([P, 2, C]), ALU.mult))
            each = iota[:, :].unsqueeze(1).to_broadcast([P, C, E])
            for k, c in ((0, coef), (1, coef2)):
                dve.tensor_tensor(c[:, :, :], each, everywhere(topf[:, :, k]), ALU.is_equal).then_inc(vec_max, 1)
            dve.wait_ge(vec_max, 2 * C + 2)
            for k, c in ((0, coef), (1, coef2)):
                dve.tensor_tensor(c[:, :, :], c[:, :, :], everywhere(small[:, 4 + k, :]), ALU.mult).then_inc(vec_max, 1)
            dve.wait_ge(vec_max, 2 * C + 4)
            link(dve.tensor_tensor(coef[:, :, :], coef[:, :, :], coef2[:, :, :], ALU.add))
            n = 0
            for e in range(E):
                for t in range(C):
                    dve.wait_ge(y_ps, n + 1)
                    if e:
                        dve.wait_ge(y_added, n - C + 1)
                    dve.scalar_tensor_tensor(x4[:, t, :], bank[Y_BANKS[n % 7]][:, :], coef[:, t, e:e + 1], x4[:, t, :],
                                             ALU.mult, ALU.add).then_inc(y_added, 1)
                    n += 1


def perceiver(nc, ins, out):
    khi_d = nc.dram_tensor("keys_high", (D, KEYS), F32, kind="Internal").ap()
    klo_d = nc.dram_tensor("keys_low", (D, KEYS), F32, kind="Internal").ap()
    qhi_d = nc.dram_tensor("queries_high", (D, S), F32, kind="Internal").ap()
    qlo_d = nc.dram_tensor("queries_low", (D, S), F32, kind="Internal").ap()
    v_d = nc.dram_tensor("values", (H, P, BLOCKS, C * HD), F32, kind="Internal").ap()
    den_d = nc.dram_tensor("denominators", (4, H, S), F32, kind="Internal").ap()
    scratch = (khi_d, klo_d, qhi_d, qlo_d, v_d)
    with ExitStack() as ctx:
        ident = ctx.enter_context(nc.sbuf_tensor("ident", [P, P], F32))
        ones = ctx.enter_context(nc.sbuf_tensor("ones", [P, P], F32))
        selectors = (ctx.enter_context(nc.sbuf_tensor("sel32", [P, HD], F32)),
                     ctx.enter_context(nc.sbuf_tensor("spread", [P, C, P], F32)))
        o_part = ctx.enter_context(nc.sbuf_tensor("o_part", [P, H, S], F32))
        with ExitStack() as shared:
            keys = shared.enter_context(nc.sbuf_tensor("keys", [P, 2, KEYS], F32R))
            q1 = shared.enter_context(nc.sbuf_tensor("q1", [P, 2, S], F32R))
            q2 = shared.enter_context(nc.sbuf_tensor("q2", [P, 2, S], F32R))
            parts = shared.enter_context(nc.sbuf_tensor("parts", [P, C, UNITS // C], F32))
            mx = shared.enter_context(nc.sbuf_tensor("mx", [P, C], F32))
            maxima = (parts, mx) + tuple(shared.enter_context(nc.semaphore(n)) for n in ("p1_ready", "part_done", "turned", "turn_copied"))
            project_context(nc, ins, scratch, ident, ones, selectors, (keys, q1, q2), maxima, o_part)
            attend(nc, scratch, ident, ones, (keys, q1, q2), maxima, o_part, den_d)
        finish(nc, ins, out, ident, ones, selectors, o_part, den_d)


def kernel(**inputs):
    import concourse.bacc as bacc
    from concourse.bass_utils import run_bass_kernel_spmd

    a = {k: np.asarray(v) for k, v in inputs.items()}

    def column(b):
        return b.reshape(C, P).T

    arrays = {
        "x": a["x"][0], "ctxT": a["ctx_1024"][0].T,
        "xWq": a["L0_xattn_Wq"], "xWk": a["L0_xattn_Wk"], "xWv": a["L0_xattn_Wv"], "xWo": a["L0_xattn_Wo"],
        "xbq_col": column(a["L0_xattn_bq"]), "xbk_col": column(a["L0_xattn_bk"]),
        "aWq": a["L0_attn_Wq"], "aWk": a["L0_attn_Wk"], "aWv": a["L0_attn_Wv"], "aWo": a["L0_attn_Wo"],
        "bias_cols": np.stack([column(a[n]) for n in ("L0_xattn_bv", "L0_attn_bq", "L0_attn_bk")], axis=1),
        "bias_rows": np.stack([a[n] for n in ("L0_xattn_bo", "L0_attn_bv", "L0_attn_bo")])[None],
        "router_wT": a["L0_ffn_router_w"].T, "router_b": a["L0_ffn_router_b"][:, None],
        "experts": a["L0_ffn_expert_weights"],
    }
    nc = bacc.Bacc("TRN2", target_bir_lowering=False, num_devices=1)
    arrays = {f"in_{k}": np.ascontiguousarray(v) for k, v in arrays.items()}
    ins = {k[3:]: nc.dram_tensor(k, v.shape, mybir.dt.from_np(v.dtype), kind="ExternalInput").ap() for k, v in arrays.items()}
    out = nc.dram_tensor("out", (S, D), F32, kind="ExternalOutput").ap()
    perceiver(nc, ins, out)
    r = run_bass_kernel_spmd(nc, [arrays], core_ids=[0])
    return r.results[0]["out"].reshape(1, S, D)
```
